# Optimizing a Trainium2 kernel written in Bass

```python
import numpy as np
import jax
import jax.numpy as jnp

def _softmax(x, axis=-1):
    return jax.nn.softmax(x, axis=axis)

def _gelu(x):
    return jax.nn.gelu(x, approximate=True)

def _silu(x):
    return jax.nn.silu(x)

def _sigmoid(x):
    return jax.nn.sigmoid(x)

def _layernorm(x, axis=-1, eps=1e-05):
    m = jnp.mean(x, axis=axis, keepdims=True)
    v = jnp.var(x, axis=axis, keepdims=True)
    return (x - m) / jnp.sqrt(v + eps)

def _scatter_add(tgt, idx, src, axis=0):
    return tgt.at[idx].add(src)

def _segment_sum(src, seg, n):
    return jax.ops.segment_sum(src, seg, n)
kernel_name = 'mk_conv_attn_hybrid_d2_conv_nchw128_r4_3943ef'

def setup_inputs(seed: int=0):
    np.random.seed(seed)
    _w = jnp.asarray

    def _rec_inputs():
        import jax
        import jax.numpy as jnp
        _gk = jax.random.key(seed)
        x = 7.22e-05 + 1 * jax.random.normal(jax.random.fold_in(_gk, 1), (16, 32, 16, 16), jnp.float32)
        return x
    x = _rec_inputs()

    def _L0_conv_setup():
        import jax, jax.numpy as jnp
        import numpy as np
        KS = 51
        DENSE_INNER = 2
        DIM = 32
        B, H, W = (16, 16, 16)

        def _make_peripheral_coords(radius, dense_inner=2):
            coords = list(range(0, min(radius, dense_inner) + 1))
            v = 1
            while v < radius:
                v *= 2
                if v > dense_inner and v < radius:
                    coords.append(v)
            if radius not in coords:
                coords.append(radius)
            return sorted(set(coords))

        def _quantise(a, coords):
            q = 0
            for c in coords:
                if c <= a:
                    q = c
                else:
                    break
            return q

        def _build_idx(kernel_size, dense_inner):
            radius = kernel_size // 2
            coords = _make_peripheral_coords(radius, dense_inner)
            signed = [-c for c in reversed(coords[1:])] + list(coords)
            P = len(signed)
            c2i = {c: i for i, c in enumerate(signed)}
            idx = []
            for i in range(kernel_size):
                oi = i - radius
                qi = _quantise(abs(oi), coords)
                ii = c2i[-qi if oi < 0 else qi]
                for j in range(kernel_size):
                    oj = j - radius
                    qj = _quantise(abs(oj), coords)
                    jj = c2i[-qj if oj < 0 else qj]
                    idx.append(ii * P + jj)
            return (np.asarray(idx, dtype=np.int32), P)
        IDX_MAP, P = _build_idx(KS, DENSE_INNER)
        key = jax.random.key(seed)
        k1, k2, k3 = jax.random.split(key, 3)
        x = jax.random.normal(k1, (B, DIM, H, W), dtype=jnp.float32)
        weight_comp = jax.random.normal(k2, (DIM, P * P), dtype=jnp.float32) * 0.02
        kpe = jax.random.normal(k3, (1, 1, KS, KS), dtype=jnp.float32) * 0.02
        return {'x': x, 'weight_comp': weight_comp, 'kpe': kpe}
    _L0_conv_all = _L0_conv_setup()
    _L0_conv_in = {k: v for k, v in _L0_conv_all.items() if k in ('weight_comp', 'kpe')}
    del _L0_conv_all

    def _L1_attn_setup():
        import jax, jax.numpy as jnp
        import numpy as np
        from jax import lax
        TAU_MEM = 10.0
        THRESHOLD = 1.0
        WINDOW = 32
        STRIDE = 16
        NUM_GLOBAL = 4

        def _spike_indicators(x, Ws, bs):
            B, S, D = x.shape
            decay = jnp.exp(jnp.float32(-1.0 / TAU_MEM))
            cur = x @ Ws + bs
            cur_t = jnp.swapaxes(cur, 0, 1)

            def step(mem, c):
                mem = decay * mem + c
                spk = mem >= THRESHOLD
                mem = jnp.where(spk, 0.0, mem)
                return (mem, spk.astype(jnp.float32))
            _, spikes = lax.scan(step, jnp.zeros((B, 1), jnp.float32), cur_t)
            spike_ind = spikes.mean(axis=1)[:, 0]
            return spike_ind != 0.0

        def _sparse_mask(S, spike_bool):
            i = jnp.arange(S)[:, None]
            j = jnp.arange(S)[None, :]
            local = (j <= i) & (j >= i - WINDOW)
            glob = j % STRIDE == 0
            first = j < NUM_GLOBAL
            return (local | glob | first) & spike_bool[None, :]
        key = jax.random.key(seed)
        ks = jax.random.split(key, 8)
        B, S, D = (2, 2048, 32)
        s = 1.0 / np.sqrt(D)
        x = jax.random.normal(ks[0], (B, S, D), jnp.float32)
        Wq = jax.random.normal(ks[1], (D, D), jnp.float32) * s
        Wk = jax.random.normal(ks[2], (D, D), jnp.float32) * s
        Wv = jax.random.normal(ks[3], (D, D), jnp.float32) * s
        Wo = jax.random.normal(ks[4], (D, D), jnp.float32) * s
        Ws = jax.random.normal(ks[5], (D, 1), jnp.float32) * s
        return {'x': x, 'Wq': Wq, 'bq': jnp.zeros((D,), jnp.float32), 'Wk': Wk, 'bk': jnp.zeros((D,), jnp.float32), 'Wv': Wv, 'bv': jnp.zeros((D,), jnp.float32), 'Wo': Wo, 'bo': jnp.zeros((D,), jnp.float32), 'Ws': Ws, 'bs': jnp.zeros((1,), jnp.float32)}
    _L1_attn_all = _L1_attn_setup()
    _L1_attn_in = {k: v for k, v in _L1_attn_all.items() if k in ('Wq', 'bq', 'Wk', 'bk', 'Wv', 'bv', 'Wo', 'bo', 'Ws', 'bs')}
    del _L1_attn_all

    def _L1_ffn_setup():
        import jax, jax.numpy as jnp
        import numpy as np
        NB, NOPS = (33, 19)
        D, H = (32, 128)
        B, S = (8, 256)
        CARRY_OPS = [0, 1, 2, 10, 11, 12, 13]

        def _build_masks():
            am = np.zeros((NB, NOPS), dtype=bool)
            fm = np.zeros((NB, NOPS), dtype=bool)
            fm[0, :] = True
            for b in range(1, 8):
                am[b, CARRY_OPS] = True
                fm[b, CARRY_OPS] = True
            am[8, [14, 15, 8, 9]] = True
            fm[8, [14, 15, 8, 9]] = True
            for b in range(16, 32):
                fm[b, [3, 4]] = True
            am[32, [10, 11, 12, 13]] = True
            fm[32, [5, 6, 7, 2, 4, 10, 11, 12, 13]] = True
            return (jnp.asarray(am), jnp.asarray(fm))
        key = jax.random.key(seed)
        ks = jax.random.split(key, 9)
        sd = 1.0 / np.sqrt(D)
        sh = 1.0 / np.sqrt(H)
        am, fm = _build_masks()
        return {'x': jax.random.normal(ks[0], (B, S, D), jnp.float32), 'ffn_w1': jax.random.normal(ks[1], (NB, NOPS, D, H), jnp.float32) * sd, 'ffn_b1': jnp.zeros((NB, NOPS, H), jnp.float32), 'ffn_w2': jax.random.normal(ks[2], (NB, NOPS, H, D), jnp.float32) * sh, 'ffn_b2': jnp.zeros((NB, NOPS, D), jnp.float32), 'wq': jax.random.normal(ks[3], (NB, NOPS, D, D), jnp.float32) * sd, 'wk': jax.random.normal(ks[4], (NB, NOPS, D, D), jnp.float32) * sd, 'wv': jax.random.normal(ks[5], (NB, NOPS, D, D), jnp.float32) * sd, 'wo': jax.random.normal(ks[6], (NB, NOPS, D, D), jnp.float32) * sd, 'attn_mask': am, 'ffn_mask': fm}
    _L1_ffn_all = _L1_ffn_setup()
    _L1_ffn_in = {k: v for k, v in _L1_ffn_all.items() if k in ('ffn_w1', 'ffn_b1', 'ffn_w2', 'ffn_b2', 'wq', 'wk', 'wv', 'wo', 'attn_mask', 'ffn_mask')}
    del _L1_ffn_all
    return {'x': x, 'L0_conv_weight_comp': _L0_conv_in['weight_comp'], 'L0_conv_kpe': _L0_conv_in['kpe'], 'L1_attn_Wq': _L1_attn_in['Wq'], 'L1_attn_bq': _L1_attn_in['bq'], 'L1_attn_Wk': _L1_attn_in['Wk'], 'L1_attn_bk': _L1_attn_in['bk'], 'L1_attn_Wv': _L1_attn_in['Wv'], 'L1_attn_bv': _L1_attn_in['bv'], 'L1_attn_Wo': _L1_attn_in['Wo'], 'L1_attn_bo': _L1_attn_in['bo'], 'L1_attn_Ws': _L1_attn_in['Ws'], 'L1_attn_bs': _L1_attn_in['bs'], 'L1_ffn_ffn_w1': _L1_ffn_in['ffn_w1'], 'L1_ffn_ffn_b1': _L1_ffn_in['ffn_b1'], 'L1_ffn_ffn_w2': _L1_ffn_in['ffn_w2'], 'L1_ffn_ffn_b2': _L1_ffn_in['ffn_b2'], 'L1_ffn_wq': _L1_ffn_in['wq'], 'L1_ffn_wk': _L1_ffn_in['wk'], 'L1_ffn_wv': _L1_ffn_in['wv'], 'L1_ffn_wo': _L1_ffn_in['wo'], 'L1_ffn_attn_mask': _L1_ffn_in['attn_mask'], 'L1_ffn_ffn_mask': _L1_ffn_in['ffn_mask']}

def reference(x, L0_conv_weight_comp, L0_conv_kpe, L1_attn_Wq, L1_attn_bq, L1_attn_Wk, L1_attn_bk, L1_attn_Wv, L1_attn_bv, L1_attn_Wo, L1_attn_bo, L1_attn_Ws, L1_attn_bs, L1_ffn_ffn_w1, L1_ffn_ffn_b1, L1_ffn_ffn_w2, L1_ffn_ffn_b2, L1_ffn_wq, L1_ffn_wk, L1_ffn_wv, L1_ffn_wo, L1_ffn_attn_mask, L1_ffn_ffn_mask):
    import jax
    import jax.numpy as jnp

    def _L0_conv_ref(x, weight_comp, kpe):
        import jax, jax.numpy as jnp
        import numpy as np
        KS = 51
        DENSE_INNER = 2
        DIM = 32
        B, H, W = (16, 16, 16)

        def _make_peripheral_coords(radius, dense_inner=2):
            coords = list(range(0, min(radius, dense_inner) + 1))
            v = 1
            while v < radius:
                v *= 2
                if v > dense_inner and v < radius:
                    coords.append(v)
            if radius not in coords:
                coords.append(radius)
            return sorted(set(coords))

        def _quantise(a, coords):
            q = 0
            for c in coords:
                if c <= a:
                    q = c
                else:
                    break
            return q

        def _build_idx(kernel_size, dense_inner):
            radius = kernel_size // 2
            coords = _make_peripheral_coords(radius, dense_inner)
            signed = [-c for c in reversed(coords[1:])] + list(coords)
            P = len(signed)
            c2i = {c: i for i, c in enumerate(signed)}
            idx = []
            for i in range(kernel_size):
                oi = i - radius
                qi = _quantise(abs(oi), coords)
                ii = c2i[-qi if oi < 0 else qi]
                for j in range(kernel_size):
                    oj = j - radius
                    qj = _quantise(abs(oj), coords)
                    jj = c2i[-qj if oj < 0 else qj]
                    idx.append(ii * P + jj)
            return (np.asarray(idx, dtype=np.int32), P)
        IDX_MAP, P = _build_idx(KS, DENSE_INNER)
        dim = weight_comp.shape[0]
        weight = weight_comp[:, IDX_MAP].reshape(dim, 1, KS, KS) + kpe
        pad = KS // 2
        return jax.lax.conv_general_dilated(x, weight, window_strides=(1, 1), padding=[(pad, pad), (pad, pad)], dimension_numbers=('NCHW', 'OIHW', 'NCHW'), feature_group_count=dim)

    def _L1_attn_ref(x, Wq, bq, Wk, bk, Wv, bv, Wo, bo, Ws, bs):
        import jax, jax.numpy as jnp
        import numpy as np
        from jax import lax
        TAU_MEM = 10.0
        THRESHOLD = 1.0
        WINDOW = 32
        STRIDE = 16
        NUM_GLOBAL = 4

        def _spike_indicators(x, Ws, bs):
            B, S, D = x.shape
            decay = jnp.exp(jnp.float32(-1.0 / TAU_MEM))
            cur = x @ Ws + bs
            cur_t = jnp.swapaxes(cur, 0, 1)

            def step(mem, c):
                mem = decay * mem + c
                spk = mem >= THRESHOLD
                mem = jnp.where(spk, 0.0, mem)
                return (mem, spk.astype(jnp.float32))
            _, spikes = lax.scan(step, jnp.zeros((B, 1), jnp.float32), cur_t)
            spike_ind = spikes.mean(axis=1)[:, 0]
            return spike_ind != 0.0

        def _sparse_mask(S, spike_bool):
            i = jnp.arange(S)[:, None]
            j = jnp.arange(S)[None, :]
            local = (j <= i) & (j >= i - WINDOW)
            glob = j % STRIDE == 0
            first = j < NUM_GLOBAL
            return (local | glob | first) & spike_bool[None, :]
        B, S, D = x.shape
        spike_bool = _spike_indicators(x, Ws, bs)
        mask = _sparse_mask(S, spike_bool)
        Q = x @ Wq + bq
        K = x @ Wk + bk
        V = x @ Wv + bv
        scale = jnp.float32(1.0 / np.sqrt(D))
        scores = jnp.einsum('bid,bjd->bij', Q, K) * scale
        scores = jnp.where(mask[None, :, :], scores, -jnp.inf)
        w = jax.nn.softmax(scores, axis=-1)
        w = jnp.nan_to_num(w, nan=0.0)
        out = jnp.einsum('bij,bjd->bid', w, V)
        return out @ Wo + bo

    def _L1_ffn_ref(x, ffn_w1, ffn_b1, ffn_w2, ffn_b2, wq, wk, wv, wo, attn_mask, ffn_mask):
        import jax, jax.numpy as jnp
        import numpy as np
        NB, NOPS = (33, 19)
        D, H = (32, 128)
        B, S = (8, 256)
        CARRY_OPS = [0, 1, 2, 10, 11, 12, 13]

        def _build_masks():
            am = np.zeros((NB, NOPS), dtype=bool)
            fm = np.zeros((NB, NOPS), dtype=bool)
            fm[0, :] = True
            for b in range(1, 8):
                am[b, CARRY_OPS] = True
                fm[b, CARRY_OPS] = True
            am[8, [14, 15, 8, 9]] = True
            fm[8, [14, 15, 8, 9]] = True
            for b in range(16, 32):
                fm[b, [3, 4]] = True
            am[32, [10, 11, 12, 13]] = True
            fm[32, [5, 6, 7, 2, 4, 10, 11, 12, 13]] = True
            return (jnp.asarray(am), jnp.asarray(fm))
        scale = jnp.asarray(1.0 / np.sqrt(D), x.dtype)

        def step(h, p):
            op = jnp.argmax(h[0, 0, :NOPS])
            q = h @ p['wq'][op]
            k = h @ p['wk'][op]
            v = h @ p['wv'][op]
            attn = jax.nn.softmax(jnp.einsum('bqd,bkd->bqk', q, k) * scale, axis=-1)
            y = jnp.einsum('bqk,bkd->bqd', attn, v) @ p['wo'][op]
            h = jnp.where(p['am'][op], y, h)
            z = jax.nn.relu(h @ p['w1'][op] + p['b1'][op]) @ p['w2'][op] + p['b2'][op]
            h = jnp.where(p['fm'][op], z, h)
            return (h, None)
        xs = {'w1': ffn_w1, 'b1': ffn_b1, 'w2': ffn_w2, 'b2': ffn_b2, 'wq': wq, 'wk': wk, 'wv': wv, 'wo': wo, 'am': attn_mask, 'fm': ffn_mask}
        out, _ = jax.lax.scan(step, x, xs)
        return out

    def _gn(v, G=32, eps=1e-05):
        B_, C_, H_, W_ = v.shape
        g = v.reshape(B_, G, C_ // G, H_, W_)
        m = jnp.mean(g, axis=(2, 3, 4), keepdims=True)
        s = jnp.var(g, axis=(2, 3, 4), keepdims=True)
        return ((g - m) / jnp.sqrt(s + eps)).reshape(v.shape)

    def _ln_c(v, eps=1e-06):
        m = jnp.mean(v, axis=1, keepdims=True)
        s = jnp.var(v, axis=1, keepdims=True)
        return (v - m) / jnp.sqrt(s + eps)

    def _ln_t(v, eps=1e-05):
        m = jnp.mean(v, axis=-1, keepdims=True)
        s = jnp.var(v, axis=-1, keepdims=True)
        return (v - m) / jnp.sqrt(s + eps)

    def _to_tokens(v):
        B_, C_, H_, W_ = v.shape
        return v.reshape(B_, C_, H_ * W_).transpose(0, 2, 1)

    def _from_tokens(t, like):
        B_, C_, H_, W_ = like.shape
        return t.transpose(0, 2, 1).reshape(B_, C_, H_, W_)
    x = x + _L0_conv_ref(_gn(x), L0_conv_weight_comp, L0_conv_kpe)
    t = _to_tokens(x)
    t = t + _L1_attn_ref(_ln_t(t), L1_attn_Wq, L1_attn_bq, L1_attn_Wk, L1_attn_bk, L1_attn_Wv, L1_attn_bv, L1_attn_Wo, L1_attn_bo, L1_attn_Ws, L1_attn_bs)
    t = t + _L1_ffn_ref(_ln_t(t), L1_ffn_ffn_w1, L1_ffn_ffn_b1, L1_ffn_ffn_w2, L1_ffn_ffn_b2, L1_ffn_wq, L1_ffn_wk, L1_ffn_wv, L1_ffn_wo, L1_ffn_attn_mask, L1_ffn_ffn_mask)
    x = _from_tokens(t, x)
    return x

_drawn_inputs = setup_inputs


def setup_inputs(seed=0):
    import zlib

    import numpy as np

    out = dict(_drawn_inputs(seed))
    spreads = {'L1_attn_bq': (0.0, 0.316),
     'L1_attn_bk': (0.0, 0.8),
     'L1_attn_bv': (0.0, 0.1),
     'L1_attn_bo': (0.0, 0.1),
     'L1_ffn_ffn_b1': (0.0, 0.1),
     'L1_ffn_ffn_b2': (0.0, 0.1)}
    factors = {'L1_ffn_wq': 7.407, 'L1_ffn_wk': 6.278}
    for name, (base, spread) in spreads.items():
        noise = np.random.default_rng([zlib.crc32(name.encode()), seed]).standard_normal(out[name].shape)
        drawn = base * np.exp(spread * noise) if base else spread * noise
        out[name] = jnp.asarray(drawn.astype(out[name].dtype))
    for name, factor in factors.items():
        out[name] = (out[name] * factor).astype(out[name].dtype)
    return out
```

```python
import numpy as np
import concourse.bass as bass
from concourse import mybir
from contextlib import ExitStack

F32 = mybir.dt.float32
BF16 = mybir.dt.bfloat16
I32 = mybir.dt.int32
U32 = mybir.dt.uint32
U8 = mybir.dt.uint8
ALU = mybir.AluOpType
ACT = mybir.ActivationFunctionType
AX = mybir.AxisListType

P = 128
B, C, HW = 16, 32, 16
S = HW * HW
NH = S // P
NG = B * C // P
GB = B // NG
KS = 51
R = KS // 2
YH = P // HW
NE = 3 * YH
NQ = 9
Q0 = 2
NP13 = 13
NOPS, NSTEPS, HID = 19, 33, 128
SCALE = float(np.float32(1.0 / np.sqrt(C)))
DECAY = float(np.exp(np.float32(-0.1)))
NEG = -1e30
FLOOR = -1e29
NONE = 4 * NSTEPS
LIF_ITERS = 12
LIF_BLOCKS = -(-S // LIF_ITERS)


def group_of(o):
    a = abs(o)
    q = 0
    for n, c in enumerate([0, 1, 2, 4, 8]):
        if c <= a:
            q = n
    return 4 + (q if o >= 0 else -q)


def constants():
    c = {}
    c["ident"] = np.eye(P, dtype=np.float32)
    c["ones256"] = np.full((P, P), 1.0 / S, np.float32)
    blk = np.zeros((P, NG, C), np.float32)
    for q in range(GB):
        blk[q * C:(q + 1) * C, q, :] = 1
    c["blk"] = blk.reshape(P, P)
    col = np.zeros((P, NG, B), np.float32)
    for g in range(NG):
        for q in range(GB):
            col[q * C:(q + 1) * C, g, g * GB + q] = 1
    c["colsel"] = col.reshape(P, NG * B)
    i = np.arange(S)[:, None]
    j = np.arange(S)[None, :]
    ok = ((j <= i) & (j >= i - 32)) | (j % 16 == 0) | (j < 4)
    m = np.where(ok, 0.0, NEG).astype(np.float32).reshape(NH, P, S).transpose(1, 0, 2)
    c["maskc"] = np.ascontiguousarray(m).reshape(P, NH * S)
    sel = np.zeros((P, 2 * HW - 1, HW), np.float32)
    for a in range(2 * HW - 1):
        for x in range(HW):
            sel[x * 8 + group_of(a - 15) % 8, a, HW - 1 - x] = 1
    c["rowsel"] = sel.reshape(P, -1)
    cs = np.zeros((NQ * NQ, 2, 2 * HW - 1, 8), np.float32)
    for i_ in range(NQ):
        for j_ in range(NQ):
            for t in range(2):
                for s in range(8):
                    if (8 if (t == 1 and s == 0) else s) == i_:
                        for b in range(2 * HW - 1):
                            if group_of(b - 15) == j_:
                                cs[i_ * NQ + j_, t, b, s] = 1
    c["colexp"] = cs.reshape(NQ * NQ, -1)
    c["stepcode"] = np.tile(4.0 * np.arange(NSTEPS - 1, -1, -1, dtype=np.float32), (NOPS, 1)) - NONE
    c["rank"] = (NOPS - np.arange(NOPS, dtype=np.float32)).reshape(1, NOPS)
    return c


def build(nc, d):
    with ExitStack() as ctx:
        def sb(name, shape, dt=F32):
            return ctx.enter_context(nc.sbuf_tensor(name, shape, dt))

        def sem(name):
            return ctx.enter_context(nc.semaphore(name))

        ident = sb("ident", [P, P])
        identb = sb("identb", [P, P], BF16)
        ones256 = sb("ones256", [P, P])
        onesb = sb("onesb", [B, P], BF16)
        blk = sb("blk", [P, NG, C])
        colsel = sb("colsel", [P, NG, B])
        maskc = sb("maskc", [P, NH, S])
        rowsel = sb("rowsel", [P, 2 * HW - 1, HW])
        colexp = sb("colexp", [NQ * NQ, 2, 2 * HW - 1, 8])
        stepcode = sb("stepcode", [NOPS, NSTEPS])
        xin = sb("xin", [P, NH, B, C])
        xrev = sb("xrev", [P, NH, B, C])
        xc = sb("xc", [P, NH, B, C])
        sq = sb("sq", [P, NH, B, C])
        stdv = sb("stdv", [P, B, C])
        eps = sb("eps", [P, 1])
        rstd = sb("rstd", [P, B, C])
        xn = sb("xn", [P, C, NH, B])
        w81 = sb("w81", [NQ * NQ, C])
        gtab = sb("gtab", [P, 2, C, HW])
        toep = sb("toep", [P, C, NE, HW])
        toepk = sb("toepk", [P, NE, HW])
        tok = sb("tok", [P, NH, B, C])
        tokb = sb("tokb", [P, NH, B, C])
        xh = sb("xh", [P, NH, B, C])
        ysb = sb("ysb", [P, NH, B, C])
        mu = sb("mu", [P, NH * B])
        var = sb("var", [P, NH * B])
        half = sb("half", [P, NH * B], I32)
        inv = sb("inv", [P, NH * B])
        newt = sb("newt", [P, NH * B])
        xt = sb("xt", [P, NG, S])
        kt = sb("kt", [P, NG, S])
        hT = sb("hT", [P, NG, S])
        outT = sb("outT", [P, NG, S])
        qz = sb("qz", [P, B, S])
        v = sb("v", [P, NH, B, C + 1])
        prob = [sb(f"prob{i}", [P, NH, S]) for i in range(2)]
        probT = [sb(f"probT{i}", [P, NH, S]) for i in range(2)]
        nmax = sb("nmax", [P, B, NH])
        rsum = sb("rsum", [P, NG, NH * GB])
        negm = sb("negm", [P, NH, S], BF16)
        wqr = sb("wqr", [P, C])
        wkr = sb("wkr", [P, C])
        wsr = sb("wsr", [P, 1])
        bqr = sb("bqr", [P, 1])
        bkr = sb("bkr", [P, 1])
        bor = sb("bor", [P, C])
        bsr = sb("bsr", [B, 1])
        bvc = sb("bvc", [C, 1])
        bqs = sb("bqs", [P, 1])
        bdq = sb("bdq", [P, NG, C])
        bdk = sb("bdk", [P, NG, C])
        bdv = sb("bdv", [P, NG, C])
        bda = sb("bda", [P, NG, C])
        wsb = sb("wsb", [P, NG, B])
        bvo = sb("bvo", [P, C])
        cur = sb("cur", [B, S])
        mem = sb("mem", [B, S])
        dec = [sb(f"dec{i}", [B, S + 1]) for i in range(2)]
        diff = sb("diff", [B, S])
        dsum = sb("dsum", [C, C])
        dsumT = sb("dsumT", [C, C])
        dmax = sb("dmax", [1, 1])
        unsettled = sb("unsettled", [1, 1], I32)
        spk = sb("spk", [B, S], BF16)
        spm = sb("spm", [P, S])
        amr8 = sb("amr8", [NOPS, NSTEPS], U8)
        fmr8 = sb("fmr8", [NOPS, NSTEPS], U8)
        amf = sb("amf", [NOPS, NSTEPS])
        fmf = sb("fmf", [NOPS, NSTEPS])
        anyf = sb("anyf", [NOPS, NSTEPS])
        code = sb("code", [NOPS, NSTEPS])
        codem = sb("codem", [NOPS, NSTEPS])
        tabf = sb("tabf", [NOPS, NSTEPS + 1])
        tabi = sb("tabi", [NOPS, NSTEPS + 1], I32)
        tab = sb("tab", [1, NOPS * (NSTEPS + 1)], I32)
        row = sb("row", [1, C])
        top = sb("top", [1, 1])
        hit = sb("hit", [1, NOPS])
        rank = sb("rank", [1, NOPS])
        opi = sb("opi", [1, 1], I32)
        wL = sb("wL", [C, 2, GB, C])
        wR = sb("wR", [C, 2, C])
        w1z = sb("w1z", [P, GB, HID])
        w2s = sb("w2s", [HID, C])
        b1s = sb("b1s", [HID, 1])
        b2s = sb("b2s", [P, 1])
        relu = sb("relu", [HID, GB, NG, S])

        tabd = nc.dram_tensor("step_table", [NOPS, NSTEPS + 1], I32)
        bank = [ctx.enter_context(nc.psum_tensor(f"bank{i}", [P, 512], F32)) for i in range(8)]

        s_tabi = sem("step_table_ready")
        s_w1v = sem("attn_value_weights_loaded")
        s_std = sem("deviation_ready")
        s_xrev = sem("reversed_x_loaded")
        s_xin, s_cst, s_mask, s_wconv, s_w1l, s_tabl, s_tabmove = (sem(n) for n in (
            "x_loaded", "constants_loaded", "mask_loaded", "conv_weights_loaded", "attn_weights_loaded",
            "step_masks_loaded", "table_moved"))
        s_wA, s_wF, s_out = sem("step_attn_weights_loaded"), sem("step_ffn_weights_loaded"), sem("out_stored")
        s_dve, s_pool, s_act = sem("dve_chain"), sem("pool_chain"), sem("act_chain")
        s_g = sem("row_group_tables_in_psum")
        s_ga, s_gb = sem("gtab_a_copied"), sem("gtab_b_copied")
        s_mean, s_xc, s_sq, s_var, s_xn = (sem(n) for n in (
            "mean_in_psum", "x_centred", "x_squared", "var_in_psum", "xn_ready"))
        s_conv, s_zero = sem("conv_in_psum"), sem("zeros_written")
        s_ln, s_bd, s_curd, s_spk, s_negm = (sem(n) for n in (
            "layernormed", "block_weights_ready", "current_ready", "spikes_ready", "mask_ready"))
        s_vb = sem("v_bias_added")
        s_task, s_da, s_dd = sem("task_in_psum"), sem("task_drained_by_act"), sem("task_drained_by_dve")
        s_S, s_nm, s_P, s_T, s_PT = (sem(n) for n in (
            "scores_in_psum", "row_max_ready", "probs_ready", "probsT_in_psum", "probsT_copied"))
        s_row, s_op = sem("token0_in_psum"), sem("op_ready")
        s_fin = sem("out_ready")

        block = ctx.enter_context(nc.Block())

        def wait(eng, s, base, k):
            if type(base) is int and base + k <= 0:
                return
            eng.wait_ge(s, base + k)

        TOEP = "AD" * (NE // 2)
        PRE = "ADAD" + "A" + "D" + "D" + "AAAA" + "AAAA" + "AAAA" + "D"
        ATTY = "DDDD"
        H0 = "ADAD" + "ADAD"
        LPRE = "DD" + "ADAD" + "ADAD"
        LPOST = "ADAD"
        FF = "ADADADAD" + "ADAD"
        NPRE = len(TOEP)
        NATT0 = NPRE + len(PRE)
        NH0 = NATT0 + len(ATTY)
        NLOOP = NH0 + len(H0)
        LATT = LPRE + ATTY + LPOST
        STATIC = TOEP + PRE + ATTY + H0

        def count(who, owners):
            return sum(o == who for o in owners)

        W_FFN = 16 * (2 * GB + 2)
        W_STEP = 16 * 2 * (GB + 1)

        class Tasks:

            def __init__(self, owners, at=0, a=0, d=0):
                self.owners, self.at, self.a, self.d = owners, at, a, d

            def bank(self, k):
                return bank[4 + k % 4]

            def fill_wait(self, pe, k):
                if k >= 4:
                    who = self.owners[k - 4]
                    n = count(who, self.owners[:k - 3])
                    wait(pe, s_da if who == "A" else s_dd, self.a if who == "A" else self.d, n)
                elif k == 0:
                    wait(pe, s_da, self.a, 0)
                    wait(pe, s_dd, self.d, 0)

            def filled(self, eng, k):
                wait(eng, s_task, self.at, k + 1)

            def all_drained(self, eng):
                wait(eng, s_da, self.a, count("A", self.owners))
                wait(eng, s_dd, self.d, count("D", self.owners))

        st = Tasks(STATIC)

        def rep(ap, n):
            p, m = ap.shape
            return ap.unsqueeze(1).broadcast_to([p, n, m])

        @block.sync
        def _(sp):
            for h in range(NH):
                sp.dma_start(xrev[:, h, :, :].rearrange("p b c -> p (b c)"), d["xrev"][h * P:(h + 1) * P, :]).then_inc(s_xrev, 16)
            sp.dma_start(colexp[:, :, :, :].rearrange("k t b s -> k (t b s)"), d["colexp"]).then_inc(s_wconv, 16)
            for i in range(NQ):
                r0 = (i + Q0) * NP13 + Q0
                sp.dma_start(w81[i * NQ:(i + 1) * NQ, :], d["wct"][r0:r0 + NQ, :]).then_inc(s_wconv, 16)
            sp.dma_start(rowsel[:, :, :].rearrange("p a x -> p (a x)"), d["rowsel"]).then_inc(s_wconv, 16)
            kf = d["kpef"]
            for y in range(YH):
                shifted = bass.AP(tensor=kf.tensor, offset=(R - YH - y) * KS + R - (HW - 1), ap=[[1, HW], [KS, NE], [1, HW]])
                sp.dma_start(toepk[y * HW:(y + 1) * HW, :, :], shifted).then_inc(s_wconv, 16)
            for h in range(NH):
                sp.dma_start(xin[:, h, :, :].rearrange("p b c -> p (b c)"), d["xtok"][h * P:(h + 1) * P, :]).then_inc(s_xin, 16)
            sp.dma_start(maskc[:, :, :].rearrange("p h j -> p (h j)"), d["maskc"]).then_inc(s_mask, 16)

            sp.wait_ge(s_tabmove, 32)
            reg_code, reg_op, reg_r = (sp.alloc_register(n) for n in ("sp_code", "sp_op", "sp_round"))
            reg_f = sp.alloc_register("sp_ffn_loads")
            reg_step, reg_kind = sp.alloc_register("sp_step"), sp.alloc_register("sp_kind")
            sp.reg_mov(reg_r, 1)
            sp.reg_mov(reg_f, W_FFN)
            sp.wait_ge(s_op, 1)
            sp.reg_load(reg_op, opi[0:1, 0:1])
            op = sp.snap(reg_op, min_val=0, max_val=NOPS - 1)
            sp.reg_load(reg_code, tab[0:1, bass.ds(op * (NSTEPS + 1) + NSTEPS, 1)])
            with sp.While(lambda: sp.snap(reg_code) < NONE):
                sp.reg_alu(reg_step, reg_code, 2, ALU.logical_shift_right)
                sp.reg_alu(reg_kind, reg_code, 3, ALU.bitwise_and)
                b = sp.snap(reg_step, min_val=0, max_val=NSTEPS - 1)
                kind = sp.snap(reg_kind)
                op = sp.snap(reg_op, min_val=0, max_val=NOPS - 1)
                n = b * NOPS + op
                r = sp.snap(reg_r)
                for i, (left, right) in enumerate((("wqT", "wkT"), ("wvT", "wo"))):
                    for q in range(GB):
                        sp.dma_start(wL[:, i, q, :], d[left][bass.ds(n, 1), :, :].rearrange("o p n -> (o p) n")).then_inc(s_wA, 16)
                    sp.dma_start(wR[:, i, :], d[right][bass.ds(n, 1), :, :].rearrange("o p n -> (o p) n")).then_inc(s_wA, 16)
                for q in range(GB):
                    sp.dma_start(w1z[q * C:(q + 1) * C, q, :], d["w1"][bass.ds(n, 1), :, :].rearrange("o p n -> (o p) n")).then_inc(s_wF, 16)
                    sp.dma_start(b2s[q * C:(q + 1) * C, :], d["b2"][bass.ds(n, 1), :].rearrange("o p -> p o")).then_inc(s_wF, 16)
                sp.dma_start(w2s[:, :], d["w2"][bass.ds(n, 1), :, :].rearrange("o p n -> (o p) n")).then_inc(s_wF, 16)
                sp.dma_start(b1s[:, :], d["b1"][bass.ds(n, 1), :].rearrange("o p -> p o")).then_inc(s_wF, 16)
                f = sp.snap(reg_f)
                sp.wait_ge(s_wA, r * W_STEP)
                sp.wait_ge(s_wF, f)
                r = sp.snap(reg_r) + 1
                sp.wait_ge(s_op, r)
                sp.reg_alu(reg_r, reg_r, 1, ALU.add)
                sp.reg_alu(reg_f, reg_f, W_FFN, ALU.add)
                sp.reg_load(reg_op, opi[0:1, 0:1])
                op = sp.snap(reg_op, min_val=0, max_val=NOPS - 1)
                sp.reg_load(reg_code, tab[0:1, bass.ds(op * (NSTEPS + 1) + (NSTEPS - 1) - b, 1)])
            for i in range(2):
                sp.wait_ge(s_fin, i + 1)
                sp.dma_start(d["out"].rearrange("(g p) s -> p g s", p=P)[:, 2 * i:2 * i + 2, :],
                             outT[:, 2 * i:2 * i + 2, :]).then_inc(s_out, 16)
            sp.wait_ge(s_out, 32)

        @block.gpsimd
        def _(pool):
            def down(name, m):
                ap = d[name]
                return bass.AP(tensor=ap.tensor, offset=0, ap=[[0, GB], [m, C], [1, m]])
            pool.dma_start(amr8[:, :], d["amr"]).then_inc(s_tabl, 16)
            pool.dma_start(fmr8[:, :], d["fmr"]).then_inc(s_tabl, 16)
            pool.dma_start(stepcode[:, :], d["stepcode"]).then_inc(s_tabl, 16)
            for q in range(GB):
                rows = slice(q * C, (q + 1) * C)
                pool.dma_start(wqr[rows, :], d["Wq"]).then_inc(s_w1l, 16)
                pool.dma_start(wkr[rows, :], d["Wk"]).then_inc(s_w1l, 16)
                pool.dma_start(wsr[rows, :], d["Ws"]).then_inc(s_w1l, 16)
                pool.dma_start(bqr[rows, :], d["bq"].rearrange("(p o) -> p o", o=1)).then_inc(s_w1l, 16)
                pool.dma_start(bkr[rows, :], d["bk"].rearrange("(p o) -> p o", o=1)).then_inc(s_w1l, 16)
            pool.dma_start(bor[:, :], d["bo"].partition_broadcast(P)).then_inc(s_w1l, 16)
            pool.dma_start(bsr[:, :], d["bs"].partition_broadcast(B)).then_inc(s_w1l, 16)
            pool.dma_start(bvc[:, :], d["bv"].rearrange("(p o) -> p o", o=1)).then_inc(s_w1l, 16)
            for q in range(GB):
                pool.dma_start(wL[:, 1, q, :], d["WvT"]).then_inc(s_w1v, 16)
            pool.dma_start(wR[:, 1, :], d["Wo"]).then_inc(s_w1v, 16)
            nc.gpsimd.memset(qz[:, :, :], 0.0).then_inc(s_zero, 1)
            nc.gpsimd.memset(v[:, :, :, :], 1.0).then_inc(s_zero, 1)
            nc.gpsimd.memset(w1z[:, :, :], 0.0).then_inc(s_zero, 1)
            nc.gpsimd.memset(dsum[:, :], 0.0).then_inc(s_zero, 1)
            nc.gpsimd.memset(eps[:, :], 1e-5).then_inc(s_zero, 1)
            nc.gpsimd.memset(onesb[:, :], 1.0).then_inc(s_zero, 1)
            pool.wait_ge(s_cst, 16 * 5)
            nc.gpsimd.tensor_copy(identb[:, :], ident[:, :]).then_inc(s_zero, 1)
            pool.wait_ge(s_tabi, 1)
            pool.dma_start(tabd[:, :], tabi[:, :]).then_inc(s_tabmove, 16)
            pool.wait_ge(s_tabmove, 16)
            pool.dma_start(tab[0:1, :], tabd[:, :].rearrange("n m -> (n m)").unsqueeze(0)).then_inc(s_tabmove, 16)
            pool.wait_ge(s_bd, 2)
            for g in range(NG):
                k = NPRE + 7 + 2 * NG + g
                wait(pool, s_da, 0, count("A", STATIC[:k + 1]))
                for h in range(NH):
                    vg = v[:, h, g * GB:(g + 1) * GB, 0:C]
                    nc.gpsimd.tensor_tensor(vg, vg, rep(bvo[:, :], GB), ALU.add).then_inc(s_vb, 1)

        def attention_pe(pe, base, t, k0, keys, masked):
            def scores(b):
                if b >= 2:
                    wait(pe, s_P, base, b - 1)
                for ih in range(NH):
                    out = bank[b % 2][:, ih * S:(ih + 1) * S]
                    mm = pe.matmul(out, qz[:, b, ih * P:(ih + 1) * P], keys[:, b // GB, :], start=True, stop=not masked)
                    if masked:
                        mm = pe.matmul(out, identb[:, :], negm[:, ih, :], start=False, stop=True)
                mm.then_inc(s_S, 1)

            def turn(b):
                wait(pe, s_P, base, b + 1)
                if b >= 2:
                    wait(pe, s_PT, base, b - 1)
                for jh in range(NH):
                    for ih in range(NH):
                        mm = pe.transpose(bank[2 + b % 2][:, jh * S + ih * P:jh * S + (ih + 1) * P],
                                          prob[b % 2][:, ih, jh * P:(jh + 1) * P], ident[:, :])
                mm.then_inc(s_T, 1)

            def weigh(b):
                g, q = divmod(b, GB)
                if q == 0:
                    t.fill_wait(pe, k0 + g)
                wait(pe, s_PT, base, b + 1)
                y = t.bank(k0 + g)[:, 0:NH * GB * (C + 1)].rearrange("p (h q c) -> p h q c", h=NH, q=GB)
                for ih in range(NH):
                    for jh in range(NH):
                        mm = pe.matmul(y[:, ih, q, :], probT[b % 2][:, jh, ih * P:(ih + 1) * P],
                                       v[:, jh, b, :], start=(jh == 0), stop=(jh == NH - 1))
                if q == GB - 1:
                    mm.then_inc(s_task, 1)

            scores(0)
            for b in range(B):
                if b + 1 < B:
                    scores(b + 1)
                turn(b)
                if b >= 1:
                    weigh(b - 1)
            weigh(B - 1)

        @block.tensor
        def _(pe):
            pe.wait_ge(s_wconv, 16 * (2 + NQ + YH))
            for tb in range(2):
                for x in range(HW):
                    mm = pe.matmul(bank[tb][:, :].rearrange("p (c x) -> p c x", x=HW)[:, :, x],
                                   colexp[:, tb, 15 - x:31 - x, :].rearrange("k b s -> k (b s)"), w81[:, :], start=(x == 0), stop=(x == HW - 1),
                                   skip_group_check=True)
            mm.then_inc(s_g, 1)
            pe.wait_ge(s_cst, 16 * 5)
            pe.wait_ge(s_xrev, 16 * NH)
            for h in range(NH):
                mm = pe.matmul(bank[2][:, :], ones256[:, :], xrev[:, h, :, :].rearrange("p b c -> p (b c)"),
                               start=(h == 0), stop=(h == NH - 1))
            mm.then_inc(s_mean, 1)
            for e in range(NE):
                if e == 0:
                    pe.wait_ge(s_gb, 1)
                if e == YH:
                    pe.wait_ge(s_ga, 1)
                if e == 6:
                    pe.wait_ge(s_sq, NH)
                    for h in range(NH):
                        mm = pe.matmul(bank[3][:, :], ones256[:, :], sq[:, h, :, :].rearrange("p b c -> p (b c)"),
                                       start=(h == 0), stop=(h == NH - 1))
                    mm.then_inc(s_var, 1)
                st.fill_wait(pe, e)
                a0 = YH - e + HW - 1
                pe.matmul(st.bank(e)[:, :], rowsel[:, a0:a0 + YH, :],
                          gtab[:, 1 if e < YH else 0, :, :].rearrange("p c x -> p (c x)"),
                          start=True, stop=True).then_inc(s_task, 1)
            pe.wait_ge(s_xn, NH)
            st_toep = Tasks(TOEP)
            for k in range(2):
                cs = slice(16 * k, 16 * (k + 1))
                out = bank[k][:, :].rearrange("p (c h b) -> p c h b", c=16, h=NH)

                def window(c, w):
                    src = toepk[:, w * YH:(w + 1) * YH, :] if c is None else toep[:, c, w * YH:(w + 1) * YH, :]
                    return src.rearrange("p e x -> p (e x)")
                pe.matmul(out[:, :, :, :].rearrange("p c h b -> p (c h b)"), window(None, 1),
                          xn[:, cs, :, :].rearrange("p c h b -> p (c h b)"), start=True, stop=False, skip_group_check=True)
                pe.matmul(out[:, :, 1, :], window(None, 2), xn[:, cs, 0, :], start=False, stop=False, skip_group_check=True)
                pe.matmul(out[:, :, 0, :], window(None, 0), xn[:, cs, 1, :], start=False, stop=False, skip_group_check=True)
                if k == 0:
                    st_toep.all_drained(pe)
                for c in range(16 * k, 16 * (k + 1)):
                    pe.matmul(out[:, c - 16 * k, :, :].rearrange("p h b -> p (h b)"), window(c, 1),
                              xn[:, c, :, :].rearrange("p h b -> p (h b)"), start=False, stop=False, skip_group_check=True)
                    pe.matmul(out[:, c - 16 * k, 1, :], window(c, 2), xn[:, c, 0, :], start=False, stop=False, skip_group_check=True)
                    mm = pe.matmul(out[:, c - 16 * k, 0, :], window(c, 0), xn[:, c, 1, :], start=False,
                                   stop=(c % 16 == 15), skip_group_check=True)
                mm.then_inc(s_conv, 1)

            def transposed(t, k, src, g):
                t.fill_wait(pe, k)
                for h in range(NH):
                    mm = pe.transpose(t.bank(k)[:, h * P:(h + 1) * P],
                                      src[:, h, g * GB:(g + 1) * GB, :].rearrange("p b c -> p (b c)"), ident[:, :])
                mm.then_inc(s_task, 1)

            def product(t, k, lhsT, rhs, cols):
                t.fill_wait(pe, k)
                pe.matmul(t.bank(k)[:, 0:cols], lhsT, rhs, start=True, stop=True).then_inc(s_task, 1)

            def values(t, k, src, g, w):
                t.fill_wait(pe, k)
                for h in range(NH):
                    mm = pe.matmul(t.bank(k)[:, h * P:(h + 1) * P], src[:, g, h * P:(h + 1) * P], w, start=True, stop=True)
                mm.then_inc(s_task, 1)

            def flat(w):
                return w[:, :, :].rearrange("p g c -> p (g c)")

            pe.wait_ge(s_ln, 1)
            k = NPRE
            for g in range(NG):
                transposed(st, k, xh, g)
                k += 1
            pe.wait_ge(s_bd, 1)
            wait(pe, s_da, 0, count("A", STATIC[:NPRE + NG]))
            wait(pe, s_dd, 0, count("D", STATIC[:NPRE + NG]))
            for g in range(NG):
                if g == 0:
                    st.fill_wait(pe, k)
                mm = pe.matmul(st.bank(k)[0:B, 0:S], wsb[:, g, :], xt[:, g, :], start=(g == 0), stop=(g == NG - 1))
            mm.then_inc(s_task, 1)
            k += 1
            pe.wait_ge(s_w1v, 16 * (GB + 1))
            pe.wait_ge(s_w1l, 16 * (5 * GB + 3))
            product(st, k, wL[:, 1, :, :].rearrange("p q c -> p (q c)"), rep(wR[:, 1, :], NG), P)
            k += 1
            product(st, k, bvc[:, :].broadcast_to([C, P]), wR[:, 1, :], C)
            k += 1
            for g in range(NG):
                product(st, k, flat(bdq), xt[:, g, :], S)
                k += 1
            for g in range(NG):
                product(st, k, flat(bdk), xt[:, g, :], S)
                k += 1
            pe.wait_ge(s_bd, 2)
            for g in range(NG):
                values(st, k, xt, g, flat(bdv))
                k += 1
            pe.wait_ge(s_spk, 1)
            pe.wait_ge(s_zero, 7)
            product(st, k, onesb[:, :], spk[:, :], S)
            k += 1
            pe.wait_ge(s_negm, 1)
            pe.wait_ge(s_vb, NG * NH)
            wait(pe, s_da, 0, count("A", STATIC[:NATT0]))
            attention_pe(pe, 0, st, k, kt, True)
            k += NG
            pe.wait_ge(s_ln, 2)
            for g in range(NG):
                transposed(st, k, xh, g)
                k += 1
            for g in range(NG):
                transposed(st, k, tok, g)
                k += 1
            st.all_drained(pe)

            def token0():
                pe.matmul(bank[0][0:1, 0:C], hT[0:C, 0, 0:1], ident[0:C, 0:C], start=True, stop=True).then_inc(s_row, 1)

            token0()
            names = ("pe_code", "pe_op", "pe_round", "pe_att", "pe_task", "pe_da", "pe_dd")
            reg_code, reg_op, reg_r, reg_att, reg_task, reg_da, reg_dd = (pe.alloc_register(n) for n in names)
            reg_step, reg_kind = pe.alloc_register("pe_step"), pe.alloc_register("pe_kind")
            pe.reg_mov(reg_r, 1)
            pe.reg_mov(reg_att, B)
            pe.reg_mov(reg_task, len(STATIC))
            pe.reg_mov(reg_da, count("A", STATIC))
            pe.reg_mov(reg_dd, count("D", STATIC))
            pe.wait_ge(s_tabmove, 32)
            pe.wait_ge(s_op, 1)
            pe.reg_load(reg_op, opi[0:1, 0:1])
            op = pe.snap(reg_op, min_val=0, max_val=NOPS - 1)
            pe.reg_load(reg_code, tab[0:1, bass.ds(op * (NSTEPS + 1) + NSTEPS, 1)])
            with pe.While(lambda: pe.snap(reg_code) < NONE):
                pe.reg_alu(reg_step, reg_code, 2, ALU.logical_shift_right)
                pe.reg_alu(reg_kind, reg_code, 3, ALU.bitwise_and)
                b = pe.snap(reg_step, min_val=0, max_val=NSTEPS - 1)
                kind = pe.snap(reg_kind)
                r = pe.snap(reg_r)
                with pe.If(kind >= 2):
                    att = pe.snap(reg_att)
                    t = Tasks(LATT, pe.snap(reg_task), pe.snap(reg_da), pe.snap(reg_dd))
                    pe.wait_ge(s_wA, r * W_STEP)
                    product(t, 0, wL[:, 0, :, :].rearrange("p q c -> p (q c)"), rep(wR[:, 0, :], NG), P)
                    product(t, 1, wL[:, 1, :, :].rearrange("p q c -> p (q c)"), rep(wR[:, 1, :], NG), P)
                    wait(pe, s_dd, t.d, 2)
                    for g in range(NG):
                        product(t, 2 + g, flat(bda), hT[:, g, :], S)
                    for g in range(NG):
                        values(t, 2 + NG + g, hT, g, flat(bdv))
                    wait(pe, s_da, t.a, count("A", LPRE))
                    wait(pe, s_dd, t.d, count("D", LPRE))
                    attention_pe(pe, att, t, len(LPRE), hT, False)
                    wait(pe, s_dd, t.d, count("D", LPRE + ATTY))
                    for g in range(NG):
                        transposed(t, len(LPRE + ATTY) + g, ysb, g)
                    t.all_drained(pe)
                    pe.reg_alu(reg_att, reg_att, B, ALU.add)
                    pe.reg_alu(reg_task, reg_task, len(LATT), ALU.add)
                    pe.reg_alu(reg_da, reg_da, count("A", LATT), ALU.add)
                    pe.reg_alu(reg_dd, reg_dd, count("D", LATT), ALU.add)
                with pe.If(kind != 2):
                    t = Tasks(FF, pe.snap(reg_task), pe.snap(reg_da), pe.snap(reg_dd))
                    pe.wait_ge(s_wF, r * W_FFN)
                    k = 0
                    for gp in range(NG // 2):
                        for q in range(GB):
                            product(t, k, w1z[:, q, :], hT[:, 2 * gp:2 * gp + 2, :].rearrange("p g s -> p (g s)"), 2 * S)
                            k += 1
                    wait(pe, s_da, t.a, count("A", FF[:2 * GB]))
                    wait(pe, s_dd, t.d, count("D", FF[:2 * GB]))
                    for g in range(NG):
                        for q in range(GB):
                            mm = pe.matmul(t.bank(k)[q * C:(q + 1) * C, 0:S], w2s[:, :], relu[:, q, g, :],
                                           start=True, stop=True, tile_position=(0, q * C))
                        mm.then_inc(s_task, 1)
                        k += 1
                    t.all_drained(pe)
                    pe.reg_alu(reg_task, reg_task, len(FF), ALU.add)
                    pe.reg_alu(reg_da, reg_da, count("A", FF), ALU.add)
                    pe.reg_alu(reg_dd, reg_dd, count("D", FF), ALU.add)
                token0()
                r = pe.snap(reg_r) + 1
                pe.wait_ge(s_op, r)
                pe.reg_alu(reg_r, reg_r, 1, ALU.add)
                pe.reg_load(reg_op, opi[0:1, 0:1])
                op = pe.snap(reg_op, min_val=0, max_val=NOPS - 1)
                pe.reg_load(reg_code, tab[0:1, bass.ds(op * (NSTEPS + 1) + (NSTEPS - 1) - b, 1)])

        def attention_act(act, base):
            for b in range(B):
                wait(act, s_nm, base, b + 1)
                if b >= 2:
                    wait(act, s_T, base, b - 1)
                for ih in range(NH):
                    e = nc.scalar.activation(prob[b % 2][:, ih, :], bank[b % 2][:, ih * S:(ih + 1) * S], ACT.Exp,
                                             bias=nmax[:, b, ih:ih + 1])
                e.then_inc(s_P, 1)

        @block.scalar
        def _(act):
            for name, t in (("ones256", ones256[:, :]), ("ident", ident[:, :]),
                            ("blk", blk[:, :, :].rearrange("p g c -> p (g c)")),
                            ("colsel", colsel[:, :, :].rearrange("p g b -> p (g b)"))):
                act.dma_start(t, d[name]).then_inc(s_cst, 16)
            act.dma_start(rank[:, :], d["rank"]).then_inc(s_cst, 16)
            act.wait_ge(s_g, 1)
            nc.scalar.activation(gtab[:, 0, :, :].rearrange("p c x -> p (c x)"), bank[0][:, :], ACT.Copy).then_inc(s_ga, 1)
            for h in range(NH):
                act.wait_ge(s_xc, h + 1)
                nc.scalar.activation(sq[:, h, :, :], xc[:, h, :, :], ACT.Square).then_inc(s_sq, 1)
            act.wait_ge(s_zero, 7)
            for e in range(0, NE, 2):
                if e == 6:
                    act.wait_ge(s_var, 1)
                    nc.scalar.activation(stdv[:, :, :].rearrange("p b c -> p (b c)"), bank[3][:, :], ACT.Sqrt,
                                         bias=eps[:, :]).then_inc(s_std, 1)
                st.filled(act, e)
                nc.scalar.activation(toep[:, :, e, :], st.bank(e)[:, :].rearrange("p (c x) -> p c x", x=HW),
                                     ACT.Copy).then_inc(s_da, 1)

            def copy(t, k, dst, src):
                t.filled(act, k)
                nc.scalar.activation(dst, src, ACT.Copy).then_inc(s_da, 1)

            k = NPRE
            for g in range(0, NG, 2):
                copy(st, k + g, xt[:, g, :], st.bank(k + g)[:, 0:S])
            k += NG
            act.wait_ge(s_w1l, 16 * (5 * GB + 3))
            st.filled(act, k)
            nc.scalar.activation(cur[:, :], st.bank(k)[0:B, 0:S], ACT.Identity, bias=bsr[:, :]).then_inc(s_da, 1)
            k += 3
            act.wait_ge(s_zero, 7)
            act.wait_ge(s_bd, 1)
            for g in range(NG):
                st.filled(act, k)
                for q in range(GB):
                    rows = slice(q * C, (q + 1) * C)
                    cp = nc.scalar.activation(qz[rows, g * GB + q, :], st.bank(k)[rows, 0:S], ACT.Identity,
                                              bias=bqs[rows, :], scale=SCALE)
                cp.then_inc(s_da, 1)
                k += 1
            for g in range(NG):
                st.filled(act, k)
                nc.scalar.activation(kt[:, g, :], st.bank(k)[:, 0:S], ACT.Identity, bias=bkr[:, :]).then_inc(s_da, 1)
                k += 1

            def copy_values(t, k, g):
                t.filled(act, k)
                for h in range(NH):
                    cp = nc.scalar.activation(v[:, h, g * GB:(g + 1) * GB, 0:C],
                                              t.bank(k)[:, h * P:(h + 1) * P].rearrange("p (b c) -> p b c", c=C), ACT.Copy)
                cp.then_inc(s_da, 1)

            for g in range(NG):
                copy_values(st, k, g)
                k += 1
            attention_act(act, 0)
            k = NH0
            for dst in (hT, outT):
                for g in range(0, NG, 2):
                    copy(st, k + g, dst[:, g, :], st.bank(k + g)[:, 0:S])
                k += NG

            names = ("act_code", "act_op", "act_round", "act_att", "act_task", "act_da")
            reg_code, reg_op, reg_r, reg_att, reg_task, reg_da = (act.alloc_register(n) for n in names)
            reg_step, reg_kind = act.alloc_register("act_step"), act.alloc_register("act_kind")
            act.reg_mov(reg_r, 1)
            act.reg_mov(reg_att, B)
            act.reg_mov(reg_task, len(STATIC))
            act.wait_ge(s_tabmove, 32)
            act.wait_ge(s_op, 1)
            act.reg_load(reg_op, opi[0:1, 0:1])
            op = act.snap(reg_op, min_val=0, max_val=NOPS - 1)
            act.reg_load(reg_code, tab[0:1, bass.ds(op * (NSTEPS + 1) + NSTEPS, 1)])
            with act.While(lambda: act.snap(reg_code) < NONE):
                act.reg_alu(reg_step, reg_code, 2, ALU.logical_shift_right)
                act.reg_alu(reg_kind, reg_code, 3, ALU.bitwise_and)
                b = act.snap(reg_step, min_val=0, max_val=NSTEPS - 1)
                kind = act.snap(reg_kind)
                r = act.snap(reg_r)
                with act.If(kind >= 2):
                    att = act.snap(reg_att)
                    t = Tasks(LATT, act.snap(reg_task))
                    k = 2
                    for g in range(NG):
                        if LATT[k] == "A":
                            t.filled(act, k)
                            for q in range(GB):
                                rows = slice(q * C, (q + 1) * C)
                                cp = nc.scalar.activation(qz[rows, g * GB + q, :], t.bank(k)[rows, 0:S], ACT.Copy)
                            cp.then_inc(s_da, 1)
                        k += 1
                    for g in range(NG):
                        if LATT[k] == "A":
                            copy_values(t, k, g)
                        k += 1
                    attention_act(act, att)
                    k = len(LPRE + ATTY)
                    for g in range(0, NG, 2):
                        copy(t, k + g, hT[:, g, :], t.bank(k + g)[:, 0:S])
                    act.reg_alu(reg_att, reg_att, B, ALU.add)
                    act.reg_alu(reg_task, reg_task, len(LATT), ALU.add)
                with act.If(kind != 2):
                    t = Tasks(FF, act.snap(reg_task))
                    act.wait_ge(s_wF, r * W_FFN)
                    for k in range(0, 2 * GB, 2):
                        gp, q = divmod(k, GB)
                        t.filled(act, k)
                        nc.scalar.activation(relu[:, q, 2 * gp:2 * gp + 2, :].rearrange("p g s -> p (g s)"),
                                             t.bank(k)[:, :], ACT.Relu, bias=b1s[:, :]).then_inc(s_da, 1)
                    for g in range(0, NG, 2):
                        k = 2 * GB + g
                        t.filled(act, k)
                        nc.scalar.activation(hT[:, g, :], t.bank(k)[:, 0:S], ACT.Identity, bias=b2s[:, :]).then_inc(s_da, 1)
                    act.reg_alu(reg_task, reg_task, len(FF), ALU.add)
                r = act.snap(reg_r) + 1
                act.wait_ge(s_op, r)
                act.reg_alu(reg_r, reg_r, 1, ALU.add)
                act.reg_load(reg_op, opi[0:1, 0:1])
                op = act.snap(reg_op, min_val=0, max_val=NOPS - 1)
                act.reg_load(reg_code, tab[0:1, bass.ds(op * (NSTEPS + 1) + (NSTEPS - 1) - b, 1)])

        @block.vector
        def _(dve):
            chain = {"base": 0, "n": 0}

            def link(ins):
                chain["n"] += 1
                ins.then_inc(s_dve, 1)
                dve.wait_ge(s_dve, chain["base"] + chain["n"])

            dve.wait_ge(s_tabl, 48)
            nc.vector.tensor_copy(amf[:, :], amr8[:, :])
            nc.vector.memset(tabf[:, 0:1], float(NONE))
            link(nc.vector.tensor_copy(fmf[:, :], fmr8[:, :]))
            nc.vector.tensor_tensor(anyf[:, :], amf[:, :], fmf[:, :], ALU.max)
            link(nc.vector.scalar_tensor_tensor(code[:, :], amf[:, :], 2.0, fmf[:, :], ALU.mult, ALU.add))
            link(nc.vector.tensor_tensor(code[:, :], code[:, :], stepcode[:, :], ALU.add))
            link(nc.vector.tensor_tensor(code[:, :], code[:, :], anyf[:, :], ALU.mult))
            link(nc.vector.tensor_scalar(codem[:, :], code[:, :], float(NONE), None, ALU.add))
            link(nc.vector.tensor_tensor_scan(tabf[:, 1:NSTEPS + 1], codem[:, :], codem[:, :], float(NONE), ALU.min, ALU.min))
            nc.vector.tensor_copy(tabi[:, :], tabf[:, :]).then_inc(s_tabi, 1)

            dve.wait_ge(s_g, 1)
            nc.vector.tensor_copy(gtab[:, 1, :, :].rearrange("p c x -> p (c x)"), bank[1][:, :]).then_inc(s_gb, 1)
            dve.wait_ge(s_mean, 1)
            dve.wait_ge(s_xrev, 16 * NH)
            for h in range(NH):
                nc.vector.tensor_tensor(xc[:, h, :, :].rearrange("p b c -> p (b c)"),
                                        xrev[:, h, :, :].rearrange("p b c -> p (b c)"), bank[2][:, :],
                                        ALU.subtract).then_inc(s_xc, 1)

            def drain_toep(e):
                st.filled(dve, e)
                nc.vector.tensor_copy(toep[:, :, e, :], st.bank(e)[:, :].rearrange("p (c x) -> p c x", x=HW)).then_inc(s_dd, 1)

            for e in (1, 3, 5):
                drain_toep(e)
            dve.wait_ge(s_std, 1)
            link(nc.vector.reciprocal(rstd[:, :, :], stdv[:, :, :]))
            dve.wait_ge(s_xc, NH)
            for h in range(NH):
                nc.vector.tensor_tensor(xn[:, :, h, :].rearrange("p c b -> p b c"), xc[:, h, :, :], rstd[:, :, :],
                                        ALU.mult).then_inc(s_xn, 1)
            for e in range(7, NE, 2):
                drain_toep(e)
            dve.wait_ge(s_cst, 16 * 5)
            dve.wait_ge(s_w1l, 16 * (5 * GB + 3))
            nc.vector.tensor_tensor(bdq[:, :, :], rep(wqr[:, :], NG), blk[:, :, :], ALU.mult)
            nc.vector.tensor_tensor(bdk[:, :, :], rep(wkr[:, :], NG), blk[:, :, :], ALU.mult)
            nc.vector.tensor_scalar(bqs[:, :], bqr[:, :], SCALE, None, ALU.mult)
            nc.vector.tensor_scalar(wsb[:, :, :], colsel[:, :, :], wsr[:, :], None, ALU.mult).then_inc(s_bd, 1)
            dve.wait_ge(s_xin, 16 * NH)
            for k in range(2):
                dve.wait_ge(s_conv, k + 1)
                cs = slice(16 * k, 16 * (k + 1))
                for h in range(NH):
                    last = nc.vector.tensor_tensor(
                        tok[:, h, :, cs], xin[:, h, :, cs],
                        bank[k][:, :].rearrange("p (c h b) -> p h b c", c=16, h=NH)[:, h, :, :], ALU.add)
            link(last)

            def layernorm():
                t2 = tok[:, :, :, :].rearrange("p h b c -> p (h b) c")
                c2 = xc[:, :, :, :].rearrange("p h b c -> p (h b) c")
                s2 = sq[:, :, :, :].rearrange("p h b c -> p (h b) c")
                x2 = xh[:, :, :, :].rearrange("p h b c -> p (h b) c")

                def wide(a):
                    return a[:, :].unsqueeze(2).broadcast_to([P, NH * B, C])
                link(nc.vector.tensor_reduce(mu[:, :], t2, AX.X, ALU.add))
                link(nc.vector.tensor_scalar(mu[:, :], mu[:, :], -1.0 / C, None, ALU.mult))
                link(nc.vector.tensor_tensor(c2, t2, wide(mu), ALU.add))
                link(nc.vector.tensor_tensor(s2, c2, c2, ALU.mult))
                link(nc.vector.tensor_reduce(var[:, :], s2, AX.X, ALU.add))
                link(nc.vector.tensor_scalar(var[:, :], var[:, :], 1.0 / C, 1e-5, ALU.mult, ALU.add))
                link(nc.vector.tensor_scalar(half[:, :], var[:, :].bitcast(I32), 1, None, ALU.logical_shift_right))
                link(nc.vector.tensor_scalar(inv[:, :].bitcast(I32), half[:, :], -1.0, float(0x5f3759df), ALU.mult, ALU.add))
                for _n in range(3):
                    link(nc.vector.scalar_tensor_tensor(newt[:, :], inv[:, :], -0.5, inv[:, :], ALU.mult, ALU.mult))
                    link(nc.vector.tensor_tensor(newt[:, :], newt[:, :], var[:, :], ALU.mult))
                    link(nc.vector.scalar_tensor_tensor(inv[:, :], newt[:, :], 1.5, inv[:, :], ALU.add, ALU.mult))
                nc.vector.tensor_tensor(x2, c2, wide(inv), ALU.mult).then_inc(s_ln, 1)

            layernorm()

            def drain_half(t, k, dst):
                for g in range(1, NG, 2):
                    t.filled(dve, k + g)
                    nc.vector.tensor_copy(dst[:, g, :], t.bank(k + g)[:, 0:S]).then_inc(s_dd, 1)

            def drain_block(t, k, dst, scale):
                t.filled(dve, k)
                nc.vector.scalar_tensor_tensor(dst[:, :, :].rearrange("p g c -> p (g c)"), t.bank(k)[:, 0:P], scale,
                                               blk[:, :, :].rearrange("p g c -> p (g c)"), ALU.mult, ALU.mult).then_inc(s_dd, 1)

            k = NPRE
            drain_half(st, k, xt)
            k += NG + 1
            st.filled(dve, k)
            nc.vector.tensor_tensor(bdv[:, :, :].rearrange("p g c -> p (g c)"), st.bank(k)[:, 0:P],
                                    blk[:, :, :].rearrange("p g c -> p (g c)"), ALU.mult).then_inc(s_dd, 1)
            k += 1
            st.filled(dve, k)
            link(nc.vector.tensor_copy(bvo[:, :], st.bank(k)[:, 0:C]))
            nc.vector.memset(dec[1][:, :], DECAY).then_inc(s_dd, 1)
            dve.wait_ge(s_dd, count("D", STATIC[:k + 1]))
            nc.vector.memset(dec[0][:, :], DECAY).then_inc(s_bd, 1)

            wait(dve, s_da, 0, count("A", STATIC[:NPRE + NG + 1]))
            dve.wait_ge(s_zero, 7)
            dve.wait_ge(s_bd, 2)

            def sweeps():
                for i in range(LIF_ITERS):
                    link(nc.vector.tensor_tensor_scan(mem[:, :], dec[i % 2][:, 0:S], cur[:, :], 0.0, ALU.mult, ALU.add))
                    link(nc.vector.tensor_scalar(dec[1 - i % 2][:, 1:S + 1], mem[:, :], 1.0, DECAY, ALU.is_lt, ALU.mult))
                link(nc.vector.tensor_tensor(diff[:, :], dec[0][:, 0:S], dec[1][:, 0:S], ALU.not_equal))
                link(nc.vector.tensor_reduce(dsum[0:B, 0:1], diff[:, :], AX.X, ALU.max))
                link(nc.vector.transpose(dsumT[:, :], dsum[:, :]))
                link(nc.vector.tensor_reduce(dmax[:, :], dsumT[0:1, :], AX.X, ALU.max))
                link(nc.vector.tensor_copy(unsettled[:, :], dmax[:, :]))

            sweeps()
            reg_u, reg_c = dve.alloc_register("dve_unsettled"), dve.alloc_register("dve_chain")
            dve.reg_mov(reg_c, chain["n"])
            dve.reg_load(reg_u, unsettled[0:1, 0:1])
            with dve.If(dve.snap(reg_u) != 0):
                with dve.Fori(0, LIF_BLOCKS) as _i:
                    with dve.If(dve.snap(reg_u) != 0):
                        chain["base"], chain["n"] = dve.snap(reg_c), 0
                        sweeps()
                        dve.reg_alu(reg_c, reg_c, chain["n"], ALU.add)
                        dve.reg_load(reg_u, unsettled[0:1, 0:1])
            chain["base"], chain["n"] = dve.snap(reg_c), 0
            nc.vector.tensor_scalar(spk[:, :], mem[:, :], 1.0, None, ALU.is_ge).then_inc(s_spk, 1)
            nc.vector.tensor_tensor(tokb[:, :, :, :].rearrange("p h b c -> p (h b) c"),
                                    tok[:, :, :, :].rearrange("p h b c -> p (h b) c"), rep(bor[:, :], NH * B), ALU.add)
            k = NATT0 - 1
            st.filled(dve, k)
            link(nc.vector.tensor_scalar(spm[:, :], st.bank(k)[:, 0:S], 0.5, NEG, ALU.is_lt, ALU.mult))
            dve.wait_ge(s_mask, 16)
            nc.vector.tensor_tensor(negm[:, :, :], maskc[:, :, :], rep(spm[:, :], NH), ALU.add).then_inc(s_negm, 1)
            dve.wait_ge(s_negm, 1)
            nc.vector.memset(mu[:, 0:1], 0.0).then_inc(s_dd, 1)

            def attention_dve(base, t, k0, masked, y_out):
                def row_max(b):
                    wait(dve, s_S, base, b + 1)
                    m = nc.vector.tensor_reduce(nmax[:, b, :], bank[b % 2][:, :].rearrange("p (h j) -> p h j", h=NH), AX.X,
                                                ALU.max, negate=True)
                    if masked:
                        link(m)
                        m = nc.vector.tensor_scalar(nmax[:, b, :], nmax[:, b, :], -FLOOR, None, ALU.min)
                    m.then_inc(s_nm, 1)

                def copy_probT(b):
                    wait(dve, s_T, base, b + 1)
                    nc.vector.tensor_copy(probT[b % 2][:, :, :].rearrange("p h i -> p (h i)"), bank[2 + b % 2][:, :]).then_inc(s_PT, 1)

                def divide(g):
                    t.filled(dve, k0 + g)
                    y = t.bank(k0 + g)[:, 0:NH * GB * (C + 1)].rearrange("p (n c) -> p n c", c=C + 1)
                    if masked:
                        link(nc.vector.tensor_scalar(rsum[:, g, :], y[:, :, C], 1e-30, None, ALU.max))
                        link(nc.vector.reciprocal(rsum[:, g, :], rsum[:, g, :]))
                    else:
                        link(nc.vector.reciprocal(rsum[:, g, :], y[:, :, C]))
                    for h in range(NH):
                        last = nc.vector.tensor_tensor(
                            y_out[:, h, g * GB:(g + 1) * GB, :], y[:, h * GB:(h + 1) * GB, 0:C],
                            rsum[:, g, h * GB:(h + 1) * GB].unsqueeze(2).broadcast_to([P, GB, C]), ALU.mult)
                    last.then_inc(s_dd, 1)

                row_max(0)
                for b in range(B):
                    if b + 1 < B:
                        row_max(b + 1)
                    copy_probT(b)
                    if b % GB == 1 and b > GB:
                        divide(b // GB - 1)
                divide(NG - 1)

            attention_dve(0, st, NATT0, True, ysb)
            dve.wait_ge(s_dd, count("D", STATIC[:NH0]))
            link(nc.vector.tensor_tensor(tok[:, :, :, :].rearrange("p h b c -> p (h b c)"),
                                         tokb[:, :, :, :].rearrange("p h b c -> p (h b c)"),
                                         ysb[:, :, :, :].rearrange("p h b c -> p (h b c)"), ALU.add))
            layernorm()
            drain_half(st, NH0, hT)
            drain_half(st, NH0 + NG, outT)

            def pick_op(r):
                dve.wait_ge(s_row, r)
                link(nc.vector.tensor_copy(row[:, :], bank[0][0:1, 0:C]))
                link(nc.vector.tensor_reduce(top[:, :], row[:, 0:NOPS], AX.X, ALU.max))
                link(nc.vector.tensor_scalar(hit[:, :], row[:, 0:NOPS], top[:, :], None, ALU.is_ge))
                link(nc.vector.tensor_tensor(hit[:, :], hit[:, :], rank[:, :], ALU.mult))
                link(nc.vector.tensor_reduce(top[:, :], hit[:, :], AX.X, ALU.max))
                nc.vector.tensor_scalar(opi[:, :], top[:, :], -1.0, float(NOPS), ALU.mult, ALU.add).then_inc(s_op, 1)

            pick_op(1)
            names = ("dve_code", "dve_op", "dve_round", "dve_att", "dve_task")
            reg_code, reg_op, reg_r, reg_att, reg_task = (dve.alloc_register(n) for n in names)
            reg_d = dve.alloc_register("dve_drained")
            dve.reg_alu(reg_c, reg_c, chain["n"], ALU.add)
            reg_step, reg_kind = dve.alloc_register("dve_step"), dve.alloc_register("dve_kind")
            dve.reg_mov(reg_r, 1)
            dve.reg_mov(reg_att, B)
            dve.reg_mov(reg_task, len(STATIC))
            dve.reg_mov(reg_d, count("D", STATIC))
            dve.wait_ge(s_tabmove, 32)
            dve.wait_ge(s_op, 1)
            dve.reg_load(reg_op, opi[0:1, 0:1])
            op = dve.snap(reg_op, min_val=0, max_val=NOPS - 1)
            dve.reg_load(reg_code, tab[0:1, bass.ds(op * (NSTEPS + 1) + NSTEPS, 1)])
            with dve.While(lambda: dve.snap(reg_code) < NONE):
                dve.reg_alu(reg_step, reg_code, 2, ALU.logical_shift_right)
                dve.reg_alu(reg_kind, reg_code, 3, ALU.bitwise_and)
                b = dve.snap(reg_step, min_val=0, max_val=NSTEPS - 1)
                kind = dve.snap(reg_kind)
                r = dve.snap(reg_r)
                with dve.If(kind >= 2):
                    att = dve.snap(reg_att)
                    chain["base"], chain["n"] = dve.snap(reg_c), 0
                    t = Tasks(LATT, dve.snap(reg_task), d=dve.snap(reg_d))
                    drain_block(t, 0, bda, SCALE)
                    drain_block(t, 1, bdv, 1.0)
                    k = 2
                    for g in range(NG):
                        if LATT[k] == "D":
                            t.filled(dve, k)
                            for q in range(GB):
                                rows = slice(q * C, (q + 1) * C)
                                cp = nc.vector.tensor_copy(qz[rows, g * GB + q, :], t.bank(k)[rows, 0:S])
                            cp.then_inc(s_dd, 1)
                        k += 1
                    for g in range(NG):
                        if LATT[k] == "D":
                            t.filled(dve, k)
                            for h in range(NH):
                                cp = nc.vector.tensor_copy(v[:, h, g * GB:(g + 1) * GB, 0:C],
                                                           t.bank(k)[:, h * P:(h + 1) * P].rearrange("p (b c) -> p b c", c=C))
                            cp.then_inc(s_dd, 1)
                        k += 1
                    attention_dve(att, t, k, False, ysb)
                    drain_half(t, k + NG, hT)
                    dve.reg_alu(reg_c, reg_c, chain["n"], ALU.add)
                    dve.reg_alu(reg_att, reg_att, B, ALU.add)
                    dve.reg_alu(reg_task, reg_task, len(LATT), ALU.add)
                    dve.reg_alu(reg_d, reg_d, count("D", LATT), ALU.add)
                with dve.If(kind != 2):
                    t = Tasks(FF, dve.snap(reg_task))
                    dve.wait_ge(s_wF, r * W_FFN)
                    for k in range(1, 2 * GB, 2):
                        gp, q = divmod(k, GB)
                        t.filled(dve, k)
                        nc.vector.tensor_scalar(relu[:, q, 2 * gp:2 * gp + 2, :].rearrange("p g s -> p (g s)"),
                                                t.bank(k)[:, :], b1s[:, :], 0.0, ALU.add, ALU.max).then_inc(s_dd, 1)
                    for g in range(1, NG, 2):
                        k = 2 * GB + g
                        t.filled(dve, k)
                        nc.vector.tensor_scalar(hT[:, g, :], t.bank(k)[:, 0:S], b2s[:, :], None, ALU.add).then_inc(s_dd, 1)
                    dve.reg_alu(reg_task, reg_task, len(FF), ALU.add)
                    dve.reg_alu(reg_d, reg_d, count("D", FF), ALU.add)
                r = dve.snap(reg_r) + 1
                chain["base"], chain["n"] = dve.snap(reg_c), 0
                pick_op(r)
                dve.reg_alu(reg_c, reg_c, chain["n"], ALU.add)
                dve.wait_ge(s_op, r)
                dve.reg_alu(reg_r, reg_r, 1, ALU.add)
                dve.reg_load(reg_op, opi[0:1, 0:1])
                op = dve.snap(reg_op, min_val=0, max_val=NOPS - 1)
                dve.reg_load(reg_code, tab[0:1, bass.ds(op * (NSTEPS + 1) + (NSTEPS - 1) - b, 1)])
            r = dve.snap(reg_r)
            dve.wait_ge(s_row, r)
            for i in range(2):
                gs = slice(2 * i, 2 * i + 2)
                nc.vector.tensor_tensor(outT[:, gs, :], outT[:, gs, :], hT[:, gs, :], ALU.add).then_inc(s_fin, 1)


def kernel(**inputs):
    import numpy as _np
    import concourse.bacc as _bacc
    from concourse import mybir as _mybir
    from concourse.bass_utils import run_bass_kernel_spmd as _run

    g = {k: _np.asarray(a) for k, a in inputs.items()}
    steps = NSTEPS * NOPS

    def swapped(a):
        return _np.ascontiguousarray(_np.swapaxes(a, -1, -2))

    arrays = {
        "xtok": _np.ascontiguousarray(g["x"].reshape(B, C, S).transpose(2, 0, 1)).reshape(S, B * C),
        "xrev": _np.ascontiguousarray(g["x"][:, :, :, ::-1].reshape(B, C, S).transpose(2, 0, 1)).reshape(S, B * C),
        "wct": swapped(g["L0_conv_weight_comp"]),
        "kpef": _np.ascontiguousarray(g["L0_conv_kpe"][0, 0, ::-1, ::-1]),
        "Wq": g["L1_attn_Wq"], "Wk": g["L1_attn_Wk"], "WvT": swapped(g["L1_attn_Wv"]), "Wo": g["L1_attn_Wo"],
        "Ws": g["L1_attn_Ws"], "bq": g["L1_attn_bq"], "bk": g["L1_attn_bk"], "bv": g["L1_attn_bv"],
        "bo": g["L1_attn_bo"], "bs": g["L1_attn_bs"],
        "wqT": swapped(g["L1_ffn_wq"]).reshape(steps, C, C), "wkT": swapped(g["L1_ffn_wk"]).reshape(steps, C, C),
        "wvT": swapped(g["L1_ffn_wv"]).reshape(steps, C, C), "wo": g["L1_ffn_wo"].reshape(steps, C, C),
        "w1": g["L1_ffn_ffn_w1"].reshape(steps, C, HID), "b1": g["L1_ffn_ffn_b1"].reshape(steps, HID),
        "w2": g["L1_ffn_ffn_w2"].reshape(steps, HID, C), "b2": g["L1_ffn_ffn_b2"].reshape(steps, C),
        "amr": _np.ascontiguousarray(g["L1_ffn_attn_mask"].T[:, ::-1]),
        "fmr": _np.ascontiguousarray(g["L1_ffn_ffn_mask"].T[:, ::-1]),
    }
    arrays.update(constants())
    nc = _bacc.Bacc("TRN2", target_bir_lowering=False, num_devices=1)
    d = {}
    for name, a in arrays.items():
        a = arrays[name] = _np.ascontiguousarray(a)
        d[name] = nc.dram_tensor(name + "_dram", a.shape, _mybir.dt.from_np(a.dtype), kind="ExternalInput").ap()
    d["out"] = nc.dram_tensor("out_dram", (B * C, S), _mybir.dt.float32, kind="ExternalOutput").ap()
    build(nc, d)
    r = _run(nc, [{name + "_dram": a for name, a in arrays.items()}], core_ids=[0])
    return r.results[0]["out_dram"].reshape(B, C, HW, HW)
```

```python
import numpy as np
import concourse.bass as bass
from concourse import mybir
from contextlib import ExitStack

F32 = mybir.dt.float32
BF16 = mybir.dt.bfloat16
I32 = mybir.dt.int32
U32 = mybir.dt.uint32
U8 = mybir.dt.uint8
U16 = mybir.dt.uint16
ALU = mybir.AluOpType
ACT = mybir.ActivationFunctionType
AX = mybir.AxisListType

P = 128
B, C, HW = 16, 32, 16
S = HW * HW
NH = S // P
NG = B * C // P
GB = B // NG
KS = 51
R = KS // 2
YH = P // HW
NE = 3 * YH
NQ = 9
Q0 = 2
NP13 = 13
NOPS, NSTEPS, HID = 19, 33, 128
SCALE = float(np.float32(1.0 / np.sqrt(C)))
DECAY = float(np.exp(np.float32(-0.1)))
NEG = -1e30
FLOOR = -1e29
NONE = 4 * NSTEPS
CG = C // GB
LIF_ITERS = 12
LIF_BLOCKS = -(-S // LIF_ITERS)


def group_of(o):
    a = abs(o)
    q = 0
    for n, c in enumerate([0, 1, 2, 4, 8]):
        if c <= a:
            q = n
    return 4 + (q if o >= 0 else -q)


def bf16_bits(a):
    return (np.asarray(a) * 0x3F80).astype(np.uint16)


def constants():
    ident = np.eye(P, dtype=np.float32)
    blk = np.zeros((P, NG, C), np.float32)
    for q in range(GB):
        blk[q * C:(q + 1) * C, q, :] = 1
    col = np.zeros((P, NG, B), np.float32)
    for g in range(NG):
        for q in range(GB):
            col[q * C:(q + 1) * C, g, g * GB + q] = 1
    rows = np.arange(P)
    same = (rows[:, None] // 32 == rows[None, :] // 32) & (rows[:, None] % B == rows[None, :] % B)
    pick = np.zeros((P, GB, B), np.float32)
    for q in range(GB):
        for b in range(B):
            pick[q * 32 + b, q, b] = 1
    stepcode = np.zeros((P, NSTEPS), np.float32)
    stepcode[:NOPS] = 4.0 * np.arange(NSTEPS - 1, -1, -1) - NONE
    rank = np.tile(NOPS - np.arange(NOPS, dtype=np.float32), (P, 1))
    c = {"constf": np.concatenate([ident, blk.reshape(P, -1), col.reshape(P, -1), same.astype(np.float32),
                                   pick.reshape(P, -1), stepcode, rank], axis=1)}
    i = np.arange(S)[:, None]
    j = np.arange(S)[None, :]
    ok = ((j <= i) & (j >= i - 32)) | (j % 16 == 0) | (j < 4)
    m = np.where(ok, 0.0, NEG).astype(np.float32).reshape(NH, P, S).transpose(1, 0, 2)
    c["maskc"] = np.ascontiguousarray(m).reshape(P, NH * S)
    sel = np.zeros((P, 2 * HW - 1, HW))
    for a in range(2 * HW - 1):
        for x in range(HW):
            sel[x * 8 + group_of(a - 15) % 8, a, HW - 1 - x] = 1
    cs = np.zeros((P, 2, 2 * HW - 1, 8))
    for i_ in range(NQ):
        for j_ in range(NQ):
            for t in range(2):
                for s in range(8):
                    if (8 if (t == 1 and s == 0) else s) == i_:
                        for b in range(2 * HW - 1):
                            if group_of(b - 15) == j_:
                                cs[i_ * NQ + j_, t, b, s] = 1
    c["constb"] = bf16_bits(np.concatenate([np.eye(P), cs.reshape(P, -1), sel.reshape(P, -1)], axis=1))
    return c


def build(nc, d):
    with ExitStack() as ctx:
        def sb(name, shape, dt=F32):
            return ctx.enter_context(nc.sbuf_tensor(name, shape, dt))

        def sem(name):
            return ctx.enter_context(nc.semaphore(name))

        NB = 2 * HW - 1
        constf = sb("constf", [P, P + NG * C + NG * B + P + GB * B + NSTEPS + NOPS])
        constb = sb("constb", [P, P + 2 * NB * 8 + NB * HW], U16)
        at = [0]

        def part(t, n):
            a = t[:, at[0]:at[0] + n]
            at[0] += n
            return a
        ident = part(constf, P)
        blk = part(constf, NG * C)
        colsel = part(constf, NG * B)
        pairs = part(constf, P)
        pick = part(constf, GB * B)
        stepcode = part(constf, NSTEPS)[0:NOPS, :]
        rank = part(constf, NOPS)[0:1, :]
        at[0] = 0
        identb = part(constb, P).bitcast(BF16)
        colexp = part(constb, 2 * NB * 8)[0:NQ * NQ, :].bitcast(BF16)
        rowsel = part(constb, NB * HW).bitcast(BF16)
        ones256 = sb("ones256", [P, P])
        onesb = sb("onesb", [B, P], BF16)
        maskc = sb("maskc", [P, NH, S])
        eps = sb("eps", [P, 1])
        xin = sb("xin", [P, NH, B, C])
        xrev = sb("xrev", [P, NH, B, C])
        xcc = sb("xcc", [P, C, NH, B])
        sqc = sb("sqc", [P, C, NH, B])
        w81 = sb("w81", [NQ * NQ, C])
        wres = sb("wres", [NQ * NQ, 2, C])
        w81p = sb("w81p", [NQ * NQ, 3, C], BF16)
        gtab = sb("gtab", [P, 2, 3, C, HW], BF16)
        big = sb("big", [P, C * NE * HW])
        toep = big[:, :].rearrange("p (c e x) -> p c e x", c=C, e=NE)
        toepk = sb("toepk", [P, NE, HW])
        convr = sb("convr", [P, CG, S])
        vhalf = sb("vhalf", [P, CG])
        stdv = sb("stdv", [P, CG])
        rstd = sb("rstd", [P, CG])
        tok = sb("tok", [P, NH, B, C])
        tokb = sb("tokb", [P, NH, B, C])
        xh = sb("xh", [P, NH, B, C])
        xc = sb("xc", [P, NH, B, C])
        sq = sb("sq", [P, NH, B, C])
        mu = sb("mu", [P, NH * B])
        var = sb("var", [P, NH * B])
        dev = sb("dev", [P, NH * B])
        inv = sb("inv", [P, NH * B])
        table = sb("table", [1, 1])
        seen = sb("seen", [1, 1])
        xt = sb("xt", [P, NG, S])
        kt = sb("kt", [P, NG, S])
        yT = sb("yT", [P, NG, S])
        hT = sb("hT", [P, NG, S])
        outT = sb("outT", [P, NG, S])
        qz = sb("qz", [P, B, S])
        v = sb("v", [P, NH, B, C])
        NPB, NTB = 3, 2 * GB
        prob = [sb(f"prob{i}", [P, NH, S]) for i in range(NPB)]
        relu = big[:, 0:GB * NG * S].rearrange("p (q g s) -> p q g s", q=GB, g=NG)
        probT = [big[:, (GB * NG + NH * i) * S:(GB * NG + NH * (i + 1)) * S].rearrange("p (h s) -> p h s", h=NH)
                 for i in range(NTB)]
        nmax = sb("nmax", [P, B, NH])
        esum = sb("esum", [P, B, NH])
        einv = sb("einv", [P, B, NH])
        negm = sb("negm", [P, NH, S], BF16)
        wl1 = sb("wl1", [P, 3 * C + 4])
        wqr, wkr, bor = wl1[:, 0:C], wl1[:, C:2 * C], wl1[:, 2 * C:3 * C]
        wsr, bqr, bkr, bsr = (wl1[:, 3 * C + i:3 * C + i + 1] for i in range(4))
        wl2 = sb("wl2", [C, GB * C + C + 1])
        wvl, wor, bvc = wl2[:, 0:GB * C], wl2[:, GB * C:GB * C + C], wl2[:, GB * C + C:GB * C + C + 1]
        bqs = sb("bqs", [P, 1])
        bdq = sb("bdq", [P, NG * C])
        bdk = sb("bdk", [P, NG * C])
        bdv = sb("bdv", [P, NG * C])
        bda = sb("bda", [P, NG * C])
        wsb = sb("wsb", [P, NG, B])
        bvo = sb("bvo", [P, C])
        cur = sb("cur", [B, S])
        mem = sb("mem", [B, S])
        dec = [sb(f"dec{i}", [B, S + 1]) for i in range(2)]
        diff = sb("diff", [B, S])
        dsum = sb("dsum", [C, C])
        dsumT = sb("dsumT", [C, C])
        dmax = sb("dmax", [1, 1])
        unsettled = sb("unsettled", [1, 1], I32)
        spk = sb("spk", [B, S], BF16)
        spm = sb("spm", [P, S])
        masks8 = sb("masks8", [NOPS, 2, NSTEPS], U8)
        maskf = sb("maskf", [NOPS, 2, NSTEPS])
        anyf = sb("anyf", [NOPS, NSTEPS])
        code = sb("code", [NOPS, NSTEPS])
        codem = sb("codem", [NOPS, NSTEPS])
        tabf = sb("tabf", [NOPS, NSTEPS + 1])
        tabi = sb("tabi", [NOPS, NSTEPS + 1], I32)
        tab = sb("tab", [1, NOPS * (NSTEPS + 1)], I32)
        row = sb("row", [1, C])
        top = sb("top", [1, 1])
        hit = sb("hit", [1, NOPS])
        opi = sb("opi", [1, 1], I32)
        wa = sb("wa", [C, 2 * GB * C + 2 * C])
        w1r = sb("w1r", [P, HID])
        wf = sb("wf", [HID, C + 2])
        w1z = sb("w1z", [P, GB, HID])
        wfs = sb("wfs", [HID, C + 2])
        w2s, b1s, b2s = wfs[:, 0:C], wfs[:, C:C + 1], wfs[:, C + 1:C + 2]

        tabd = nc.dram_tensor("step_table", [NOPS, NSTEPS + 1], I32)
        bank = [ctx.enter_context(nc.psum_tensor(f"bank{i}", [P, 512], F32)) for i in range(8)]

        s_xrev, s_xin, s_cb, s_cf, s_mask, s_w81, s_kpe, s_wl1, s_wl2, s_tabl = (sem(n) for n in (
            "reversed_x_loaded", "x_loaded", "constb_loaded", "constf_loaded", "mask_loaded", "w81_loaded", "kpe_loaded",
            "attn_weights_loaded", "attn_value_weights_loaded", "step_masks_loaded"))
        s_tabi, s_tabmove = sem("step_table_ready"), sem("step_table_moved")
        s_wA, s_wF, s_out = sem("step_attn_weights_loaded"), sem("step_ffn_weights_loaded"), sem("out_stored")
        s_dve = sem("dve_chain")
        s_zero, s_w81p = sem("pool_constants_written"), sem("w81_parts_ready")
        s_gb, s_ga = sem("table_b_in_psum"), sem("table_a_in_psum")
        s_gcopy = [sem("table_a_banks_copied"), sem("table_b_banks_copied")]
        s_mean, s_xc, s_sq, s_vh, s_vhs, s_vp, s_std, s_rstd = (sem(n) for n in (
            "mean_in_psum", "x_centred", "x_squared", "half_vars_in_psum", "half_vars_copied", "vars_in_psum",
            "deviation_ready", "rstd_ready"))
        s_conv, s_convA, s_convD = sem("conv_in_psum"), sem("conv_scaled_by_act"), sem("conv_scaled_by_dve")
        s_lnc, s_lns, s_lnv, s_lnd, s_ln = (sem(n) for n in (
            "half_centred", "half_squared", "variance_ready", "ln_deviation_ready", "half_normed"))
        s_bd, s_bdv, s_bvo, s_spk, s_negm, s_vb = (sem(n) for n in (
            "block_weights_ready", "value_weights_ready", "value_bias_ready", "spikes_ready", "mask_ready", "v_bias_added"))
        s_t2 = sem("residual_after_attention_ready")
        s_task, s_da, s_dd = sem("task_in_psum"), sem("task_drained_by_act"), sem("task_drained_by_dve")
        s_S, s_nm, s_P, s_ri, s_Pn, s_T, s_PT = (sem(n) for n in (
            "scores_in_psum", "row_max_ready", "exponentials_ready", "row_sums_inverted", "probs_ready",
            "probsT_in_psum", "probsT_copied"))
        s_w1z, s_row, s_op, s_seen, s_wp, s_bd2 = sem("ffn_weights_placed"), sem("token0_in_psum"), sem("op_ready"), sem("op_seen_by_pool"), sem(
            "step_weight_products_in_psum"), sem("step_block_weights_ready")
        s_fin = sem("out_ready")

        block = ctx.enter_context(nc.Block())

        def wait(eng, s, base, k):
            if type(base) is int and base + k <= 0:
                return
            eng.wait_ge(s, base + k)

        RING = 3
        SCORES = (0, 1, 4)
        AHEAD = len(SCORES)
        TOEP = "D" * NE
        CONVT = "DD"
        PRE = "ADAD" + "A" + "D" + "D" + "AAAA" + "AAAA" + "AAAA" + "D"
        ATTY = "AAAA"
        YTOK = "DD"
        H0 = "AAAA" + "ADAD"
        LPRE = "ADAD" + "ADAD"
        FF = "ADADAD" + "AD" + "AD" + "AD"
        K_CONVT = len(TOEP)
        K_PRE = K_CONVT + len(CONVT)
        K_CUR = K_PRE + NG
        K_Q = K_CUR + 3
        K_V = K_Q + 2 * NG
        K_CNT = K_V + NG
        K_ATT = K_CNT + 1
        K_YTOK = K_ATT + len(ATTY)
        K_H0 = K_YTOK + len(YTOK)
        STATIC = TOEP + CONVT + PRE + ATTY + YTOK + H0
        assert K_H0 + len(H0) == len(STATIC) and K_ATT == len(TOEP + CONVT + PRE)
        LATT = LPRE + ATTY
        HORDER = [("H", 0), ("H", 1), ("H", 2), ("H", 3), ("H", 4), ("H", 5), ("Z", 0), ("Z", 1), ("H", 6), ("H", 7),
                  ("Z", 2), ("Z", 3)]
        assert len(HORDER) == len(FF)

        def count(who, owners):
            return sum(o == who for o in owners)

        W_FFN = 16 * (GB + 1)

        class Tasks:

            def __init__(self, owners, at=0, a=0, d=0):
                self.owners, self.at, self.a, self.d = owners, at, a, d

            def bank(self, k):
                return bank[8 - RING + k % RING]

            def fill_wait(self, pe, k):
                if k >= RING:
                    who = self.owners[k - RING]
                    n = count(who, self.owners[:k - RING + 1])
                    wait(pe, s_da if who == "A" else s_dd, self.a if who == "A" else self.d, n)
                elif k == 0:
                    wait(pe, s_da, self.a, 0)
                    wait(pe, s_dd, self.d, 0)

            def filled(self, eng, k):
                wait(eng, s_task, self.at, k + 1)

            def drained(self, eng, k):
                wait(eng, s_da, self.a, count("A", self.owners[:k]))
                wait(eng, s_dd, self.d, count("D", self.owners[:k]))

        st = Tasks(STATIC)

        def rep(ap, n):
            p, m = ap.shape
            return ap.unsqueeze(1).broadcast_to([p, n, m])

        def flat(ap):
            names = "abcd"[:len(ap.shape) - 1]
            return ap.rearrange(f"p {' '.join(names)} -> p ({' '.join(names)})")

        @block.sync
        def _(sp):
            sp.dma_start(w81[:, :], d["w81"]).then_inc(s_w81, 16)
            sp.dma_start(constb[:, :], d["constb"]).then_inc(s_cb, 16)
            sp.dma_start(flat(xrev[:, :, :, :]).rearrange("p (h n) -> p h n", h=NH),
                         d["xrev"].rearrange("(h p) n -> p h n", p=P)).then_inc(s_xrev, 16)
            sp.dma_start(constf[:, :], d["constf"]).then_inc(s_cf, 16)
            kf = d["kpef"]
            for y in range(YH):
                shifted = bass.AP(tensor=kf.tensor, offset=(R - YH - y) * KS + R - (HW - 1), ap=[[1, HW], [KS, NE], [1, HW]])
                sp.dma_start(toepk[y * HW:(y + 1) * HW, :, :], shifted).then_inc(s_kpe, 16)
            sp.dma_start(wl1[:, :], d["wl1"]).then_inc(s_wl1, 16)
            sp.dma_start(wl2[:, :], d["wl2"]).then_inc(s_wl2, 16)
            sp.dma_start(flat(xin[:, :, :, :]).rearrange("p (h n) -> p h n", h=NH),
                         d["xtok"].rearrange("(h p) n -> p h n", p=P)).then_inc(s_xin, 16)
            sp.dma_start(masks8[:, :, :], d["masks"]).then_inc(s_tabl, 16)
            sp.dma_start(flat(maskc[:, :, :]), d["maskc"]).then_inc(s_mask, 16)
            sp.wait_ge(s_tabi, 1)
            sp.dma_start(tabd[:, :], tabi[:, :]).then_inc(s_tabmove, 16)
            sp.wait_ge(s_tabmove, 16)
            sp.dma_start(tab[0:1, :], tabd[:, :].rearrange("n m -> (n m)").unsqueeze(0)).then_inc(s_tabmove, 16)

            reg_f = sp.alloc_register("sp_ffn_loads")
            sp.reg_mov(reg_f, W_FFN)
            reg_code, reg_op, reg_step, reg_kind, reg_r = (
                sp.alloc_register("sp_" + n) for n in ("code", "op", "step", "kind", "round"))
            sp.reg_mov(reg_r, 1)
            sp.wait_ge(s_tabmove, 32)
            sp.wait_ge(s_op, 1)
            sp.reg_load(reg_op, opi[0:1, 0:1])
            op = sp.snap(reg_op, min_val=0, max_val=NOPS - 1)
            sp.reg_load(reg_code, tab[0:1, bass.ds(op * (NSTEPS + 1) + NSTEPS, 1)])
            with sp.While(lambda: sp.snap(reg_code) < NONE):
                sp.reg_alu(reg_step, reg_code, 2, ALU.logical_shift_right)
                sp.reg_alu(reg_kind, reg_code, 3, ALU.bitwise_and)
                b = sp.snap(reg_step, min_val=0, max_val=NSTEPS - 1)
                kind = sp.snap(reg_kind)
                op = sp.snap(reg_op, min_val=0, max_val=NOPS - 1)
                n = b * NOPS + op
                r = sp.snap(reg_r)
                sp.dma_start(wa[:, :], d["wa"][bass.ds(n, 1), :, :].rearrange("o p n -> (o p) n")).then_inc(s_wA, 16)
                for q in range(GB):
                    sp.dma_start(w1r[q * C:(q + 1) * C, :], d["w1"][bass.ds(n, 1), :, :].rearrange("o p n -> (o p) n")).then_inc(s_wF, 16)
                sp.dma_start(wf[:, :], d["wf"][bass.ds(n, 1), :, :].rearrange("o p n -> (o p) n")).then_inc(s_wF, 16)
                f = sp.snap(reg_f)
                sp.wait_ge(s_wA, r * 16)
                sp.wait_ge(s_wF, f)
                r = sp.snap(reg_r) + 1
                sp.wait_ge(s_op, r)
                sp.reg_alu(reg_r, reg_r, 1, ALU.add)
                sp.reg_alu(reg_f, reg_f, W_FFN, ALU.add)
                sp.reg_load(reg_op, opi[0:1, 0:1])
                op = sp.snap(reg_op, min_val=0, max_val=NOPS - 1)
                sp.reg_load(reg_code, tab[0:1, bass.ds(op * (NSTEPS + 1) + (NSTEPS - 1) - b, 1)])
            for i in range(2):
                sp.wait_ge(s_fin, i + 1)
                sp.dma_start(d["out"].rearrange("(g p) s -> p g s", p=P)[:, 2 * i:2 * i + 2, :],
                             outT[:, 2 * i:2 * i + 2, :]).then_inc(s_out, 16)
            sp.wait_ge(s_out, 32)

        def attention_pool(pool, reg_att=None):
            for b in range(B):
                if reg_att is None:
                    pool.wait_ge(s_ri, b + 1)
                else:
                    att = pool.snap(reg_att) + 1
                    pool.wait_ge(s_ri, att)
                    pool.reg_alu(reg_att, reg_att, 1, ALU.add)
                for ih in range(NH):
                    last = nc.gpsimd.tensor_scalar(prob[b % NPB][:, ih, :], prob[b % NPB][:, ih, :], einv[:, b, ih:ih + 1], 1.0,
                                                   ALU.mult, ALU.mult)
                last.then_inc(s_Pn, 1)

        @block.gpsimd
        def _(pool):
            nc.gpsimd.memset(ones256[:, :], 1.0 / S).then_inc(s_zero, 1)
            nc.gpsimd.memset(eps[:, :], 1e-5).then_inc(s_zero, 1)
            nc.gpsimd.memset(onesb[:, :], 1.0).then_inc(s_zero, 1)
            nc.gpsimd.memset(dsum[:, :], 0.0).then_inc(s_zero, 1)
            nc.gpsimd.memset(qz[:, :, :], 0.0).then_inc(s_zero, 1)
            nc.gpsimd.memset(w1z[:, :, :], 0.0).then_inc(s_zero, 1)
            pool.wait_ge(s_bvo, 1)
            for g in range(NG):
                wait(pool, s_da, 0, count("A", STATIC[:K_V + g + 1]))
                for h in range(NH):
                    vg = v[:, h, g * GB:(g + 1) * GB, :]
                    nc.gpsimd.tensor_tensor(vg, vg, rep(bvo[:, :], GB), ALU.add).then_inc(s_vb, 1)
            attention_pool(pool)
            reg_att = pool.alloc_register("pool_att")
            pool.reg_mov(reg_att, B)
            reg_code, reg_op, reg_step, reg_kind, reg_r = (
                pool.alloc_register("pool_" + n) for n in ("code", "op", "step", "kind", "round"))
            pool.reg_mov(reg_r, 1)
            pool.wait_ge(s_tabmove, 32)
            pool.wait_ge(s_op, 1)
            pool.reg_load(reg_op, opi[0:1, 0:1])
            op = pool.snap(reg_op, min_val=0, max_val=NOPS - 1)
            pool.reg_load(reg_code, tab[0:1, bass.ds(op * (NSTEPS + 1) + NSTEPS, 1)])
            with pool.While(lambda: pool.snap(reg_code) < NONE):
                pool.reg_alu(reg_step, reg_code, 2, ALU.logical_shift_right)
                pool.reg_alu(reg_kind, reg_code, 3, ALU.bitwise_and)
                b = pool.snap(reg_step, min_val=0, max_val=NSTEPS - 1)
                kind = pool.snap(reg_kind)
                nc.gpsimd.memset(seen[:, :], 0.0).then_inc(s_seen, 1)
                with pool.If(kind >= 2):
                    attention_pool(pool, reg_att)
                r = pool.snap(reg_r) + 1
                pool.wait_ge(s_op, r)
                pool.reg_alu(reg_r, reg_r, 1, ALU.add)
                pool.reg_load(reg_op, opi[0:1, 0:1])
                op = pool.snap(reg_op, min_val=0, max_val=NOPS - 1)
                pool.reg_load(reg_code, tab[0:1, bass.ds(op * (NSTEPS + 1) + (NSTEPS - 1) - b, 1)])

        def product_pe(pe, t, k, lhsT, rhs, cols):
            t.fill_wait(pe, k)
            pe.matmul(t.bank(k)[:, 0:cols], lhsT, rhs, start=True, stop=True).then_inc(s_task, 1)

        def attention_pe(pe, base, t, k0, keys, masked):
            def scores(b):
                if b >= AHEAD:
                    wait(pe, s_P, base, b - AHEAD + 1)
                for ih in range(NH):
                    mm = pe.matmul(bank[SCORES[b % AHEAD]][:, ih * S:(ih + 1) * S], qz[:, b, ih * P:(ih + 1) * P],
                                   keys[:, b // GB, :], start=(ih == 0 or not masked), stop=not masked)
                if not masked:
                    mm.then_inc(s_S, 1)

            def add_mask(b):
                for ih in range(NH):
                    mm = pe.matmul(bank[SCORES[b % AHEAD]][:, ih * S:(ih + 1) * S], identb, negm[:, ih, :],
                                   start=False, stop=(ih == NH - 1))
                mm.then_inc(s_S, 1)

            def turn(b):
                wait(pe, s_Pn, base, b + 1)
                if b >= 2:
                    wait(pe, s_PT, base, b - 1)
                for jh in range(NH):
                    for ih in range(NH):
                        mm = pe.transpose(bank[2 + b % 2][:, jh * S + ih * P:jh * S + (ih + 1) * P],
                                          prob[b % NPB][:, ih, jh * P:(jh + 1) * P], ident)
                mm.then_inc(s_T, 1)

            def weigh(g):
                t.fill_wait(pe, k0 + g)
                wait(pe, s_PT, base, GB * (g + 1))
                for jh in range(NH):
                    for q in range(GB):
                        b = g * GB + q
                        mm = pe.matmul(t.bank(k0 + g)[q * C:(q + 1) * C, 0:S], v[:, jh, b, :], probT[b % NTB][:, jh, :],
                                       start=(jh == 0), stop=(jh == NH - 1), tile_position=(0, q * C))
                mm.then_inc(s_task, 1)

            for b in range(AHEAD):
                scores(b)
            if masked:
                pe.wait_ge(s_spk, 1)
                product_pe(pe, st, K_CNT, onesb[:, :], spk[:, :], S)
                pe.wait_ge(s_negm, 1)
                for b in range(AHEAD):
                    add_mask(b)
            for b in range(B):
                if b + AHEAD < B:
                    scores(b + AHEAD)
                    if masked:
                        add_mask(b + AHEAD)
                turn(b)
                if b % GB == 0 and b:
                    weigh(b // GB - 1)
            weigh(NG - 1)

        @block.tensor
        def _(pe):
            pe.wait_ge(s_cb, 16)
            pe.wait_ge(s_w81p, 1)
            cexp = colexp.rearrange("k (t b s) -> k t (b s)", t=2, s=8)

            def table(tb, x, out):
                return pe.matmul(out[:, (x % 5) * 3 * C:(x % 5 + 1) * 3 * C], cexp[:, tb, (HW - 1 - x) * 8:(2 * HW - 1 - x) * 8],
                                 flat(w81p[:, :, :]), start=True, stop=True)
            for x in range(HW):
                mm = table(1, x, bank[4 + x // 5])
            mm.then_inc(s_gb, 1)
            pe.wait_ge(s_zero, 3)
            pe.wait_ge(s_xrev, 16)
            for h in range(NH):
                mm = pe.matmul(bank[1][:, :], ones256[:, :], flat(xrev[:, h, :, :]), start=(h == 0), stop=(h == NH - 1))
            mm.then_inc(s_mean, 1)
            for x in range(HW):
                if x == HW - 1:
                    pe.wait_ge(s_xc, NH)
                mm = table(0, x, bank[(2, 3, 0, 1)[x // 5]])
            mm.then_inc(s_ga, 1)
            for e in range(NE):
                if e == 0:
                    pe.wait_ge(s_gcopy[1], 4)
                if e == YH:
                    pe.wait_ge(s_gcopy[0], 4)
                if e == 12:
                    pe.wait_ge(s_sq, 2)
                    for cg in range(CG):
                        mm = pe.matmul(bank[2][:, cg:cg + 1], flat(sqc[:, cg * GB:(cg + 1) * GB, :, :]), ones256[:, 0:1],
                                       start=True, stop=True)
                    mm.then_inc(s_vh, 1)
                if e == 16:
                    pe.wait_ge(s_vhs, 1)
                    pe.wait_ge(s_cf, 16)
                    pe.matmul(bank[3][:, 0:CG], pairs, vhalf[:, :], start=True, stop=True).then_inc(s_vp, 1)
                st.fill_wait(pe, e)
                a0 = YH - e + HW - 1
                for i in range(3):
                    mm = pe.matmul(st.bank(e)[:, :], rowsel[:, a0 * HW:(a0 + YH) * HW],
                                   flat(gtab[:, 1 if e < YH else 0, i, :, :]), start=(i == 0), stop=(i == 2))
                mm.then_inc(s_task, 1)
            st.drained(pe, K_CONVT)
            pe.wait_ge(s_std, 1)
            for j in range(CG // 2):
                for cg in (2 * j, 2 * j + 1):
                    for hi in range(NH):
                        for q in range(GB):
                            c = cg * GB + q
                            if hi == 0:
                                left, rows = flat(xcc[:, c, :, :]), NH * B
                            else:
                                left, rows = xcc[:, c, 1, :], B
                            mm = pe.matmul(bank[j][q * 32:q * 32 + rows, (cg % 2) * S:(cg % 2 + 1) * S], left,
                                           flat(toep[:, c, (1 - hi) * YH:(3 - hi) * YH, :]), start=(hi == 0), stop=(hi == 1),
                                           tile_position=(0, q * 32))
                mm.then_inc(s_conv, 1)
            for h in range(NH):
                st.fill_wait(pe, K_CONVT + h)
                for cg in range(CG):
                    if cg % 2 == 0:
                        pe.wait_ge(s_convA if cg % 4 == 0 else s_convD, cg // 4 + 1)
                    mm = pe.matmul(st.bank(K_CONVT + h)[:, cg * GB * B:(cg + 1) * GB * B], convr[:, cg, h * P:(h + 1) * P], pick,
                                   start=True, stop=True)
                mm.then_inc(s_task, 1)

            def transposed(t, k, src, g):
                t.fill_wait(pe, k)
                for h in range(NH):
                    mm = pe.transpose(t.bank(k)[:, h * P:(h + 1) * P], flat(src[:, h, g * GB:(g + 1) * GB, :]), ident)
                mm.then_inc(s_task, 1)

            def values(t, k, src, g, w):
                t.fill_wait(pe, k)
                for h in range(NH):
                    mm = pe.matmul(t.bank(k)[:, h * P:(h + 1) * P], src[:, g, h * P:(h + 1) * P], w, start=True, stop=True)
                mm.then_inc(s_task, 1)

            pe.wait_ge(s_ln, NH)
            for g in range(NG):
                transposed(st, K_PRE + g, xh, g)
            pe.wait_ge(s_bd, 1)
            st.drained(pe, K_CUR)
            st.fill_wait(pe, K_CUR)
            for g in range(NG):
                mm = pe.matmul(st.bank(K_CUR)[0:B, 0:S], wsb[:, g, :], xt[:, g, :], start=(g == 0), stop=(g == NG - 1))
            mm.then_inc(s_task, 1)
            pe.wait_ge(s_wl2, 16)
            product_pe(pe, st, K_CUR + 1, wvl, rep(wor, NG), P)
            product_pe(pe, st, K_CUR + 2, bvc.broadcast_to([C, P]), wor, C)
            for g in range(NG):
                product_pe(pe, st, K_Q + g, bdq[:, :], xt[:, g, :], S)
            for g in range(NG):
                product_pe(pe, st, K_Q + NG + g, bdk[:, :], xt[:, g, :], S)
            pe.wait_ge(s_bdv, 1)
            for g in range(NG):
                values(st, K_V + g, xt, g, bdv[:, :])
            st.drained(pe, K_V)
            pe.wait_ge(s_vb, NG * NH)
            attention_pe(pe, 0, st, K_ATT, kt, True)
            wait(pe, s_da, 0, count("A", STATIC[:K_YTOK]))
            for h in range(NH):
                st.fill_wait(pe, K_YTOK + h)
                for g in range(NG):
                    mm = pe.transpose(st.bank(K_YTOK + h)[:, g * P:(g + 1) * P], yT[:, g, h * P:(h + 1) * P], ident)
                mm.then_inc(s_task, 1)
            pe.wait_ge(s_t2, 1)
            for g in range(NG):
                transposed(st, K_H0 + g, tok, g)
            pe.wait_ge(s_ln, 2 * NH)
            for g in range(NG):
                transposed(st, K_H0 + NG + g, xh, g)

            reg_att, reg_task, reg_da, reg_dd = (pe.alloc_register(n) for n in ("pe_att", "pe_task", "pe_da", "pe_dd"))
            pe.reg_mov(reg_att, B)
            reg_wp = pe.alloc_register("pe_weight_products")
            pe.reg_mov(reg_wp, 0)
            pe.reg_mov(reg_task, len(STATIC))
            pe.reg_mov(reg_da, count("A", STATIC))
            pe.reg_mov(reg_dd, count("D", STATIC))
            reg_code, reg_op, reg_step, reg_kind, reg_r = (
                pe.alloc_register("pe_" + n) for n in ("code", "op", "step", "kind", "round"))
            pe.reg_mov(reg_r, 1)
            pe.wait_ge(s_tabmove, 32)
            pe.wait_ge(s_op, 1)
            pe.reg_load(reg_op, opi[0:1, 0:1])
            op = pe.snap(reg_op, min_val=0, max_val=NOPS - 1)
            pe.reg_load(reg_code, tab[0:1, bass.ds(op * (NSTEPS + 1) + NSTEPS, 1)])
            with pe.While(lambda: pe.snap(reg_code) < NONE):
                pe.reg_alu(reg_step, reg_code, 2, ALU.logical_shift_right)
                pe.reg_alu(reg_kind, reg_code, 3, ALU.bitwise_and)
                b = pe.snap(reg_step, min_val=0, max_val=NSTEPS - 1)
                kind = pe.snap(reg_kind)
                r = pe.snap(reg_r)
                with pe.If(kind >= 2):
                    att = pe.snap(reg_att)
                    t = Tasks(LATT, pe.snap(reg_task), pe.snap(reg_da), pe.snap(reg_dd))
                    wp = pe.snap(reg_wp)
                    pe.wait_ge(s_wA, r * 16)
                    for i in range(2):
                        pe.matmul(bank[2 + i][:, 0:P], wa[:, i * GB * C:(i + 1) * GB * C],
                                  rep(wa[:, (2 * GB + i) * C:(2 * GB + i + 1) * C], NG), start=True, stop=True).then_inc(s_wp, 1)
                    wait(pe, s_bd2, wp, 2)
                    for g in range(NG):
                        product_pe(pe, t, g, bda[:, :], hT[:, g, :], S)
                    for g in range(NG):
                        values(t, NG + g, hT, g, bdv[:, :])
                    t.drained(pe, len(LPRE))
                    attention_pe(pe, att, t, len(LPRE), hT, False)
                    pe.reg_alu(reg_wp, reg_wp, 2, ALU.add)
                    pe.reg_alu(reg_att, reg_att, B, ALU.add)
                    pe.reg_alu(reg_task, reg_task, len(LATT), ALU.add)
                    pe.reg_alu(reg_da, reg_da, count("A", LATT), ALU.add)
                    pe.reg_alu(reg_dd, reg_dd, count("D", LATT), ALU.add)
                with pe.If(kind == 2):
                    da, dd = pe.snap(reg_da), pe.snap(reg_dd)
                    pe.wait_ge(s_da, da)
                    pe.wait_ge(s_dd, dd)
                    pe.matmul(bank[0][0:1, 0:C], hT[:, 0, 0:1], ident[:, 0:C], start=True, stop=True).then_inc(s_row, 1)
                with pe.If(kind != 2):
                    t = Tasks(FF, pe.snap(reg_task), pe.snap(reg_da), pe.snap(reg_dd))
                    pe.wait_ge(s_w1z, r)
                    for k, (what, n) in enumerate(HORDER):
                        if what == "H":
                            gp, q = divmod(n, GB)
                            product_pe(pe, t, k, w1z[:, q, :], flat(hT[:, 2 * gp:2 * gp + 2, :]), 2 * S)
                            if k == 1:
                                wait(pe, s_da, t.a, 1)
                                pe.matmul(bank[0][0:1, 0:C], relu[:, 0, 0, 0:1], w2s, start=True, stop=False)
                                pe.matmul(bank[0][0:1, 0:C], b2s, ident[:, 0:C], start=False, stop=True).then_inc(s_row, 1)
                        else:
                            hid = [i for i, (w, m) in enumerate(HORDER) if w == "H" and m // GB <= n // 2]
                            t.fill_wait(pe, k)
                            t.drained(pe, max(i for i in hid if HORDER[i][1] // GB == n // 2) + 1)
                            for q in range(GB):
                                mm = pe.matmul(t.bank(k)[q * C:(q + 1) * C, 0:S], w2s, relu[:, q, n, :],
                                               start=True, stop=True, tile_position=(0, q * C))
                            mm.then_inc(s_task, 1)
                    pe.reg_alu(reg_task, reg_task, len(FF), ALU.add)
                    pe.reg_alu(reg_da, reg_da, count("A", FF), ALU.add)
                    pe.reg_alu(reg_dd, reg_dd, count("D", FF), ALU.add)
                r = pe.snap(reg_r) + 1
                pe.wait_ge(s_op, r)
                pe.reg_alu(reg_r, reg_r, 1, ALU.add)
                pe.reg_load(reg_op, opi[0:1, 0:1])
                op = pe.snap(reg_op, min_val=0, max_val=NOPS - 1)
                pe.reg_load(reg_code, tab[0:1, bass.ds(op * (NSTEPS + 1) + (NSTEPS - 1) - b, 1)])

        def attention_act(act, base, t, k0, dst):
            def drain(g):
                t.filled(act, k0 + g)
                nc.scalar.activation(dst[:, g, :], t.bank(k0 + g)[:, 0:S], ACT.Copy).then_inc(s_da, 1)

            for b in range(B):
                wait(act, s_nm, base, b + 1)
                if b >= NPB:
                    wait(act, s_T, base, b - NPB + 1)
                for ih in range(NH):
                    e = nc.scalar.activation(prob[b % NPB][:, ih, :], bank[SCORES[b % AHEAD]][:, ih * S:(ih + 1) * S], ACT.Exp,
                                             bias=nmax[:, b, ih:ih + 1], accum_out=esum[:, b, ih:ih + 1])
                e.then_inc(s_P, 1)
                if b >= 6 and (b - 6) % GB == 0:
                    drain((b - 6) // GB)
            drain(NG - 1)

        @block.scalar
        def _(act):
            def copy_table(t, i, src):
                n = min(5, HW - 5 * i)
                nc.scalar.activation(gtab[:, t, :, :, 5 * i:5 * i + n].rearrange("p t c x -> p x (t c)"),
                                     src[:, 0:n * 3 * C].rearrange("p (x n) -> p x n", x=n), ACT.Copy).then_inc(s_gcopy[t], 1)

            def ln_act(n):
                for h in range(NH):
                    act.wait_ge(s_lnc, NH * n + h + 1)
                    nc.scalar.activation(sq[:, h, :, :], xc[:, h, :, :], ACT.Square).then_inc(s_lns, 1)
                act.wait_ge(s_lnv, NH * (n + 1))
                nc.scalar.activation(dev[:, :], var[:, :], ACT.Sqrt, bias=eps[:, :], scale=1.0 / C).then_inc(s_lnd, 1)

            act.wait_ge(s_gb, 1)
            for i in range(2):
                copy_table(1, i, bank[4 + i])
            act.wait_ge(s_ga, 1)
            for i in range(2):
                copy_table(0, i, bank[2 + i])
            act.wait_ge(s_xc, NH)
            for i in range(2):
                cs = slice(i * C // 2, (i + 1) * C // 2)
                nc.scalar.activation(flat(sqc[:, cs, :, :]), flat(xcc[:, cs, :, :]), ACT.Square).then_inc(s_sq, 1)
            act.wait_ge(s_vh, 1)
            nc.scalar.activation(vhalf[:, :], bank[2][:, 0:CG], ACT.Copy).then_inc(s_vhs, 1)
            act.wait_ge(s_zero, 3)
            act.wait_ge(s_vp, 1)
            nc.scalar.activation(stdv[:, :], bank[3][:, 0:CG], ACT.Sqrt, bias=eps[:, :]).then_inc(s_std, 1)
            act.wait_ge(s_rstd, 1)
            for j in range(0, CG // 2, 2):
                act.wait_ge(s_conv, j + 1)
                for cg in (2 * j, 2 * j + 1):
                    cp = nc.scalar.activation(convr[:, cg, :], bank[j][:, (cg % 2) * S:(cg % 2 + 1) * S], ACT.Copy,
                                              scale=rstd[:, cg:cg + 1])
                cp.then_inc(s_convA, 1)
            ln_act(0)

            def copy(t, k, dst, src):
                t.filled(act, k)
                nc.scalar.activation(dst, src, ACT.Copy).then_inc(s_da, 1)

            for g in range(0, NG, 2):
                copy(st, K_PRE + g, xt[:, g, :], st.bank(K_PRE + g)[:, 0:S])
            act.wait_ge(s_wl1, 16)
            st.filled(act, K_CUR)
            nc.scalar.activation(cur[:, :], st.bank(K_CUR)[0:B, 0:S], ACT.Identity, bias=bsr[0:B, :]).then_inc(s_da, 1)
            act.wait_ge(s_zero, 6)
            act.wait_ge(s_bd, 1)
            for g in range(NG):
                k = K_Q + g
                st.filled(act, k)
                for q in range(GB):
                    rows = slice(q * C, (q + 1) * C)
                    cp = nc.scalar.activation(qz[rows, g * GB + q, :], st.bank(k)[rows, 0:S], ACT.Identity,
                                              bias=bqs[rows, :], scale=SCALE)
                cp.then_inc(s_da, 1)
            for g in range(NG):
                k = K_Q + NG + g
                st.filled(act, k)
                nc.scalar.activation(kt[:, g, :], st.bank(k)[:, 0:S], ACT.Identity, bias=bkr).then_inc(s_da, 1)

            def copy_values(t, k, g):
                t.filled(act, k)
                nc.scalar.activation(v[:, :, g * GB:(g + 1) * GB, :].rearrange("p h b c -> p h (b c)"),
                                     t.bank(k)[:, 0:S].rearrange("p (h n) -> p h n", h=NH), ACT.Copy).then_inc(s_da, 1)

            for g in range(NG):
                copy_values(st, K_V + g, g)
            attention_act(act, 0, st, K_ATT, yT)
            for g in range(NG):
                if g == 0:
                    st.filled(act, K_H0)
                copy(st, K_H0 + g, outT[:, g, :], st.bank(K_H0 + g)[:, 0:S])
            ln_act(1)
            nc.scalar.activation(table[:, :], eps[0:1, :], ACT.Exp)
            for g in range(0, NG, 2):
                copy(st, K_H0 + NG + g, hT[:, g, :], st.bank(K_H0 + NG + g)[:, 0:S])

            reg_att, reg_task = act.alloc_register("act_att"), act.alloc_register("act_task")
            act.reg_mov(reg_att, B)
            act.reg_mov(reg_task, len(STATIC))
            reg_code, reg_op, reg_step, reg_kind, reg_r = (
                act.alloc_register("act_" + n) for n in ("code", "op", "step", "kind", "round"))
            act.reg_mov(reg_r, 1)
            act.wait_ge(s_tabmove, 32)
            act.wait_ge(s_op, 1)
            act.reg_load(reg_op, opi[0:1, 0:1])
            op = act.snap(reg_op, min_val=0, max_val=NOPS - 1)
            act.reg_load(reg_code, tab[0:1, bass.ds(op * (NSTEPS + 1) + NSTEPS, 1)])
            with act.While(lambda: act.snap(reg_code) < NONE):
                act.reg_alu(reg_step, reg_code, 2, ALU.logical_shift_right)
                act.reg_alu(reg_kind, reg_code, 3, ALU.bitwise_and)
                b = act.snap(reg_step, min_val=0, max_val=NSTEPS - 1)
                kind = act.snap(reg_kind)
                r = act.snap(reg_r)
                with act.If(kind >= 2):
                    att = act.snap(reg_att)
                    t = Tasks(LATT, act.snap(reg_task))
                    for g in range(0, NG, 2):
                        t.filled(act, g)
                        for q in range(GB):
                            rows = slice(q * C, (q + 1) * C)
                            cp = nc.scalar.activation(qz[rows, g * GB + q, :], t.bank(g)[rows, 0:S], ACT.Copy)
                        cp.then_inc(s_da, 1)
                    for g in range(0, NG, 2):
                        copy_values(t, NG + g, g)
                    attention_act(act, att, t, len(LPRE), hT)
                    act.reg_alu(reg_att, reg_att, B, ALU.add)
                    act.reg_alu(reg_task, reg_task, len(LATT), ALU.add)
                with act.If(kind != 2):
                    t = Tasks(FF, act.snap(reg_task))
                    act.wait_ge(s_w1z, r)
                    for k, (what, n) in enumerate(HORDER):
                        if FF[k] == "A":
                            t.filled(act, k)
                            if what == "H":
                                gp, q = divmod(n, GB)
                                nc.scalar.activation(relu[:, q, 2 * gp:2 * gp + 2, :],
                                                     t.bank(k)[:, :].rearrange("p (g s) -> p g s", g=2),
                                                     ACT.Relu, bias=b1s).then_inc(s_da, 1)
                            else:
                                nc.scalar.activation(hT[:, n, :], t.bank(k)[:, 0:S], ACT.Identity, bias=b2s).then_inc(s_da, 1)
                    act.reg_alu(reg_task, reg_task, len(FF), ALU.add)
                r = act.snap(reg_r) + 1
                act.wait_ge(s_op, r)
                act.reg_alu(reg_r, reg_r, 1, ALU.add)
                act.reg_load(reg_op, opi[0:1, 0:1])
                op = act.snap(reg_op, min_val=0, max_val=NOPS - 1)
                act.reg_load(reg_code, tab[0:1, bass.ds(op * (NSTEPS + 1) + (NSTEPS - 1) - b, 1)])

        @block.vector
        def _(dve):
            chain = {"base": 0, "n": 0}

            def link(ins):
                chain["n"] += 1
                ins.then_inc(s_dve, 1)
                dve.wait_ge(s_dve, chain["base"] + chain["n"])

            dve.wait_ge(s_w81, 16)
            link(nc.vector.tensor_copy(w81p[:, 0, :], w81[:, :]))
            link(nc.vector.tensor_tensor(wres[:, 0, :], w81[:, :], w81p[:, 0, :], ALU.subtract))
            link(nc.vector.tensor_copy(w81p[:, 1, :], wres[:, 0, :]))
            link(nc.vector.tensor_tensor(wres[:, 1, :], wres[:, 0, :], w81p[:, 1, :], ALU.subtract))
            nc.vector.tensor_copy(w81p[:, 2, :], wres[:, 1, :]).then_inc(s_w81p, 1)

            def copy_table(t, i, src):
                n = min(5, HW - 5 * i)
                nc.vector.tensor_copy(gtab[:, t, :, :, 5 * i:5 * i + n].rearrange("p t c x -> p x (t c)"),
                                      src[:, 0:n * 3 * C].rearrange("p (x n) -> p x n", x=n)).then_inc(s_gcopy[t], 1)

            dve.wait_ge(s_gb, 1)
            for i in range(2, 4):
                copy_table(1, i, bank[4 + i])
            dve.wait_ge(s_xrev, 16)
            dve.wait_ge(s_mean, 1)
            for h in range(NH):
                nc.vector.tensor_tensor(xcc[:, :, h, :].rearrange("p c b -> p b c"), xrev[:, h, :, :],
                                        bank[1][:, :].rearrange("p (b c) -> p b c", b=B), ALU.subtract).then_inc(s_xc, 1)
            dve.wait_ge(s_ga, 1)
            for i in range(2, 4):
                copy_table(0, i, bank[(2, 3, 0, 1)[i]])
            dve.wait_ge(s_kpe, 16 * YH)
            for e in range(NE):
                st.filled(dve, e)
                nc.vector.tensor_tensor(toep[:, :, e, :], st.bank(e)[:, :].rearrange("p (c x) -> p c x", x=HW),
                                        rep(toepk[:, e, :], C), ALU.add).then_inc(s_dd, 1)
                if e == 20:
                    dve.wait_ge(s_std, 1)
                    nc.vector.reciprocal(rstd[:, :], stdv[:, :]).then_inc(s_rstd, 1)
            dve.wait_ge(s_rstd, 1)
            dve.wait_ge(s_cf, 16)
            dve.wait_ge(s_wl1, 16)
            blk3 = blk.rearrange("p (g c) -> p g c", g=NG)
            nc.vector.tensor_tensor(bdq[:, :].rearrange("p (g c) -> p g c", g=NG), rep(wqr, NG), blk3, ALU.mult)
            nc.vector.tensor_tensor(bdk[:, :].rearrange("p (g c) -> p g c", g=NG), rep(wkr, NG), blk3, ALU.mult)
            nc.vector.tensor_scalar(bqs[:, :], bqr, SCALE, None, ALU.mult)
            nc.vector.tensor_scalar(flat(wsb[:, :, :]), colsel, wsr, None, ALU.mult).then_inc(s_bd, 1)
            dve.wait_ge(s_tabl, 16)
            nc.vector.memset(tabf[:, 0:1], float(NONE))
            link(nc.vector.tensor_copy(maskf[:, :, :], masks8[:, :, :]))
            nc.vector.tensor_tensor(anyf[:, :], maskf[:, 0, :], maskf[:, 1, :], ALU.max)
            link(nc.vector.scalar_tensor_tensor(code[:, :], maskf[:, 0, :], 2.0, maskf[:, 1, :], ALU.mult, ALU.add))
            link(nc.vector.tensor_tensor(code[:, :], code[:, :], stepcode, ALU.add))
            link(nc.vector.tensor_tensor(code[:, :], code[:, :], anyf[:, :], ALU.mult))
            link(nc.vector.tensor_scalar(codem[:, :], code[:, :], float(NONE), None, ALU.add))
            link(nc.vector.tensor_tensor_scan(tabf[:, 1:NSTEPS + 1], codem[:, :], codem[:, :], float(NONE), ALU.min, ALU.min))
            nc.vector.tensor_copy(tabi[:, :], tabf[:, :]).then_inc(s_tabi, 1)
            for j in range(1, CG // 2, 2):
                dve.wait_ge(s_conv, j + 1)
                for cg in (2 * j, 2 * j + 1):
                    cp = nc.vector.tensor_scalar(convr[:, cg, :], bank[j][:, (cg % 2) * S:(cg % 2 + 1) * S],
                                                 rstd[:, cg:cg + 1], None, ALU.mult)
                cp.then_inc(s_convD, 1)

            def argmax_op(values):
                link(nc.vector.tensor_reduce(top[:, :], values, AX.X, ALU.max))
                link(nc.vector.scalar_tensor_tensor(hit[:, :], values, top[:, :], rank, ALU.is_ge, ALU.mult))
                link(nc.vector.tensor_reduce(top[:, :], hit[:, :], AX.X, ALU.max))
                nc.vector.tensor_scalar(opi[:, :], top[:, :], -1.0, float(NOPS), ALU.mult, ALU.add).then_inc(s_op, 1)

            def pick_op(r):
                dve.wait_ge(s_row, r)
                dve.wait_ge(s_seen, r)
                link(nc.vector.tensor_copy(row[:, :], bank[0][0:1, 0:C]))
                argmax_op(row[:, 0:NOPS])

            def layernorm(n, residual):
                for h in range(NH):
                    hb = slice(h * B, (h + 1) * B)
                    residual(h)
                    link(nc.vector.tensor_reduce(mu[:, hb], tok[:, h, :, :], AX.X, ALU.add))
                    link(nc.vector.tensor_scalar(mu[:, hb], mu[:, hb], -1.0 / C, None, ALU.mult))
                    nc.vector.tensor_tensor(xc[:, h, :, :], tok[:, h, :, :], mu[:, hb].unsqueeze(2).broadcast_to([P, B, C]),
                                            ALU.add).then_inc(s_lnc, 1)
                if n == 1:
                    dve.wait_ge(s_lnc, NH * (n + 1))
                    argmax_op(xc[0:1, 0, 0, 0:NOPS])
                for h in range(NH):
                    dve.wait_ge(s_lns, NH * n + h + 1)
                    nc.vector.tensor_reduce(var[:, h * B:(h + 1) * B], sq[:, h, :, :], AX.X, ALU.add).then_inc(s_lnv, 1)
                dve.wait_ge(s_lnd, n + 1)
                link(nc.vector.reciprocal(inv[:, :], dev[:, :]))
                for h in range(NH):
                    nc.vector.tensor_tensor(xh[:, h, :, :], xc[:, h, :, :],
                                            inv[:, h * B:(h + 1) * B].unsqueeze(2).broadcast_to([P, B, C]), ALU.mult).then_inc(s_ln, 1)

            dve.wait_ge(s_xin, 16)

            def conv_residual(h):
                st.filled(dve, K_CONVT + h)
                nc.vector.tensor_tensor(tok[:, h, :, :], xin[:, h, :, :],
                                        st.bank(K_CONVT + h)[:, :].rearrange("p (c b) -> p b c", b=B), ALU.add).then_inc(s_dd, 1)
                wait(dve, s_dd, 0, count("D", STATIC[:K_CONVT + h + 1]))

            layernorm(0, conv_residual)

            def drain_half(t, k, dst):
                for g in range(1, NG, 2):
                    t.filled(dve, k + g)
                    nc.vector.tensor_copy(dst[:, g, :], t.bank(k + g)[:, 0:S]).then_inc(s_dd, 1)

            def block_diagonal(dst, src, scale):
                return nc.vector.scalar_tensor_tensor(dst[:, :], src, scale, blk, ALU.mult, ALU.mult)

            drain_half(st, K_PRE, xt)
            nc.vector.memset(dec[1][:, :], DECAY)
            link(nc.vector.memset(dec[0][:, :], DECAY))
            st.filled(dve, K_CUR + 1)
            nc.vector.tensor_tensor(bdv[:, :], st.bank(K_CUR + 1)[:, 0:P], blk, ALU.mult).then_inc(s_bdv, 1)
            dve.wait_ge(s_bdv, 1)
            nc.vector.memset(spm[:, 0:1], 0.0).then_inc(s_dd, 1)
            st.filled(dve, K_CUR + 2)
            nc.vector.tensor_copy(bvo[:, :], st.bank(K_CUR + 2)[:, 0:C]).then_inc(s_bvo, 1)
            dve.wait_ge(s_bvo, 1)
            nc.vector.memset(spm[:, 0:1], 0.0).then_inc(s_dd, 1)
            wait(dve, s_da, 0, count("A", STATIC[:K_CUR + 1]))
            dve.wait_ge(s_zero, 4)

            def sweeps():
                for i in range(LIF_ITERS):
                    link(nc.vector.tensor_tensor_scan(mem[:, :], dec[i % 2][:, 0:S], cur[:, :], 0.0, ALU.mult, ALU.add))
                    link(nc.vector.tensor_scalar(dec[1 - i % 2][:, 1:S + 1], mem[:, :], 1.0, DECAY, ALU.is_lt, ALU.mult))
                link(nc.vector.tensor_tensor(diff[:, :], dec[0][:, 0:S], dec[1][:, 0:S], ALU.not_equal))
                link(nc.vector.tensor_reduce(dsum[0:B, 0:1], diff[:, :], AX.X, ALU.max))
                link(nc.vector.transpose(dsumT[:, :], dsum[:, :]))
                link(nc.vector.tensor_reduce(dmax[:, :], dsumT[0:1, :], AX.X, ALU.max))
                link(nc.vector.tensor_copy(unsettled[:, :], dmax[:, :]))

            sweeps()
            reg_u, reg_c = dve.alloc_register("dve_unsettled"), dve.alloc_register("dve_chain")
            dve.reg_mov(reg_c, chain["n"])
            dve.reg_load(reg_u, unsettled[0:1, 0:1])
            with dve.If(dve.snap(reg_u) != 0):
                with dve.Fori(0, LIF_BLOCKS) as _i:
                    with dve.If(dve.snap(reg_u) != 0):
                        chain["base"], chain["n"] = dve.snap(reg_c), 0
                        sweeps()
                        dve.reg_alu(reg_c, reg_c, chain["n"], ALU.add)
                        dve.reg_load(reg_u, unsettled[0:1, 0:1])
            chain["base"], chain["n"] = dve.snap(reg_c), 0
            nc.vector.tensor_scalar(spk[:, :], mem[:, :], 1.0, None, ALU.is_ge).then_inc(s_spk, 1)
            nc.vector.tensor_tensor(tokb[:, :, :, :].rearrange("p h b c -> p (h b) c"),
                                    tok[:, :, :, :].rearrange("p h b c -> p (h b) c"), rep(bor, NH * B), ALU.add)
            st.filled(dve, K_CNT)
            link(nc.vector.tensor_scalar(spm[:, :], st.bank(K_CNT)[:, 0:S], 0.5, NEG, ALU.is_lt, ALU.mult))
            dve.wait_ge(s_mask, 16)
            nc.vector.tensor_tensor(negm[:, :, :], maskc[:, :, :], rep(spm[:, :], NH), ALU.add).then_inc(s_negm, 1)
            nc.vector.memset(mu[:, 0:1], 0.0).then_inc(s_dd, 1)

            def attention_dve(base, masked):
                def row_max(b):
                    wait(dve, s_S, base, b + 1)
                    m = nc.vector.tensor_reduce(nmax[:, b, :], bank[SCORES[b % AHEAD]][:, :].rearrange("p (h j) -> p h j", h=NH), AX.X,
                                                ALU.max, negate=True)
                    if masked:
                        link(m)
                        m = nc.vector.tensor_scalar(nmax[:, b, :], nmax[:, b, :], -FLOOR, None, ALU.min)
                    m.then_inc(s_nm, 1)

                def invert(b):
                    wait(dve, s_P, base, b + 1)
                    if masked:
                        link(nc.vector.tensor_scalar(esum[:, b, :], esum[:, b, :], 1e-30, None, ALU.max))
                    nc.vector.reciprocal(einv[:, b, :], esum[:, b, :]).then_inc(s_ri, 1)

                def copy_probT(b):
                    wait(dve, s_T, base, b + 1)
                    nc.vector.tensor_copy(flat(probT[b % NTB]), bank[2 + b % 2][:, :]).then_inc(s_PT, 1)

                for b in range(AHEAD):
                    row_max(b)
                invert(0)
                for b in range(B):
                    if b + 1 < B:
                        invert(b + 1)
                    if b + AHEAD < B:
                        row_max(b + AHEAD)
                    copy_probT(b)

            attention_dve(0, True)

            def attention_residual(h):
                st.filled(dve, K_YTOK + h)
                nc.vector.tensor_tensor(flat(tok[:, h, :, :]), flat(tokb[:, h, :, :]), st.bank(K_YTOK + h)[:, :],
                                        ALU.add).then_inc(s_dd, 1)
                wait(dve, s_dd, 0, count("D", STATIC[:K_YTOK + h + 1]))
                if h == NH - 1:
                    dve.sem_inc(s_t2, 1)

            layernorm(1, attention_residual)
            drain_half(st, K_H0 + NG, hT)
            reg_att, reg_task, reg_da, reg_dd = (dve.alloc_register(n) for n in ("dve_att", "dve_task", "dve_da", "dve_dd"))
            dve.reg_alu(reg_c, reg_c, chain["n"], ALU.add)
            dve.reg_mov(reg_att, B)
            reg_wp, reg_ff = dve.alloc_register("dve_weight_products"), dve.alloc_register("dve_ffn_drained")
            dve.reg_mov(reg_wp, 0)
            dve.reg_mov(reg_ff, count("A", STATIC))
            dve.reg_mov(reg_task, len(STATIC))
            dve.reg_mov(reg_da, count("A", STATIC))
            dve.reg_mov(reg_dd, count("D", STATIC))
            reg_code, reg_op, reg_step, reg_kind, reg_r = (
                dve.alloc_register("dve_" + n) for n in ("code", "op", "step", "kind", "round"))
            dve.reg_mov(reg_r, 1)
            dve.wait_ge(s_tabmove, 32)
            dve.wait_ge(s_op, 1)
            dve.reg_load(reg_op, opi[0:1, 0:1])
            op = dve.snap(reg_op, min_val=0, max_val=NOPS - 1)
            dve.reg_load(reg_code, tab[0:1, bass.ds(op * (NSTEPS + 1) + NSTEPS, 1)])
            with dve.While(lambda: dve.snap(reg_code) < NONE):
                dve.reg_alu(reg_step, reg_code, 2, ALU.logical_shift_right)
                dve.reg_alu(reg_kind, reg_code, 3, ALU.bitwise_and)
                b = dve.snap(reg_step, min_val=0, max_val=NSTEPS - 1)
                kind = dve.snap(reg_kind)
                r = dve.snap(reg_r)
                with dve.If(kind >= 2):
                    att = dve.snap(reg_att)
                    chain["base"], chain["n"] = dve.snap(reg_c), 0
                    t = Tasks(LATT, dve.snap(reg_task))
                    wp = dve.snap(reg_wp)
                    for i, (diagonal, scale) in enumerate(((bda, SCALE), (bdv, 1.0))):
                        dve.wait_ge(s_wp, wp + (i + 1))
                        block_diagonal(diagonal, bank[2 + i][:, 0:P], scale).then_inc(s_bd2, 1)
                    for g in range(1, NG, 2):
                        t.filled(dve, g)
                        for q in range(GB):
                            rows = slice(q * C, (q + 1) * C)
                            cp = nc.vector.tensor_copy(qz[rows, g * GB + q, :], t.bank(g)[rows, 0:S])
                        cp.then_inc(s_dd, 1)
                    for g in range(1, NG, 2):
                        k = NG + g
                        t.filled(dve, k)
                        nc.vector.tensor_copy(v[:, :, g * GB:(g + 1) * GB, :].rearrange("p h b c -> p h (b c)"),
                                              t.bank(k)[:, 0:S].rearrange("p (h n) -> p h n", h=NH)).then_inc(s_dd, 1)
                    attention_dve(att, False)
                    dve.reg_alu(reg_c, reg_c, chain["n"], ALU.add)
                    dve.reg_alu(reg_wp, reg_wp, 2, ALU.add)
                    dve.reg_alu(reg_att, reg_att, B, ALU.add)
                    dve.reg_alu(reg_task, reg_task, len(LATT), ALU.add)
                    dve.reg_alu(reg_da, reg_da, count("A", LATT), ALU.add)
                    dve.reg_alu(reg_dd, reg_dd, count("D", LATT), ALU.add)
                ff = dve.snap(reg_ff)
                dve.wait_ge(s_da, ff)
                dve.wait_ge(s_wF, r * W_FFN)
                for q in range(GB):
                    rows = slice(q * C, (q + 1) * C)
                    nc.vector.tensor_copy(w1z[rows, q, :], w1r[rows, :])
                nc.vector.tensor_copy(wfs[:, :], wf[:, :]).then_inc(s_w1z, 1)
                chain["base"], chain["n"] = dve.snap(reg_c), 0
                with dve.If(kind == 2):
                    pick_op(r)
                with dve.If(kind != 2):
                    t = Tasks(FF, dve.snap(reg_task), dve.snap(reg_da), dve.snap(reg_dd))
                    dve.wait_ge(s_w1z, r)
                    picked = False
                    for k, (what, n) in enumerate(HORDER):
                        if FF[k] == "D":
                            if k > 1 and not picked:
                                chain["n"] = 0
                                pick_op(r)
                                picked = True
                            t.filled(dve, k)
                            if what == "H":
                                gp, q = divmod(n, GB)
                                nc.vector.tensor_scalar(relu[:, q, 2 * gp:2 * gp + 2, :],
                                                        t.bank(k)[:, :].rearrange("p (g s) -> p g s", g=2), b1s, 0.0,
                                                        ALU.add, ALU.max).then_inc(s_dd, 1)
                            else:
                                nc.vector.tensor_scalar(hT[:, n, :], t.bank(k)[:, 0:S], b2s, None, ALU.add).then_inc(s_dd, 1)
                    dve.reg_alu(reg_task, reg_task, len(FF), ALU.add)
                    dve.reg_alu(reg_da, reg_da, count("A", FF), ALU.add)
                    dve.reg_alu(reg_dd, reg_dd, count("D", FF), ALU.add)
                    dve.reg_alu(reg_ff, reg_da, 0, ALU.add)
                dve.reg_alu(reg_c, reg_c, chain["n"], ALU.add)
                r = dve.snap(reg_r) + 1
                dve.wait_ge(s_op, r)
                dve.reg_alu(reg_r, reg_r, 1, ALU.add)
                dve.reg_load(reg_op, opi[0:1, 0:1])
                op = dve.snap(reg_op, min_val=0, max_val=NOPS - 1)
                dve.reg_load(reg_code, tab[0:1, bass.ds(op * (NSTEPS + 1) + (NSTEPS - 1) - b, 1)])
            da, dd = dve.snap(reg_da), dve.snap(reg_dd)
            dve.wait_ge(s_da, da)
            dve.wait_ge(s_dd, dd)
            for i in range(2):
                gs = slice(2 * i, 2 * i + 2)
                nc.vector.tensor_tensor(outT[:, gs, :], outT[:, gs, :], hT[:, gs, :], ALU.add).then_inc(s_fin, 1)


def kernel(**inputs):
    import numpy as _np
    import concourse.bacc as _bacc
    from concourse import mybir as _mybir
    from concourse.bass_utils import run_bass_kernel_spmd as _run

    g = {k: _np.asarray(a) for k, a in inputs.items()}
    steps = NSTEPS * NOPS

    def swapped(a):
        return _np.swapaxes(a, -1, -2)

    def tok(a):
        return a.reshape(B, C, S).transpose(2, 0, 1).reshape(S, B * C)

    def down(a):
        return _np.tile(a.reshape(1, -1), (P, 1))

    def reps(a):
        return _np.tile(a.reshape(C, -1), (GB, 1))

    wc = g["L0_conv_weight_comp"].reshape(C, NP13, NP13)[:, Q0:Q0 + NQ, Q0:Q0 + NQ]
    at = {n: g["L1_attn_" + n] for n in ("Wq", "Wk", "Wv", "Wo", "Ws", "bq", "bk", "bv", "bo", "bs")}
    ff = {n: g["L1_ffn_" + n].reshape((steps,) + g["L1_ffn_" + n].shape[2:])
          for n in ("wq", "wk", "wv", "wo", "ffn_w1", "ffn_b1", "ffn_w2", "ffn_b2")}
    arrays = {
        "xtok": tok(g["x"]), "xrev": tok(g["x"][:, :, :, ::-1]),
        "w81": wc.reshape(C, NQ * NQ).T,
        "kpef": g["L0_conv_kpe"][0, 0, ::-1, ::-1],
        "wl1": _np.concatenate([reps(at["Wq"]), reps(at["Wk"]), down(at["bo"]), reps(at["Ws"]), reps(at["bq"]),
                                reps(at["bk"]), down(at["bs"])], axis=1),
        "wl2": _np.concatenate([_np.tile(at["Wv"].T, (1, GB)), at["Wo"], at["bv"].reshape(C, 1)], axis=1),
        "wa": _np.concatenate([_np.tile(swapped(ff["wq"]), (1, 1, GB)), _np.tile(swapped(ff["wv"]), (1, 1, GB)),
                               swapped(ff["wk"]), ff["wo"]], axis=2),
        "w1": ff["ffn_w1"],
        "wf": _np.concatenate([ff["ffn_w2"], ff["ffn_b1"][:, :, None], _np.tile(ff["ffn_b2"], (1, GB))[:, :, None]], axis=2),
        "masks": _np.stack([g["L1_ffn_attn_mask"].T[:, ::-1], g["L1_ffn_ffn_mask"].T[:, ::-1]], axis=1),
    }
    arrays.update(constants())
    nc = _bacc.Bacc("TRN2", target_bir_lowering=False, num_devices=1)
    d = {}
    for name, a in arrays.items():
        a = arrays[name] = _np.ascontiguousarray(a)
        d[name] = nc.dram_tensor(name + "_dram", a.shape, _mybir.dt.from_np(a.dtype), kind="ExternalInput").ap()
    d["out"] = nc.dram_tensor("out_dram", (B * C, S), _mybir.dt.float32, kind="ExternalOutput").ap()
    build(nc, d)
    r = _run(nc, [{name + "_dram": a for name, a in arrays.items()}], core_ids=[0])
    return r.results[0]["out_dram"].reshape(B, C, HW, HW)
```

```python
import numpy as np
import concourse.bass as bass
from concourse import mybir
from contextlib import ExitStack

F32 = mybir.dt.float32
BF16 = mybir.dt.bfloat16
I32 = mybir.dt.int32
U32 = mybir.dt.uint32
U8 = mybir.dt.uint8
U16 = mybir.dt.uint16
ALU = mybir.AluOpType
ACT = mybir.ActivationFunctionType
AX = mybir.AxisListType

P = 128
B, C, HW = 16, 32, 16
S = HW * HW
NH = S // P
NG = B * C // P
GB = B // NG
KS = 51
R = KS // 2
YH = P // HW
NE = 3 * YH
NQ = 9
Q0 = 2
NP13 = 13
NOPS, NSTEPS, HID = 19, 33, 128
SCALE = float(np.float32(1.0 / np.sqrt(C)))
DECAY = float(np.exp(np.float32(-0.1)))
NEG = -1e30
FLOOR = -1e29
NONE = 4 * NSTEPS
CG = C // GB
LIF_ITERS = 12
LIF_BLOCKS = -(-S // LIF_ITERS)


def group_of(o):
    a = abs(o)
    q = 0
    for n, c in enumerate([0, 1, 2, 4, 8]):
        if c <= a:
            q = n
    return 4 + (q if o >= 0 else -q)


def bf16_bits(a):
    return (np.asarray(a) * 0x3F80).astype(np.uint16)


def constants():
    ident = np.eye(P, dtype=np.float32)
    blk = np.zeros((P, NG, C), np.float32)
    for q in range(GB):
        blk[q * C:(q + 1) * C, q, :] = 1
    col = np.zeros((P, NG, B), np.float32)
    for g in range(NG):
        for q in range(GB):
            col[q * C:(q + 1) * C, g, g * GB + q] = 1
    rows = np.arange(P)
    same = (rows[:, None] // 32 == rows[None, :] // 32) & (rows[:, None] % B == rows[None, :] % B)
    pick = np.zeros((P, GB, B), np.float32)
    for q in range(GB):
        for b in range(B):
            pick[q * 32 + b, q, b] = 1
    stepcode = np.zeros((P, NSTEPS), np.float32)
    stepcode[:NOPS] = 4.0 * np.arange(NSTEPS - 1, -1, -1) - NONE
    rank = np.tile(NOPS - np.arange(NOPS, dtype=np.float32), (P, 1))
    c = {"constf": np.concatenate([ident, blk.reshape(P, -1), col.reshape(P, -1), same.astype(np.float32),
                                   pick.reshape(P, -1), stepcode, rank], axis=1)}
    i = np.arange(S)[:, None]
    j = np.arange(S)[None, :]
    ok = ((j <= i) & (j >= i - 32)) | (j % 16 == 0) | (j < 4)
    m = np.where(ok, 0.0, NEG).astype(np.float32).reshape(NH, P, S).transpose(1, 0, 2)
    c["maskc"] = np.ascontiguousarray(m).reshape(P, NH * S)
    sel = np.zeros((P, 2 * HW - 1, HW))
    for a in range(2 * HW - 1):
        for x in range(HW):
            sel[x * 8 + group_of(a - 15) % 8, a, HW - 1 - x] = 1
    cs = np.zeros((P, 2, 2 * HW - 1, 8))
    for i_ in range(NQ):
        for j_ in range(NQ):
            for t in range(2):
                for s in range(8):
                    if (8 if (t == 1 and s == 0) else s) == i_:
                        for b in range(2 * HW - 1):
                            if group_of(b - 15) == j_:
                                cs[i_ * NQ + j_, t, b, s] = 1
    c["constb"] = bf16_bits(np.concatenate([np.eye(P), cs.reshape(P, -1), sel.reshape(P, -1)], axis=1))
    return c


def build(nc, d):
    with ExitStack() as ctx:
        def sb(name, shape, dt=F32):
            return ctx.enter_context(nc.sbuf_tensor(name, shape, dt))

        def sem(name):
            return ctx.enter_context(nc.semaphore(name))

        NB = 2 * HW - 1
        constf = sb("constf", [P, P + NG * C + NG * B + P + GB * B + NSTEPS + NOPS])
        constb = sb("constb", [P, P + 2 * NB * 8 + NB * HW], U16)
        at = [0]

        def part(t, n):
            a = t[:, at[0]:at[0] + n]
            at[0] += n
            return a
        ident = part(constf, P)
        blk = part(constf, NG * C)
        colsel = part(constf, NG * B)
        pairs = part(constf, P)
        pick = part(constf, GB * B)
        stepcode = part(constf, NSTEPS)[0:NOPS, :]
        rank = part(constf, NOPS)[0:1, :]
        at[0] = 0
        identb = part(constb, P).bitcast(BF16)
        colexp = part(constb, 2 * NB * 8)[0:NQ * NQ, :].bitcast(BF16)
        rowsel = part(constb, NB * HW).bitcast(BF16)
        ones256 = sb("ones256", [P, P])
        onesb = sb("onesb", [B, P], BF16)
        maskc = sb("maskc", [P, NH, S])
        eps = sb("eps", [P, 1])
        xin = sb("xin", [P, NH, B, C])
        xrev = sb("xrev", [P, NH, B, C])
        xcc = sb("xcc", [P, C, NH, B])
        sqc = sb("sqc", [P, C, NH, B])
        w81 = sb("w81", [NQ * NQ, C])
        wres = sb("wres", [NQ * NQ, 2, C])
        w81p = sb("w81p", [NQ * NQ, 3, C], BF16)
        gtab = sb("gtab", [P, 2, 3, C, HW], BF16)
        big = sb("big", [P, C * NE * HW])
        toep = big[:, :].rearrange("p (c e x) -> p c e x", c=C, e=NE)
        toepk = sb("toepk", [P, NE, HW])
        convr = sb("convr", [P, CG, S])
        vhalf = sb("vhalf", [P, CG])
        stdv = sb("stdv", [P, CG])
        rstd = sb("rstd", [P, CG])
        tok = sb("tok", [P, NH, B, C])
        tokb = sb("tokb", [P, NH, B, C])
        xh = sb("xh", [P, NH, B, C])
        xc = sb("xc", [P, NH, B, C])
        sq = sb("sq", [P, NH, B, C])
        mu = sb("mu", [P, NH * B])
        var = sb("var", [P, NH * B])
        dev = sb("dev", [P, NH * B])
        inv = sb("inv", [P, NH * B])
        table = sb("table", [1, 1])
        seen = sb("seen", [1, 1])
        xt = sb("xt", [P, NG, S])
        kt = sb("kt", [P, NG, S])
        yT = sb("yT", [P, NG, S])
        hT = sb("hT", [P, NG, S])
        outT = sb("outT", [P, NG, S])
        qz = sb("qz", [P, B, S])
        v = sb("v", [P, NH, B, C])
        NPB, NTB = 3, 2 * GB
        prob = [sb(f"prob{i}", [P, NH, S]) for i in range(NPB)]
        relu = big[:, 0:GB * NG * S].rearrange("p (q g s) -> p q g s", q=GB, g=NG)
        probT = [big[:, (GB * NG + NH * i) * S:(GB * NG + NH * (i + 1)) * S].rearrange("p (h s) -> p h s", h=NH)
                 for i in range(NTB)]
        nmax = sb("nmax", [P, B, NH])
        esum = sb("esum", [P, B, NH])
        einv = sb("einv", [P, B, NH])
        negm = sb("negm", [P, NH, S])
        minus = [sb(f"minus{i}", [P, NH, S]) for i in range(3)]
        wl1 = sb("wl1", [P, 3 * C + 4])
        wqr, wkr, bor = wl1[:, 0:C], wl1[:, C:2 * C], wl1[:, 2 * C:3 * C]
        wsr, bqr, bkr, bsr = (wl1[:, 3 * C + i:3 * C + i + 1] for i in range(4))
        wl2 = sb("wl2", [C, GB * C + C + 1])
        wvl, wor, bvc = wl2[:, 0:GB * C], wl2[:, GB * C:GB * C + C], wl2[:, GB * C + C:GB * C + C + 1]
        bqs = sb("bqs", [P, 1])
        bdq = sb("bdq", [P, NG * C])
        bdk = sb("bdk", [P, NG * C])
        bdv = sb("bdv", [P, NG * C])
        bda = sb("bda", [P, NG * C])
        wsb = sb("wsb", [P, NG, B])
        wvo = sb("wvo", [P, P])
        bvo = sb("bvo", [P, C])
        cur = sb("cur", [B, S])
        mem = sb("mem", [B, S])
        dec = [sb(f"dec{i}", [B, S + 1]) for i in range(2)]
        diff = sb("diff", [B, S])
        dsum = sb("dsum", [C, C])
        dsumT = sb("dsumT", [C, C])
        dmax = sb("dmax", [1, 1])
        unsettled = sb("unsettled", [1, 1], I32)
        spk = sb("spk", [B, S], BF16)
        spm = sb("spm", [P, S])
        masks8 = sb("masks8", [NOPS, 2, NSTEPS], U8)
        maskf = sb("maskf", [NOPS, 2, NSTEPS])
        anyf = sb("anyf", [NOPS, NSTEPS])
        code = sb("code", [NOPS, NSTEPS])
        codem = sb("codem", [NOPS, NSTEPS])
        tabf = sb("tabf", [NOPS, NSTEPS + 1])
        tabi = sb("tabi", [NOPS, NSTEPS + 1], I32)
        tab = sb("tab", [1, NOPS * (NSTEPS + 1)], I32)
        row = sb("row", [1, C])
        top = sb("top", [1, 1])
        hit = sb("hit", [1, NOPS])
        opi = sb("opi", [1, 1], I32)
        NWA = 2 * GB * C + 2 * C
        wa = sb("wa", [C, NWA + HID])
        wf = sb("wf", [HID, C + 2])
        w1z = sb("w1z", [P, GB, HID])
        wfs = sb("wfs", [HID, C + 2])
        w2s, b1s, b2s = wfs[:, 0:C], wfs[:, C:C + 1], wfs[:, C + 1:C + 2]

        tabd = nc.dram_tensor("step_table", [NOPS, NSTEPS + 1], I32)
        bank = [ctx.enter_context(nc.psum_tensor(f"bank{i}", [P, 512], F32)) for i in range(8)]

        s_xrev, s_xin, s_cb, s_cf, s_mask, s_w81, s_kpe, s_wl1, s_wl2, s_tabl = (sem(n) for n in (
            "reversed_x_loaded", "x_loaded", "constb_loaded", "constf_loaded", "mask_loaded", "w81_loaded", "kpe_loaded",
            "attn_weights_loaded", "attn_value_weights_loaded", "step_masks_loaded"))
        s_tabi, s_tabmove = sem("step_table_ready"), sem("step_table_moved")
        s_wA, s_wF, s_out = sem("step_attn_weights_loaded"), sem("step_ffn_weights_loaded"), sem("out_stored")
        s_dve = sem("dve_chain")
        s_zero, s_w81p = sem("pool_constants_written"), sem("w81_parts_ready")
        s_gb, s_ga = sem("table_b_in_psum"), sem("table_a_in_psum")
        s_gcopy = [sem("table_a_banks_copied"), sem("table_b_banks_copied")]
        s_mean, s_xc, s_sq, s_vh, s_vhs, s_vp, s_std, s_rstd = (sem(n) for n in (
            "mean_in_psum", "x_centred", "x_squared", "half_vars_in_psum", "half_vars_copied", "vars_in_psum",
            "deviation_ready", "rstd_ready"))
        s_conv, s_convA, s_convD = sem("conv_in_psum"), sem("conv_scaled_by_act"), sem("conv_scaled_by_dve")
        s_lnc, s_lns, s_lnv, s_lnd, s_ln = (sem(n) for n in (
            "half_centred", "half_squared", "variance_ready", "ln_deviation_ready", "half_normed"))
        s_bd, s_bdv, s_spk, s_negm, s_vb = (sem(n) for n in (
            "block_weights_ready", "value_weights_ready", "spikes_ready", "mask_ready", "v_bias_added"))
        s_tokb = sem("residual_ready")
        s_task, s_da, s_dd = sem("task_in_psum"), sem("task_drained_by_act"), sem("task_drained_by_dve")
        s_S, s_nm, s_P, s_ri, s_Pn, s_T, s_PT = (sem(n) for n in (
            "scores_in_psum", "row_max_ready", "exponentials_ready", "row_sums_inverted", "probs_ready",
            "probsT_in_psum", "probsT_copied"))
        s_w1z, s_row, s_op, s_seen, s_wp, s_bd2 = sem("ffn_weights_placed"), sem("token0_in_psum"), sem("op_ready"), sem("op_seen_by_pool"), sem(
            "step_weight_products_in_psum"), sem("step_block_weights_ready")
        s_fin = sem("out_ready")

        block = ctx.enter_context(nc.Block())

        def wait(eng, s, base, k):
            if type(base) is int and base + k <= 0:
                return
            eng.wait_ge(s, base + k)

        RING = 3
        SCORES = (0, 1, 4)
        AHEAD = len(SCORES)
        TOEP = "D" * NE
        CONVT = "DA"
        PRE = "A" + "A" + "AD" + "A" + "AAAA" + "AAAA" + "AAAA" + "D"
        ATTY = "AAAA"
        YTOK = "AA"
        H0 = "AA" + "AD"
        LPRE = "ADAD" + "ADAD"
        FF = "ADADAD" + "AD" + "AD" + "AD"
        K_CONVT = len(TOEP)
        K_WVO = K_CONVT + len(CONVT)
        K_PRE = K_WVO + 2
        K_CUR = K_PRE + NH
        K_Q = K_CUR + 1
        K_V = K_Q + 2 * NG
        K_CNT = K_V + NG
        K_ATT = K_CNT + 1
        K_YTOK = K_ATT + len(ATTY)
        K_H0 = K_YTOK + len(YTOK)
        STATIC = TOEP + CONVT + PRE + ATTY + YTOK + H0
        assert K_H0 + len(H0) == len(STATIC) and K_ATT == len(TOEP + CONVT + PRE)
        LATT = LPRE + ATTY
        HORDER = [("H", 0), ("H", 1), ("H", 2), ("H", 3), ("H", 4), ("H", 5), ("Z", 0), ("Z", 1), ("H", 6), ("H", 7),
                  ("Z", 2), ("Z", 3)]
        assert len(HORDER) == len(FF)
        SPARE = 7
        MAIN = B - GB + 1
        YORDER = HORDER[:3] + [("Y", NG - 1)] + HORDER[3:]
        LATTF = LPRE + ATTY[:NG - 1] + FF[:3] + "A" + FF[3:]
        K_YF = len(LPRE) + NG - 1

        def count(who, owners):
            return sum(o == who for o in owners)

        class Tasks:

            def __init__(self, owners, at=0, a=0, d=0):
                self.owners, self.at, self.a, self.d = owners, at, a, d

            def bank(self, k):
                return bank[8 - RING + k % RING]

            def fill_wait(self, pe, k):
                if k >= RING:
                    who = self.owners[k - RING]
                    n = count(who, self.owners[:k - RING + 1])
                    wait(pe, s_da if who == "A" else s_dd, self.a if who == "A" else self.d, n)
                elif k == 0:
                    wait(pe, s_da, self.a, 0)
                    wait(pe, s_dd, self.d, 0)

            def filled(self, eng, k):
                wait(eng, s_task, self.at, k + 1)

            def drained(self, eng, k):
                wait(eng, s_da, self.a, count("A", self.owners[:k]))
                wait(eng, s_dd, self.d, count("D", self.owners[:k]))

        st = Tasks(STATIC)

        def rep(ap, n):
            p, m = ap.shape
            return ap.unsqueeze(1).broadcast_to([p, n, m])

        def flat(ap):
            names = "abcd"[:len(ap.shape) - 1]
            return ap.rearrange(f"p {' '.join(names)} -> p ({' '.join(names)})")

        def next_step(eng, step, reg_r, reg_op, reg_code):
            r = eng.snap(reg_r) + 1
            eng.wait_ge(s_op, r)
            eng.reg_alu(reg_r, reg_r, 1, ALU.add)
            eng.reg_load(reg_op, opi[0:1, 0:1])
            op = eng.snap(reg_op, min_val=0, max_val=NOPS - 1)
            eng.reg_load(reg_code, tab[0:1, bass.ds(op * (NSTEPS + 1) + (NSTEPS - 1) - step, 1)])

        @block.sync
        def _(sp):
            sp.dma_start(w81[:, :], d["w81"]).then_inc(s_w81, 16)
            sp.dma_start(constb[:, :], d["constb"]).then_inc(s_cb, 16)
            sp.dma_start(flat(xrev[:, :, :, :]).rearrange("p (h n) -> p h n", h=NH),
                         d["xrev"].rearrange("(h p) n -> p h n", p=P)).then_inc(s_xrev, 16)
            sp.dma_start(constf[:, :], d["constf"]).then_inc(s_cf, 16)
            kf = d["kpef"]
            for y in range(YH):
                shifted = bass.AP(tensor=kf.tensor, offset=(R - YH - y) * KS + R - (HW - 1), ap=[[1, HW], [KS, NE], [1, HW]])
                sp.dma_start(toepk[y * HW:(y + 1) * HW, :, :], shifted).then_inc(s_kpe, 16)
            sp.dma_start(wl1[:, :], d["wl1"]).then_inc(s_wl1, 16)
            sp.dma_start(wl2[:, :], d["wl2"]).then_inc(s_wl2, 16)
            sp.dma_start(flat(xin[:, :, :, :]).rearrange("p (h n) -> p h n", h=NH),
                         d["xtok"].rearrange("(h p) n -> p h n", p=P)).then_inc(s_xin, 16)
            sp.dma_start(masks8[:, :, :], d["masks"]).then_inc(s_tabl, 16)
            sp.dma_start(flat(maskc[:, :, :]), d["maskc"]).then_inc(s_mask, 16)
            sp.wait_ge(s_tabi, 1)
            sp.dma_start(tabd[:, :], tabi[:, :]).then_inc(s_tabmove, 16)
            sp.wait_ge(s_tabmove, 16)
            sp.dma_start(tab[0:1, :], tabd[:, :].rearrange("n m -> (n m)").unsqueeze(0)).then_inc(s_tabmove, 16)

            reg_f = sp.alloc_register("sp_ffn_loads")
            sp.reg_mov(reg_f, 16)
            reg_code, reg_op, reg_step, reg_kind, reg_r = (
                sp.alloc_register("sp_" + n) for n in ("code", "op", "step", "kind", "round"))
            sp.reg_mov(reg_r, 1)
            sp.wait_ge(s_tabmove, 32)
            sp.wait_ge(s_op, 1)
            sp.reg_load(reg_op, opi[0:1, 0:1])
            op = sp.snap(reg_op, min_val=0, max_val=NOPS - 1)
            sp.reg_load(reg_code, tab[0:1, bass.ds(op * (NSTEPS + 1) + NSTEPS, 1)])
            with sp.While(lambda: sp.snap(reg_code) < NONE):
                sp.reg_alu(reg_step, reg_code, 2, ALU.logical_shift_right)
                sp.reg_alu(reg_kind, reg_code, 3, ALU.bitwise_and)
                b = sp.snap(reg_step, min_val=0, max_val=NSTEPS - 1)
                kind = sp.snap(reg_kind)
                op = sp.snap(reg_op, min_val=0, max_val=NOPS - 1)
                n = b * NOPS + op
                r = sp.snap(reg_r)
                sp.dma_start(wa[:, :], d["wa"][bass.ds(n, 1), :, :].rearrange("o p n -> (o p) n")).then_inc(s_wA, 16)
                sp.dma_start(wf[:, :], d["wf"][bass.ds(n, 1), :, :].rearrange("o p n -> (o p) n")).then_inc(s_wF, 16)
                f = sp.snap(reg_f)
                sp.wait_ge(s_wA, r * 16)
                sp.wait_ge(s_wF, f)
                r = sp.snap(reg_r) + 1
                sp.wait_ge(s_op, r)
                sp.reg_alu(reg_r, reg_r, 1, ALU.add)
                sp.reg_alu(reg_f, reg_f, 16, ALU.add)
                sp.reg_load(reg_op, opi[0:1, 0:1])
                op = sp.snap(reg_op, min_val=0, max_val=NOPS - 1)
                sp.reg_load(reg_code, tab[0:1, bass.ds(op * (NSTEPS + 1) + (NSTEPS - 1) - b, 1)])
            for i in range(2):
                sp.wait_ge(s_fin, i + 1)
                sp.dma_start(d["out"].rearrange("(g p) s -> p g s", p=P)[:, 2 * i:2 * i + 2, :],
                             outT[:, 2 * i:2 * i + 2, :]).then_inc(s_out, 16)
            sp.wait_ge(s_out, 32)

        def attention_pool(pool, reg_att=None):
            for b in range(B):
                if reg_att is None:
                    pool.wait_ge(s_ri, b + 1)
                else:
                    att = pool.snap(reg_att) + 1
                    pool.wait_ge(s_ri, att)
                    pool.reg_alu(reg_att, reg_att, 1, ALU.add)
                for ih in range(NH):
                    last = nc.gpsimd.tensor_scalar(prob[b % NPB][:, ih, :], prob[b % NPB][:, ih, :], einv[:, b, ih:ih + 1], 1.0,
                                                   ALU.mult, ALU.mult)
                last.then_inc(s_Pn, 1)

        @block.gpsimd
        def _(pool):
            nc.gpsimd.memset(ones256[:, :], 1.0 / S).then_inc(s_zero, 1)
            nc.gpsimd.memset(eps[:, :], 1e-5).then_inc(s_zero, 1)
            nc.gpsimd.memset(onesb[:, :], 1.0).then_inc(s_zero, 1)
            nc.gpsimd.memset(dsum[:, :], 0.0).then_inc(s_zero, 1)
            nc.gpsimd.memset(qz[:, :, :], 0.0).then_inc(s_zero, 1)
            nc.gpsimd.memset(w1z[:, :, :], 0.0).then_inc(s_zero, 1)
            wait(pool, s_da, 0, count("A", STATIC[:K_PRE]))
            pool.wait_ge(s_cf, 16)
            nc.gpsimd.tensor_tensor(bdv[:, :], wvo[:, :], blk, ALU.mult).then_inc(s_bdv, 1)
            for g in range(NG):
                wait(pool, s_da, 0, count("A", STATIC[:K_V + g + 1]))
                for h in range(NH):
                    vg = v[:, h, g * GB:(g + 1) * GB, :]
                    nc.gpsimd.tensor_tensor(vg, vg, rep(bvo[:, :], GB), ALU.add).then_inc(s_vb, 1)
            attention_pool(pool)
            reg_att = pool.alloc_register("pool_att")
            pool.reg_mov(reg_att, B)
            reg_code, reg_op, reg_step, reg_kind, reg_r = (
                pool.alloc_register("pool_" + n) for n in ("code", "op", "step", "kind", "round"))
            pool.reg_mov(reg_r, 1)
            pool.wait_ge(s_tabmove, 32)
            pool.wait_ge(s_op, 1)
            pool.reg_load(reg_op, opi[0:1, 0:1])
            op = pool.snap(reg_op, min_val=0, max_val=NOPS - 1)
            pool.reg_load(reg_code, tab[0:1, bass.ds(op * (NSTEPS + 1) + NSTEPS, 1)])
            with pool.While(lambda: pool.snap(reg_code) < NONE):
                pool.reg_alu(reg_step, reg_code, 2, ALU.logical_shift_right)
                pool.reg_alu(reg_kind, reg_code, 3, ALU.bitwise_and)
                b = pool.snap(reg_step, min_val=0, max_val=NSTEPS - 1)
                kind = pool.snap(reg_kind)
                nc.gpsimd.memset(seen[:, :], 0.0).then_inc(s_seen, 1)
                with pool.If(kind >= 2):
                    attention_pool(pool, reg_att)
                next_step(pool, b, reg_r, reg_op, reg_code)

        def product_pe(pe, t, k, lhsT, rhs, cols):
            t.fill_wait(pe, k)
            pe.matmul(t.bank(k)[:, 0:cols], lhsT, rhs, start=True, stop=True).then_inc(s_task, 1)

        def turn_pe(pe, base, b):
            wait(pe, s_Pn, base, b + 1)
            if b >= 2:
                wait(pe, s_PT, base, b - 1)
            for jh in range(NH):
                for ih in range(NH):
                    mm = pe.transpose(bank[2 + b % 2][:, jh * S + ih * P:jh * S + (ih + 1) * P],
                                      prob[b % NPB][:, ih, jh * P:(jh + 1) * P], ident)
            mm.then_inc(s_T, 1)

        def weigh_pe(pe, base, t, k0, g):
            t.fill_wait(pe, k0 + g)
            if g == 0:
                t.drained(pe, k0)
                if t is st:
                    pe.wait_ge(s_vb, NG * NH)
            wait(pe, s_PT, base, GB * (g + 1))
            for jh in range(NH):
                for q in range(GB):
                    b = g * GB + q
                    mm = pe.matmul(t.bank(k0 + g)[q * C:(q + 1) * C, 0:S], v[:, jh, b, :], probT[b % NTB][:, jh, :],
                                   start=(jh == 0), stop=(jh == NH - 1), tile_position=(0, q * C))
            mm.then_inc(s_task, 1)

        def attention_pe(pe, base, t, k0, keys, masked, meanwhile=None):
            def scores(b):
                if b >= AHEAD:
                    wait(pe, s_P, base, b - AHEAD + 1)
                if not masked and b % GB == 0:
                    t.drained(pe, b // GB + 1)
                for ih in range(NH):
                    mm = pe.matmul(bank[SCORES[b % AHEAD]][:, ih * S:(ih + 1) * S], qz[:, b, ih * P:(ih + 1) * P],
                                   keys[:, b // GB, :], start=True, stop=True)
                mm.then_inc(s_S, 1)

            for b in range(AHEAD):
                scores(b)
            if meanwhile:
                meanwhile()
            if masked:
                pe.wait_ge(s_spk, 1)
                product_pe(pe, st, K_CNT, onesb[:, :], spk[:, :], S)
            for b in range(MAIN):
                if b + AHEAD < B:
                    scores(b + AHEAD)
                turn_pe(pe, base, b)
                if b % GB == 0 and b:
                    weigh_pe(pe, base, t, k0, b // GB - 1)

        @block.tensor
        def _(pe):
            def keep_clock(n):
                for h in range(NH + 1):
                    if h:
                        pe.wait_ge(s_lnc, NH * n + h)
                    for i in range(SPARE):
                        pe.matmul(bank[0][:, :], identb, constb[:, 0:512].bitcast(BF16), start=True, stop=True)

            pe.wait_ge(s_cb, 16)
            pe.wait_ge(s_w81p, 1)
            cexp = colexp.rearrange("k (t b s) -> k t (b s)", t=2, s=8)

            def table(tb, x, out):
                return pe.matmul(out[:, (x % 5) * 3 * C:(x % 5 + 1) * 3 * C], cexp[:, tb, (HW - 1 - x) * 8:(2 * HW - 1 - x) * 8],
                                 flat(w81p[:, :, :]), start=True, stop=True)
            for x in range(HW):
                mm = table(1, x, bank[4 + x // 5])
            mm.then_inc(s_gb, 1)
            pe.wait_ge(s_zero, 3)
            pe.wait_ge(s_xrev, 16)
            for h in range(NH):
                mm = pe.matmul(bank[1][:, :], ones256[:, :], flat(xrev[:, h, :, :]), start=(h == 0), stop=(h == NH - 1))
            mm.then_inc(s_mean, 1)
            for x in range(HW):
                if x == HW - 1:
                    pe.wait_ge(s_xc, NH)
                mm = table(0, x, bank[(2, 3, 0, 1)[x // 5]])
            mm.then_inc(s_ga, 1)
            for e in range(NE):
                if e == 0:
                    pe.wait_ge(s_gcopy[1], 4)
                if e == YH:
                    pe.wait_ge(s_gcopy[0], 4)
                if e == 12:
                    pe.wait_ge(s_sq, 2)
                    for cg in range(CG):
                        mm = pe.matmul(bank[2][:, cg:cg + 1], flat(sqc[:, cg * GB:(cg + 1) * GB, :, :]), ones256[:, 0:1],
                                       start=True, stop=True)
                    mm.then_inc(s_vh, 1)
                if e == 16:
                    pe.wait_ge(s_vhs, 1)
                    pe.wait_ge(s_cf, 16)
                    pe.matmul(bank[3][:, 0:CG], pairs, vhalf[:, :], start=True, stop=True).then_inc(s_vp, 1)
                st.fill_wait(pe, e)
                a0 = YH - e + HW - 1
                for i in range(3):
                    mm = pe.matmul(st.bank(e)[:, :], rowsel[:, a0 * HW:(a0 + YH) * HW],
                                   flat(gtab[:, 1 if e < YH else 0, i, :, :]), start=(i == 0), stop=(i == 2))
                mm.then_inc(s_task, 1)
            st.fill_wait(pe, K_CONVT + 1)
            pe.wait_ge(s_xin, 16)
            pe.matmul(st.bank(K_CONVT + 1)[:, :], ident, xin[:, 1, :, :].rearrange("p b c -> p c b"), start=True, stop=False)
            st.drained(pe, K_CONVT)
            pe.wait_ge(s_std, 1)
            for j in range(CG // 2):
                for cg in (2 * j, 2 * j + 1):
                    for hi in range(NH):
                        for q in range(GB):
                            c = cg * GB + q
                            if hi == 0:
                                left, rows = flat(xcc[:, c, :, :]), NH * B
                            else:
                                left, rows = xcc[:, c, 1, :], B
                            mm = pe.matmul(bank[j][q * 32:q * 32 + rows, (cg % 2) * S:(cg % 2 + 1) * S], left,
                                           flat(toep[:, c, (1 - hi) * YH:(3 - hi) * YH, :]), start=(hi == 0), stop=(hi == 1),
                                           tile_position=(0, q * 32))
                mm.then_inc(s_conv, 1)
            for h in range(NH):
                if h == 0:
                    st.fill_wait(pe, K_CONVT)
                for cg in range(CG):
                    if h == 0 and cg % 2 == 0:
                        pe.wait_ge(s_convA if cg % 4 == 0 else s_convD, cg // 4 + 1)
                    mm = pe.matmul(st.bank(K_CONVT + h)[:, cg * GB * B:(cg + 1) * GB * B], convr[:, cg, h * P:(h + 1) * P], pick,
                                   start=(h == 0 and cg == 0), stop=(cg == CG - 1))
                mm.then_inc(s_task, 1)

            def transposed(k, src, h):
                st.fill_wait(pe, k)
                for g in range(NG):
                    mm = pe.transpose(st.bank(k)[:, g * P:(g + 1) * P], flat(src[:, h, g * GB:(g + 1) * GB, :]), ident)
                mm.then_inc(s_task, 1)

            def values(t, k, src, g, w):
                t.fill_wait(pe, k)
                for h in range(NH):
                    mm = pe.matmul(t.bank(k)[:, h * P:(h + 1) * P], src[:, g, h * P:(h + 1) * P], w, start=True, stop=True)
                mm.then_inc(s_task, 1)

            pe.wait_ge(s_wl2, 16)
            product_pe(pe, st, K_WVO, wvl, rep(wor, NG), P)
            product_pe(pe, st, K_WVO + 1, bvc.broadcast_to([C, P]), wor, C)
            keep_clock(0)
            for h in range(NH):
                pe.wait_ge(s_ln, h + 1)
                transposed(K_PRE + h, xh, h)
            pe.wait_ge(s_bd, 1)
            st.drained(pe, K_CUR)
            st.fill_wait(pe, K_CUR)
            for g in range(NG):
                mm = pe.matmul(st.bank(K_CUR)[0:B, 0:S], wsb[:, g, :], xt[:, g, :], start=(g == 0), stop=(g == NG - 1))
            mm.then_inc(s_task, 1)
            for g in range(NG):
                product_pe(pe, st, K_Q + g, bdq[:, :], xt[:, g, :], S)
            for g in range(NG):
                product_pe(pe, st, K_Q + NG + g, bdk[:, :], xt[:, g, :], S)
            pe.wait_ge(s_bdv, 1)
            for g in range(NG):
                values(st, K_V + g, xt, g, bdv[:, :])
            st.drained(pe, K_V)
            attention_pe(pe, 0, st, K_ATT, kt, True)
            for b in range(MAIN, B):
                turn_pe(pe, 0, b)
                if b > MAIN:
                    h = b - MAIN - 1
                    st.fill_wait(pe, K_YTOK + h)
                    pe.wait_ge(s_tokb, 1)
                    pe.matmul(st.bank(K_YTOK + h)[:, :], ident, flat(tokb[:, h, :, :]), start=True, stop=False)
            weigh_pe(pe, 0, st, K_ATT, NG - 1)
            wait(pe, s_da, 0, count("A", STATIC[:K_YTOK]))
            for h in range(NH):
                for g in range(NG):
                    mm = pe.matmul(st.bank(K_YTOK + h)[:, g * P:(g + 1) * P], yT[:, g, h * P:(h + 1) * P], ident,
                                   start=False, stop=(g == NG - 1))
                mm.then_inc(s_task, 1)
            st.drained(pe, K_YTOK + 1)
            transposed(K_H0, tok, 0)
            reg_att, reg_task, reg_da, reg_dd = (pe.alloc_register(n) for n in ("pe_att", "pe_task", "pe_da", "pe_dd"))
            pe.reg_mov(reg_att, B)
            reg_wp = pe.alloc_register("pe_weight_products")
            pe.reg_mov(reg_wp, 0)
            pe.reg_mov(reg_task, len(STATIC))
            pe.reg_mov(reg_da, count("A", STATIC))
            pe.reg_mov(reg_dd, count("D", STATIC))
            reg_code, reg_op, reg_step, reg_kind, reg_r = (
                pe.alloc_register("pe_" + n) for n in ("code", "op", "step", "kind", "round"))
            pe.reg_mov(reg_r, 1)
            pe.wait_ge(s_tabmove, 32)
            pe.wait_ge(s_op, 1)
            pe.reg_load(reg_op, opi[0:1, 0:1])
            op = pe.snap(reg_op, min_val=0, max_val=NOPS - 1)
            pe.reg_load(reg_code, tab[0:1, bass.ds(op * (NSTEPS + 1) + NSTEPS, 1)])
            reg_next, reg_loads = pe.alloc_register("pe_next_kind"), pe.alloc_register("pe_attn_loads")

            def weight_products():
                pe.reg_alu(reg_next, reg_code, 2, ALU.bitwise_and)
                with pe.If(pe.snap(reg_next) != 0):
                    pe.reg_alu(reg_loads, reg_r, 16, ALU.mult)
                    loads = pe.snap(reg_loads)
                    pe.wait_ge(s_wA, loads)
                    for i in range(2):
                        pe.matmul(bank[2 + i][:, 0:P], wa[:, i * GB * C:(i + 1) * GB * C],
                                  rep(wa[:, (2 * GB + i) * C:(2 * GB + i + 1) * C], NG), start=True, stop=True).then_inc(s_wp, 1)

            weight_products()
            st.drained(pe, K_YTOK + NH)
            transposed(K_H0 + 1, tok, 1)
            for h in range(NH):
                pe.wait_ge(s_ln, NH + h + 1)
                transposed(K_H0 + NH + h, xh, h)
            with pe.While(lambda: pe.snap(reg_code) < NONE):
                pe.reg_alu(reg_step, reg_code, 2, ALU.logical_shift_right)
                pe.reg_alu(reg_kind, reg_code, 3, ALU.bitwise_and)
                b = pe.snap(reg_step, min_val=0, max_val=NSTEPS - 1)
                kind = pe.snap(reg_kind)
                r = pe.snap(reg_r)
                with pe.If(kind >= 2):
                    att = pe.snap(reg_att)
                    t = Tasks(LATT, pe.snap(reg_task), pe.snap(reg_da), pe.snap(reg_dd))
                    wp = pe.snap(reg_wp)
                    wait(pe, s_bd2, wp, 2)
                    for g in range(NG):
                        product_pe(pe, t, g, bda[:, :], hT[:, g, :], S)

                    def all_values():
                        for g in range(NG):
                            values(t, NG + g, hT, g, bdv[:, :])

                    attention_pe(pe, att, t, len(LPRE), hT, False, all_values)

                def count_tasks(owners, attended):
                    if attended:
                        pe.reg_alu(reg_wp, reg_wp, 2, ALU.add)
                        pe.reg_alu(reg_att, reg_att, B, ALU.add)
                    pe.reg_alu(reg_task, reg_task, len(owners), ALU.add)
                    pe.reg_alu(reg_da, reg_da, count("A", owners), ALU.add)
                    pe.reg_alu(reg_dd, reg_dd, count("D", owners), ALU.add)

                def ffn(t, k0, order, att=None):
                    for i, (what, n) in enumerate(order):
                        k = k0 + i
                        if what == "H":
                            if att is not None and i < 3:
                                turn_pe(pe, att, MAIN + i)
                            if i == 0:
                                pe.wait_ge(s_w1z, r)
                            if att is not None and n == GB:
                                t.drained(pe, k0 + order.index(("Y", NG - 1)) + 1)
                            gp, q = divmod(n, GB)
                            product_pe(pe, t, k, w1z[:, q, :], flat(hT[:, 2 * gp:2 * gp + 2, :]), 2 * S)
                            if i == 2:
                                t.drained(pe, k0 + 1)
                                pe.matmul(bank[0][0:1, 0:C], relu[:, 0, 0, 0:1], w2s, start=True, stop=False)
                                pe.matmul(bank[0][0:1, 0:C], b2s, ident[:, 0:C], start=False, stop=True).then_inc(s_row, 1)
                        elif what == "Y":
                            weigh_pe(pe, att, t, k - n, n)
                        else:
                            if n == 2:
                                next_step(pe, b, reg_r, reg_op, reg_code)
                                weight_products()
                            t.fill_wait(pe, k)
                            t.drained(pe, k0 + order.index(("H", GB * (n // 2 + 1) - 1)) + 1)
                            for q in range(GB):
                                mm = pe.matmul(t.bank(k)[q * C:(q + 1) * C, 0:S], w2s, relu[:, q, n, :],
                                               start=True, stop=True, tile_position=(0, q * C))
                            mm.then_inc(s_task, 1)

                with pe.If(kind == 1):
                    ffn(Tasks(FF, pe.snap(reg_task), pe.snap(reg_da), pe.snap(reg_dd)), 0, HORDER)
                    count_tasks(FF, False)
                with pe.If(kind == 3):
                    ffn(Tasks(LATTF, pe.snap(reg_task), pe.snap(reg_da), pe.snap(reg_dd)), K_YF, YORDER, pe.snap(reg_att))
                    count_tasks(LATTF, True)
                with pe.If(kind == 2):
                    att = pe.snap(reg_att)
                    t = Tasks(LATT, pe.snap(reg_task), pe.snap(reg_da), pe.snap(reg_dd))
                    for last in range(MAIN, B):
                        turn_pe(pe, att, last)
                    weigh_pe(pe, att, t, len(LPRE), NG - 1)
                    count_tasks(LATT, True)
                    da, dd = pe.snap(reg_da), pe.snap(reg_dd)
                    pe.wait_ge(s_da, da)
                    pe.wait_ge(s_dd, dd)
                    pe.matmul(bank[0][0:1, 0:C], hT[:, 0, 0:1], ident[:, 0:C], start=True, stop=True).then_inc(s_row, 1)
                    next_step(pe, b, reg_r, reg_op, reg_code)
                    weight_products()

        def drain_y(act, t, k0, g, dst):
            t.filled(act, k0 + g)
            nc.scalar.activation(dst[:, g, :], t.bank(k0 + g)[:, 0:S], ACT.Copy).then_inc(s_da, 1)

        def attention_act(act, base, t, k0, dst, masked, meanwhile=None):
            for b in range(B):
                wait(act, s_nm, base, b + 1)
                if b >= NPB:
                    wait(act, s_T, base, b - NPB + 1)
                for ih in range(NH):
                    scores = minus[b % AHEAD][:, ih, :] if masked else bank[SCORES[b % AHEAD]][:, ih * S:(ih + 1) * S]
                    e = nc.scalar.activation(prob[b % NPB][:, ih, :], scores, ACT.Exp, bias=nmax[:, b, ih:ih + 1],
                                             scale=-1.0 if masked else 1.0, accum_out=esum[:, b, ih:ih + 1])
                e.then_inc(s_P, 1)
                if meanwhile and b < NG // 2:
                    meanwhile(2 * b)
                if b >= 6 and (b - 6) % GB == 0:
                    drain_y(act, t, k0, (b - 6) // GB, dst)

        @block.scalar
        def _(act):
            def copy_table(t, i, src):
                n = min(5, HW - 5 * i)
                nc.scalar.activation(gtab[:, t, :, :, 5 * i:5 * i + n].rearrange("p t c x -> p x (t c)"),
                                     src[:, 0:n * 3 * C].rearrange("p (x n) -> p x n", x=n), ACT.Copy).then_inc(s_gcopy[t], 1)

            def ln_act(n, copy_tok):
                for h in range(NH):
                    act.wait_ge(s_lnc, NH * n + h + 1)
                    nc.scalar.activation(sq[:, h, :, :], xc[:, h, :, :], ACT.Square).then_inc(s_lns, 1)
                    if h == 0:
                        copy_tok(0)
                for h in range(NH):
                    hb = slice(h * B, (h + 1) * B)
                    act.wait_ge(s_lnv, NH * n + h + 1)
                    nc.scalar.activation(dev[:, hb], var[:, hb], ACT.Sqrt, bias=eps[:, :], scale=1.0 / C).then_inc(s_lnd, 1)
                    if h == 0:
                        copy_tok(1)

            act.wait_ge(s_gb, 1)
            for i in range(2):
                copy_table(1, i, bank[4 + i])
            act.wait_ge(s_ga, 1)
            for i in range(2):
                copy_table(0, i, bank[2 + i])
            act.wait_ge(s_xc, NH)
            for i in range(2):
                cs = slice(i * C // 2, (i + 1) * C // 2)
                nc.scalar.activation(flat(sqc[:, cs, :, :]), flat(xcc[:, cs, :, :]), ACT.Square).then_inc(s_sq, 1)
            act.wait_ge(s_vh, 1)
            nc.scalar.activation(vhalf[:, :], bank[2][:, 0:CG], ACT.Copy).then_inc(s_vhs, 1)
            act.wait_ge(s_zero, 3)
            act.wait_ge(s_vp, 1)
            nc.scalar.activation(stdv[:, :], bank[3][:, 0:CG], ACT.Sqrt, bias=eps[:, :]).then_inc(s_std, 1)
            act.wait_ge(s_rstd, 1)
            for j in range(0, CG // 2, 2):
                act.wait_ge(s_conv, j + 1)
                for cg in (2 * j, 2 * j + 1):
                    cp = nc.scalar.activation(convr[:, cg, :], bank[j][:, (cg % 2) * S:(cg % 2 + 1) * S], ACT.Copy,
                                              scale=rstd[:, cg:cg + 1])
                cp.then_inc(s_convA, 1)

            def copy(t, k, dst, src):
                t.filled(act, k)
                nc.scalar.activation(dst, src, ACT.Copy).then_inc(s_da, 1)

            def copy_conv_residual(h):
                if h == 1:
                    copy(st, K_CONVT + h, tok[:, h, :, :], st.bank(K_CONVT + h)[:, :].rearrange("p (c b) -> p b c", b=B))

            ln_act(0, copy_conv_residual)
            copy(st, K_WVO, wvo[:, :], st.bank(K_WVO)[:, 0:P])
            copy(st, K_WVO + 1, bvo[:, :], st.bank(K_WVO + 1)[:, 0:C])

            def copy_half(k, h, dst):
                copy(st, k, dst[:, :, h * P:(h + 1) * P], st.bank(k)[:, :].rearrange("p (g s) -> p g s", g=NG))

            copy_half(K_PRE, 0, xt)
            act.wait_ge(s_wl1, 16)
            st.filled(act, K_CUR)
            nc.scalar.activation(cur[:, :], st.bank(K_CUR)[0:B, 0:S], ACT.Identity, bias=bsr[0:B, :]).then_inc(s_da, 1)
            act.wait_ge(s_zero, 6)
            act.wait_ge(s_bd, 1)
            for g in range(NG):
                k = K_Q + g
                st.filled(act, k)
                for q in range(GB):
                    rows = slice(q * C, (q + 1) * C)
                    cp = nc.scalar.activation(qz[rows, g * GB + q, :], st.bank(k)[rows, 0:S], ACT.Identity,
                                              bias=bqs[rows, :], scale=SCALE)
                cp.then_inc(s_da, 1)
            for g in range(NG):
                k = K_Q + NG + g
                st.filled(act, k)
                nc.scalar.activation(kt[:, g, :], st.bank(k)[:, 0:S], ACT.Identity, bias=bkr).then_inc(s_da, 1)

            def copy_values(t, k, g):
                t.filled(act, k)
                nc.scalar.activation(v[:, :, g * GB:(g + 1) * GB, :].rearrange("p h b c -> p h (b c)"),
                                     t.bank(k)[:, 0:S].rearrange("p (h n) -> p h n", h=NH), ACT.Copy).then_inc(s_da, 1)

            for g in range(NG):
                copy_values(st, K_V + g, g)
            nc.scalar.activation(table[:, :], eps[0:1, :], ACT.Exp)
            attention_act(act, 0, st, K_ATT, yT, True)
            drain_y(act, st, K_ATT, NG - 1, yT)
            nc.scalar.activation(table[:, :], eps[0:1, :], ACT.Sqrt)

            ln_act(1, lambda h: copy(st, K_YTOK + h, flat(tok[:, h, :, :]), st.bank(K_YTOK + h)[:, :]))
            for h in range(NH):
                copy_half(K_H0 + h, h, outT)
            reg_att, reg_task = act.alloc_register("act_att"), act.alloc_register("act_task")
            act.reg_mov(reg_att, B)
            act.reg_mov(reg_task, len(STATIC))
            reg_code, reg_op, reg_step, reg_kind, reg_r = (
                act.alloc_register("act_" + n) for n in ("code", "op", "step", "kind", "round"))
            act.reg_mov(reg_r, 1)
            act.wait_ge(s_tabmove, 32)
            act.wait_ge(s_op, 1)
            act.reg_load(reg_op, opi[0:1, 0:1])
            op = act.snap(reg_op, min_val=0, max_val=NOPS - 1)
            act.reg_load(reg_code, tab[0:1, bass.ds(op * (NSTEPS + 1) + NSTEPS, 1)])
            reg_next = act.alloc_register("act_next_kind")
            act.reg_alu(reg_next, reg_code, 3, ALU.bitwise_and)
            with act.If(act.snap(reg_next) == 1):
                act.wait_ge(s_wA, 16)
                act.wait_ge(s_wF, 16)
                for q in range(GB):
                    nc.scalar.activation(w1z[q * C:(q + 1) * C, q, :], wa[:, NWA:NWA + HID], ACT.Copy)
                nc.scalar.activation(wfs[:, :], wf[:, :], ACT.Copy).then_inc(s_w1z, 1)
            copy_half(K_H0 + NH, 0, hT)
            nc.scalar.activation(table[:, :], eps[0:1, :], ACT.Exp)
            with act.While(lambda: act.snap(reg_code) < NONE):
                act.reg_alu(reg_step, reg_code, 2, ALU.logical_shift_right)
                act.reg_alu(reg_kind, reg_code, 3, ALU.bitwise_and)
                b = act.snap(reg_step, min_val=0, max_val=NSTEPS - 1)
                kind = act.snap(reg_kind)
                r = act.snap(reg_r)
                with act.If(kind >= 2):
                    att = act.snap(reg_att)
                    t = Tasks(LATT, act.snap(reg_task))
                    for g in range(0, NG, 2):
                        t.filled(act, g)
                        for q in range(GB):
                            rows = slice(q * C, (q + 1) * C)
                            cp = nc.scalar.activation(qz[rows, g * GB + q, :], t.bank(g)[rows, 0:S], ACT.Copy)
                        cp.then_inc(s_da, 1)
                    attention_act(act, att, t, len(LPRE), hT, False, lambda g: copy_values(t, NG + g, g))
                    act.reg_alu(reg_att, reg_att, B, ALU.add)

                def ffn(t, k0, order):
                    for i, (what, n) in enumerate(order):
                        k = k0 + i
                        if t.owners[k] != "A":
                            continue
                        if i == 0:
                            act.wait_ge(s_w1z, r)
                        if (what, n) == ("Z", 2):
                            next_step(act, b, reg_r, reg_op, reg_code)
                        if what == "Y":
                            drain_y(act, t, k - n, n, hT)
                            continue
                        t.filled(act, k)
                        if what == "H":
                            gp, q = divmod(n, GB)
                            nc.scalar.activation(relu[:, q, 2 * gp:2 * gp + 2, :],
                                                 t.bank(k)[:, :].rearrange("p (g s) -> p g s", g=2),
                                                 ACT.Relu, bias=b1s).then_inc(s_da, 1)
                        else:
                            nc.scalar.activation(hT[:, n, :], t.bank(k)[:, 0:S], ACT.Identity, bias=b2s).then_inc(s_da, 1)

                with act.If(kind == 1):
                    ffn(Tasks(FF, act.snap(reg_task)), 0, HORDER)
                    act.reg_alu(reg_task, reg_task, len(FF), ALU.add)
                with act.If(kind == 3):
                    ffn(Tasks(LATTF, act.snap(reg_task)), K_YF, YORDER)
                    act.reg_alu(reg_task, reg_task, len(LATTF), ALU.add)
                with act.If(kind == 2):
                    drain_y(act, Tasks(LATT, act.snap(reg_task)), len(LPRE), NG - 1, hT)
                    act.reg_alu(reg_task, reg_task, len(LATT), ALU.add)
                    next_step(act, b, reg_r, reg_op, reg_code)

        @block.vector
        def _(dve):
            chain = {"base": 0, "n": 0}

            def link(ins):
                chain["n"] += 1
                ins.then_inc(s_dve, 1)
                dve.wait_ge(s_dve, chain["base"] + chain["n"])

            dve.wait_ge(s_w81, 16)
            link(nc.vector.tensor_copy(w81p[:, 0, :], w81[:, :]))
            link(nc.vector.tensor_tensor(wres[:, 0, :], w81[:, :], w81p[:, 0, :], ALU.subtract))
            link(nc.vector.tensor_copy(w81p[:, 1, :], wres[:, 0, :]))
            link(nc.vector.tensor_tensor(wres[:, 1, :], wres[:, 0, :], w81p[:, 1, :], ALU.subtract))
            nc.vector.tensor_copy(w81p[:, 2, :], wres[:, 1, :]).then_inc(s_w81p, 1)

            def copy_table(t, i, src):
                n = min(5, HW - 5 * i)
                nc.vector.tensor_copy(gtab[:, t, :, :, 5 * i:5 * i + n].rearrange("p t c x -> p x (t c)"),
                                      src[:, 0:n * 3 * C].rearrange("p (x n) -> p x n", x=n)).then_inc(s_gcopy[t], 1)

            dve.wait_ge(s_gb, 1)
            for i in range(2, 4):
                copy_table(1, i, bank[4 + i])
            dve.wait_ge(s_xrev, 16)
            dve.wait_ge(s_mean, 1)
            for h in range(NH):
                nc.vector.tensor_tensor(xcc[:, :, h, :].rearrange("p c b -> p b c"), xrev[:, h, :, :],
                                        bank[1][:, :].rearrange("p (b c) -> p b c", b=B), ALU.subtract).then_inc(s_xc, 1)
            dve.wait_ge(s_ga, 1)
            for i in range(2, 4):
                copy_table(0, i, bank[(2, 3, 0, 1)[i]])
            dve.wait_ge(s_kpe, 16 * YH)
            for e in range(NE):
                st.filled(dve, e)
                nc.vector.tensor_tensor(toep[:, :, e, :], st.bank(e)[:, :].rearrange("p (c x) -> p c x", x=HW),
                                        rep(toepk[:, e, :], C), ALU.add).then_inc(s_dd, 1)
                if e == 20:
                    dve.wait_ge(s_std, 1)
                    nc.vector.reciprocal(rstd[:, :], stdv[:, :]).then_inc(s_rstd, 1)
            dve.wait_ge(s_rstd, 1)
            dve.wait_ge(s_cf, 16)
            dve.wait_ge(s_wl1, 16)
            blk3 = blk.rearrange("p (g c) -> p g c", g=NG)
            nc.vector.tensor_tensor(bdq[:, :].rearrange("p (g c) -> p g c", g=NG), rep(wqr, NG), blk3, ALU.mult)
            nc.vector.tensor_tensor(bdk[:, :].rearrange("p (g c) -> p g c", g=NG), rep(wkr, NG), blk3, ALU.mult)
            nc.vector.tensor_scalar(bqs[:, :], bqr, SCALE, None, ALU.mult)
            nc.vector.tensor_scalar(flat(wsb[:, :, :]), colsel, wsr, None, ALU.mult).then_inc(s_bd, 1)
            nc.vector.memset(dec[1][:, :], DECAY)
            nc.vector.memset(dec[0][:, :], DECAY)
            dve.wait_ge(s_tabl, 16)
            nc.vector.memset(tabf[:, 0:1], float(NONE))
            link(nc.vector.tensor_copy(maskf[:, :, :], masks8[:, :, :]))
            nc.vector.tensor_tensor(anyf[:, :], maskf[:, 0, :], maskf[:, 1, :], ALU.max)
            link(nc.vector.scalar_tensor_tensor(code[:, :], maskf[:, 0, :], 2.0, maskf[:, 1, :], ALU.mult, ALU.add))
            link(nc.vector.tensor_tensor(code[:, :], code[:, :], stepcode, ALU.add))
            link(nc.vector.tensor_tensor(code[:, :], code[:, :], anyf[:, :], ALU.mult))
            link(nc.vector.tensor_scalar(codem[:, :], code[:, :], float(NONE), None, ALU.add))
            link(nc.vector.tensor_tensor_scan(tabf[:, 1:NSTEPS + 1], codem[:, :], codem[:, :], float(NONE), ALU.min, ALU.min))
            nc.vector.tensor_copy(tabi[:, :], tabf[:, :]).then_inc(s_tabi, 1)
            for j in range(1, CG // 2, 2):
                dve.wait_ge(s_conv, j + 1)
                for cg in (2 * j, 2 * j + 1):
                    cp = nc.vector.tensor_scalar(convr[:, cg, :], bank[j][:, (cg % 2) * S:(cg % 2 + 1) * S],
                                                 rstd[:, cg:cg + 1], None, ALU.mult)
                cp.then_inc(s_convD, 1)

            def argmax_op(values):
                link(nc.vector.tensor_reduce(top[:, :], values, AX.X, ALU.max))
                link(nc.vector.scalar_tensor_tensor(hit[:, :], values, top[:, :], rank, ALU.is_ge, ALU.mult))
                link(nc.vector.tensor_reduce(top[:, :], hit[:, :], AX.X, ALU.max))
                nc.vector.tensor_scalar(opi[:, :], top[:, :], -1.0, float(NOPS), ALU.mult, ALU.add).then_inc(s_op, 1)

            def pick_op(r):
                dve.wait_ge(s_row, r)
                dve.wait_ge(s_seen, r)
                link(nc.vector.tensor_copy(row[:, :], bank[0][0:1, 0:C]))
                argmax_op(row[:, 0:NOPS])

            def layernorm(n, residual):
                for h in range(NH):
                    hb = slice(h * B, (h + 1) * B)
                    t = residual(h)
                    link(nc.vector.tensor_reduce(mu[:, hb], t, AX.X, ALU.add))
                    link(nc.vector.tensor_scalar(mu[:, hb], mu[:, hb], -1.0 / C, None, ALU.mult))
                    nc.vector.tensor_tensor(xc[:, h, :, :], t, mu[:, hb].unsqueeze(2).broadcast_to([P, B, C]),
                                            ALU.add).then_inc(s_lnc, 1)
                    if (n, h) == (1, 0):
                        dve.wait_ge(s_lnc, NH * n + 1)
                        argmax_op(xc[0:1, 0, 0, 0:NOPS])
                for h in range(NH):
                    dve.wait_ge(s_lns, NH * n + h + 1)
                    nc.vector.tensor_reduce(var[:, h * B:(h + 1) * B], sq[:, h, :, :], AX.X, ALU.add).then_inc(s_lnv, 1)
                for h in range(NH):
                    hb = slice(h * B, (h + 1) * B)
                    dve.wait_ge(s_lnd, NH * n + h + 1)
                    link(nc.vector.reciprocal(inv[:, hb], dev[:, hb]))
                    nc.vector.tensor_tensor(xh[:, h, :, :], xc[:, h, :, :], inv[:, hb].unsqueeze(2).broadcast_to([P, B, C]),
                                            ALU.mult).then_inc(s_ln, 1)

            dve.wait_ge(s_xin, 16)

            def conv_residual(h):
                conv = st.bank(K_CONVT + h)[:, :].rearrange("p (c b) -> p b c", b=B)
                st.filled(dve, K_CONVT + h)
                if h == 1:
                    return conv
                nc.vector.tensor_tensor(tok[:, h, :, :], xin[:, h, :, :], conv, ALU.add).then_inc(s_dd, 1)
                wait(dve, s_dd, 0, count("D", STATIC[:K_CONVT + 1]))
                return tok[:, h, :, :]

            layernorm(0, conv_residual)

            def copy_half(k, h, dst):
                st.filled(dve, k)
                nc.vector.tensor_copy(dst[:, :, h * P:(h + 1) * P],
                                      st.bank(k)[:, :].rearrange("p (g s) -> p g s", g=NG)).then_inc(s_dd, 1)

            def block_diagonal(dst, src, scale):
                return nc.vector.scalar_tensor_tensor(dst[:, :], src, scale, blk, ALU.mult, ALU.mult)

            copy_half(K_PRE + 1, 1, xt)
            wait(dve, s_da, 0, count("A", STATIC[:K_CUR + 1]))
            dve.wait_ge(s_zero, 4)

            def sweeps():
                for i in range(LIF_ITERS):
                    link(nc.vector.tensor_tensor_scan(mem[:, :], dec[i % 2][:, 0:S], cur[:, :], 0.0, ALU.mult, ALU.add))
                    link(nc.vector.tensor_scalar(dec[1 - i % 2][:, 1:S + 1], mem[:, :], 1.0, DECAY, ALU.is_lt, ALU.mult))
                link(nc.vector.tensor_tensor(diff[:, :], dec[0][:, 0:S], dec[1][:, 0:S], ALU.not_equal))
                link(nc.vector.tensor_reduce(dsum[0:B, 0:1], diff[:, :], AX.X, ALU.max))
                link(nc.vector.transpose(dsumT[:, :], dsum[:, :]))
                link(nc.vector.tensor_reduce(dmax[:, :], dsumT[0:1, :], AX.X, ALU.max))
                link(nc.vector.tensor_copy(unsettled[:, :], dmax[:, :]))

            sweeps()
            reg_u, reg_c = dve.alloc_register("dve_unsettled"), dve.alloc_register("dve_chain")
            dve.reg_mov(reg_c, chain["n"])
            dve.reg_load(reg_u, unsettled[0:1, 0:1])
            with dve.If(dve.snap(reg_u) != 0):
                with dve.Fori(0, LIF_BLOCKS) as _i:
                    with dve.If(dve.snap(reg_u) != 0):
                        chain["base"], chain["n"] = dve.snap(reg_c), 0
                        sweeps()
                        dve.reg_alu(reg_c, reg_c, chain["n"], ALU.add)
                        dve.reg_load(reg_u, unsettled[0:1, 0:1])
            chain["base"], chain["n"] = dve.snap(reg_c), 0
            nc.vector.tensor_scalar(spk[:, :], mem[:, :], 1.0, None, ALU.is_ge).then_inc(s_spk, 1)
            st.filled(dve, K_CNT)
            link(nc.vector.tensor_scalar(spm[:, :], st.bank(K_CNT)[:, 0:S], 0.5, NEG, ALU.is_lt, ALU.mult))
            dve.wait_ge(s_mask, 16)
            nc.vector.tensor_tensor(negm[:, :, :], maskc[:, :, :], rep(spm[:, :], NH), ALU.add).then_inc(s_negm, 1)
            dve.wait_ge(s_negm, 1)
            nc.vector.memset(mu[:, 0:1], 0.0).then_inc(s_dd, 1)

            def row_max(base, b, masked):
                wait(dve, s_S, base, b + 1)
                if masked:
                    for ih in range(NH):
                        m = nc.vector.tensor_tensor_reduce(minus[b % AHEAD][:, ih, :], bank[SCORES[b % AHEAD]][:, ih * S:(ih + 1) * S],
                                                           negm[:, ih, :], -1.0, -FLOOR, ALU.add, ALU.min, nmax[:, b, ih:ih + 1])
                else:
                    m = nc.vector.tensor_reduce(nmax[:, b, :], bank[SCORES[b % AHEAD]][:, :].rearrange("p (h j) -> p h j", h=NH),
                                                AX.X, ALU.max, negate=True)
                m.then_inc(s_nm, 1)

            def invert(base, b, masked):
                wait(dve, s_P, base, b + 1)
                if masked:
                    link(nc.vector.tensor_scalar(esum[:, b, :], esum[:, b, :], 1e-30, None, ALU.max))
                nc.vector.reciprocal(einv[:, b, :], esum[:, b, :]).then_inc(s_ri, 1)

            def copy_probT(base, b):
                wait(dve, s_T, base, b + 1)
                nc.vector.tensor_copy(flat(probT[b % NTB]), bank[2 + b % 2][:, :]).then_inc(s_PT, 1)

            def attention_dve(base, masked, early=None, late=None):
                for b in range(AHEAD):
                    row_max(base, b, masked)
                    if masked and b == 0:
                        nc.vector.tensor_tensor(tokb[:, :, :, :].rearrange("p h b c -> p (h b) c"),
                                                tok[:, :, :, :].rearrange("p h b c -> p (h b) c"), rep(bor, NH * B), ALU.add).then_inc(s_tokb, 1)
                if early:
                    early(1)
                invert(base, 0, masked)
                if early:
                    early(3)
                for b in range(MAIN):
                    if b + 1 < B:
                        invert(base, b + 1, masked)
                    if b + AHEAD < B:
                        row_max(base, b + AHEAD, masked)
                    copy_probT(base, b)
                    if late and b >= MAIN - 2 - GB and b < MAIN - 2:
                        late(b - (MAIN - 2 - GB))

            def attention_rest(base, b, masked):
                if b + 1 < B:
                    invert(base, b + 1, masked)
                copy_probT(base, b)

            attention_dve(0, True)
            for b in range(MAIN, B):
                attention_rest(0, b, True)

            def attention_residual(h):
                st.filled(dve, K_YTOK + h)
                return st.bank(K_YTOK + h)[:, :].rearrange("p (b c) -> p b c", b=B)

            layernorm(1, attention_residual)
            reg_att, reg_task, reg_da, reg_dd = (dve.alloc_register(n) for n in ("dve_att", "dve_task", "dve_da", "dve_dd"))
            dve.reg_alu(reg_c, reg_c, chain["n"], ALU.add)
            dve.reg_mov(reg_att, B)
            reg_wp, reg_ffa, reg_ffd = (dve.alloc_register("dve_" + n) for n in ("weight_products", "ffn_act", "ffn_dve"))
            dve.reg_mov(reg_wp, 0)
            dve.reg_mov(reg_ffa, count("A", STATIC[:K_YTOK]))
            dve.reg_mov(reg_ffd, count("D", STATIC[:K_YTOK]))
            dve.reg_mov(reg_task, len(STATIC))
            dve.reg_mov(reg_da, count("A", STATIC))
            dve.reg_mov(reg_dd, count("D", STATIC))
            reg_code, reg_op, reg_step, reg_kind, reg_r = (
                dve.alloc_register("dve_" + n) for n in ("code", "op", "step", "kind", "round"))
            dve.reg_mov(reg_r, 1)
            dve.wait_ge(s_tabmove, 32)
            dve.wait_ge(s_op, 1)
            dve.reg_load(reg_op, opi[0:1, 0:1])
            op = dve.snap(reg_op, min_val=0, max_val=NOPS - 1)
            dve.reg_load(reg_code, tab[0:1, bass.ds(op * (NSTEPS + 1) + NSTEPS, 1)])
            reg_next = dve.alloc_register("dve_next_kind")

            def place_weights(q, r):
                rows = slice(q * C, (q + 1) * C)
                if q == 0:
                    ffa, ffd = dve.snap(reg_ffa), dve.snap(reg_ffd)
                    dve.wait_ge(s_da, ffa)
                    dve.wait_ge(s_dd, ffd)
                    dve.wait_ge(s_wA, r * 16)
                    dve.wait_ge(s_wF, r * 16)
                nc.vector.tensor_copy(w1z[rows, q, :], wa[:, NWA:NWA + HID])
                if q == GB - 1:
                    nc.vector.tensor_copy(wfs[:, :], wf[:, :]).then_inc(s_w1z, 1)

            def place_next():
                dve.reg_alu(reg_next, reg_code, 3, ALU.bitwise_and)
                with dve.If(dve.snap(reg_next) == 1):
                    r = dve.snap(reg_r)
                    for q in range(GB):
                        place_weights(q, r)

            copy_half(K_H0 + NH + 1, 1, hT)

            def weight_diagonals():
                dve.reg_alu(reg_next, reg_code, 2, ALU.bitwise_and)
                with dve.If(dve.snap(reg_next) != 0):
                    wp = dve.snap(reg_wp)
                    for i, (diagonal, scale) in enumerate(((bda, SCALE), (bdv, 1.0))):
                        dve.wait_ge(s_wp, wp + (i + 1))
                        block_diagonal(diagonal, bank[2 + i][:, 0:P], scale).then_inc(s_bd2, 1)
                    dve.reg_alu(reg_wp, reg_wp, 2, ALU.add)

            weight_diagonals()
            with dve.While(lambda: dve.snap(reg_code) < NONE):
                dve.reg_alu(reg_step, reg_code, 2, ALU.logical_shift_right)
                dve.reg_alu(reg_kind, reg_code, 3, ALU.bitwise_and)
                b = dve.snap(reg_step, min_val=0, max_val=NSTEPS - 1)
                kind = dve.snap(reg_kind)
                r = dve.snap(reg_r)
                with dve.If(kind >= 2):
                    att = dve.snap(reg_att)
                    chain["base"], chain["n"] = dve.snap(reg_c), 0
                    t = Tasks(LATT, dve.snap(reg_task))
                    for g in range(1, NG, 2):
                        t.filled(dve, g)
                        for q in range(GB):
                            rows = slice(q * C, (q + 1) * C)
                            cp = nc.vector.tensor_copy(qz[rows, g * GB + q, :], t.bank(g)[rows, 0:S])
                        cp.then_inc(s_dd, 1)

                    def copy_values(g):
                        t.filled(dve, NG + g)
                        nc.vector.tensor_copy(v[:, :, g * GB:(g + 1) * GB, :].rearrange("p h b c -> p h (b c)"),
                                              t.bank(NG + g)[:, 0:S].rearrange("p (h n) -> p h n", h=NH)).then_inc(s_dd, 1)

                    attention_dve(att, False, copy_values, lambda q: place_weights(q, r))

                def count_tasks(owners, attended):
                    dve.reg_alu(reg_c, reg_c, chain["n"], ALU.add)
                    if attended:
                        dve.reg_alu(reg_att, reg_att, B, ALU.add)
                    dve.reg_alu(reg_task, reg_task, len(owners), ALU.add)
                    dve.reg_alu(reg_da, reg_da, count("A", owners), ALU.add)
                    dve.reg_alu(reg_dd, reg_dd, count("D", owners), ALU.add)

                def ffn(t, k0, order, att=None):
                    for i, (what, n) in enumerate(order):
                        k = k0 + i
                        if att is not None and i in (0, 1, 3):
                            attention_rest(att, MAIN + (i if i < 3 else 2), False)
                        if i == 3:
                            pick_op(r)
                        if t.owners[k] != "D":
                            continue
                        if (what, n) == ("Z", 3):
                            next_step(dve, b, reg_r, reg_op, reg_code)
                            weight_diagonals()
                            count_tasks(t.owners, att is not None)
                            dve.reg_alu(reg_ffa, reg_da, 0, ALU.add)
                            dve.reg_alu(reg_ffd, reg_dd, 0, ALU.add)
                        t.filled(dve, k)
                        if what == "H":
                            gp, q = divmod(n, GB)
                            nc.vector.tensor_scalar(relu[:, q, 2 * gp:2 * gp + 2, :],
                                                    t.bank(k)[:, :].rearrange("p (g s) -> p g s", g=2), b1s, 0.0,
                                                    ALU.add, ALU.max).then_inc(s_dd, 1)
                        else:
                            nc.vector.tensor_scalar(hT[:, n, :], t.bank(k)[:, 0:S], b2s, None, ALU.add).then_inc(s_dd, 1)

                with dve.If(kind == 1):
                    chain["base"], chain["n"] = dve.snap(reg_c), 0
                    ffn(Tasks(FF, dve.snap(reg_task), dve.snap(reg_da), dve.snap(reg_dd)), 0, HORDER)
                    place_next()
                with dve.If(kind == 3):
                    chain["base"], chain["n"] = dve.snap(reg_c), 0
                    ffn(Tasks(LATTF, dve.snap(reg_task), dve.snap(reg_da), dve.snap(reg_dd)), K_YF, YORDER, dve.snap(reg_att))
                    place_next()
                with dve.If(kind == 2):
                    chain["base"], chain["n"] = dve.snap(reg_c), 0
                    att = dve.snap(reg_att)
                    for last in range(MAIN, B):
                        attention_rest(att, last, False)
                    pick_op(r)
                    count_tasks(LATT, True)
                    next_step(dve, b, reg_r, reg_op, reg_code)
                    weight_diagonals()
                    place_next()
            da, dd = dve.snap(reg_da), dve.snap(reg_dd)
            dve.wait_ge(s_da, da)
            dve.wait_ge(s_dd, dd)
            for i in range(2):
                gs = slice(2 * i, 2 * i + 2)
                nc.vector.tensor_tensor(outT[:, gs, :], outT[:, gs, :], hT[:, gs, :], ALU.add).then_inc(s_fin, 1)


def kernel(**inputs):
    import numpy as _np
    import concourse.bacc as _bacc
    from concourse import mybir as _mybir
    from concourse.bass_utils import run_bass_kernel_spmd as _run

    g = {k: _np.asarray(a) for k, a in inputs.items()}
    steps = NSTEPS * NOPS

    def swapped(a):
        return _np.swapaxes(a, -1, -2)

    def tok(a):
        return a.reshape(B, C, S).transpose(2, 0, 1).reshape(S, B * C)

    def down(a):
        return _np.tile(a.reshape(1, -1), (P, 1))

    def reps(a):
        return _np.tile(a.reshape(C, -1), (GB, 1))

    wc = g["L0_conv_weight_comp"].reshape(C, NP13, NP13)[:, Q0:Q0 + NQ, Q0:Q0 + NQ]
    at = {n: g["L1_attn_" + n] for n in ("Wq", "Wk", "Wv", "Wo", "Ws", "bq", "bk", "bv", "bo", "bs")}
    ff = {n: g["L1_ffn_" + n].reshape((steps,) + g["L1_ffn_" + n].shape[2:])
          for n in ("wq", "wk", "wv", "wo", "ffn_w1", "ffn_b1", "ffn_w2", "ffn_b2")}
    arrays = {
        "xtok": tok(g["x"]), "xrev": tok(g["x"][:, :, :, ::-1]),
        "w81": wc.reshape(C, NQ * NQ).T,
        "kpef": g["L0_conv_kpe"][0, 0, ::-1, ::-1],
        "wl1": _np.concatenate([reps(at["Wq"]), reps(at["Wk"]), down(at["bo"]), reps(at["Ws"]), reps(at["bq"]),
                                reps(at["bk"]), down(at["bs"])], axis=1),
        "wl2": _np.concatenate([_np.tile(at["Wv"].T, (1, GB)), at["Wo"], at["bv"].reshape(C, 1)], axis=1),
        "wa": _np.concatenate([_np.tile(swapped(ff["wq"]), (1, 1, GB)), _np.tile(swapped(ff["wv"]), (1, 1, GB)),
                               swapped(ff["wk"]), ff["wo"], ff["ffn_w1"]], axis=2),
        "wf": _np.concatenate([ff["ffn_w2"], ff["ffn_b1"][:, :, None], _np.tile(ff["ffn_b2"], (1, GB))[:, :, None]], axis=2),
        "masks": _np.stack([g["L1_ffn_attn_mask"].T[:, ::-1], g["L1_ffn_ffn_mask"].T[:, ::-1]], axis=1),
    }
    arrays.update(constants())
    nc = _bacc.Bacc("TRN2", target_bir_lowering=False, num_devices=1)
    d = {}
    for name, a in arrays.items():
        a = arrays[name] = _np.ascontiguousarray(a)
        d[name] = nc.dram_tensor(name + "_dram", a.shape, _mybir.dt.from_np(a.dtype), kind="ExternalInput").ap()
    d["out"] = nc.dram_tensor("out_dram", (B * C, S), _mybir.dt.float32, kind="ExternalOutput").ap()
    build(nc, d)
    r = _run(nc, [{name + "_dram": a for name, a in arrays.items()}], core_ids=[0])
    return r.results[0]["out_dram"].reshape(B, C, HW, HW)
```
